# Optimizing a Trainium2 kernel written in Bass

```python
import numpy as np
import jax
import jax.numpy as jnp

def _softmax(x, axis=-1):
    return jax.nn.softmax(x, axis=axis)

def _gelu(x):
    return jax.nn.gelu(x, approximate=True)

def _silu(x):
    return jax.nn.silu(x)

def _sigmoid(x):
    return jax.nn.sigmoid(x)

def _layernorm(x, axis=-1, eps=1e-05):
    m = jnp.mean(x, axis=axis, keepdims=True)
    v = jnp.var(x, axis=axis, keepdims=True)
    return (x - m) / jnp.sqrt(v + eps)

def _scatter_add(tgt, idx, src, axis=0):
    return tgt.at[idx].add(src)

def _segment_sum(src, seg, n):
    return jax.ops.segment_sum(src, seg, n)
kernel_name = 'mk_lm_tower_d1_tok_ids512_r4_3dceb4'

def setup_inputs(seed: int=0):
    np.random.seed(seed)
    _w = jnp.asarray

    def _rec_inputs():
        import jax
        import jax.numpy as jnp
        _rk = jax.random.key(seed)
        x = jax.random.randint(jax.random.fold_in(_rk, 1), (8, 512), 0, 128, jnp.int32)
        mask_BS_i1_0 = jnp.where(jnp.ones((8, 512), dtype=bool), 1, 0).astype(jnp.int32)
        itok_BS_0_999 = jax.random.randint(jax.random.fold_in(_rk, 22), (8, 512), 0, 250, jnp.int32)
        itok_BS_0_63 = jax.random.randint(jax.random.fold_in(_rk, 23), (8, 512), 0, 64, jnp.int32)
        mask_BS_i0_1 = jnp.where(jnp.ones((8, 512), dtype=bool), 0, 1).astype(jnp.int32)
        mask_BS_b0_1 = jnp.logical_not(jnp.ones((8, 512), dtype=bool))
        return (x, mask_BS_i1_0, itok_BS_0_999, itok_BS_0_63, mask_BS_i0_1, mask_BS_b0_1)
    x, mask_BS_i1_0, itok_BS_0_999, itok_BS_0_63, mask_BS_i0_1, mask_BS_b0_1 = _rec_inputs()

    def _L0_tok_setup():
        import jax, jax.numpy as jnp
        import numpy as np
        B, S, D, H, W, L, V, FF = (8, 1024, 192, 12, 128, 2, 128, 768)
        G_IDX = (0,)

        def _ln(x, g, b):
            m = x.mean(-1, keepdims=True)
            v = ((x - m) ** 2).mean(-1, keepdims=True)
            return (x - m) * jax.lax.rsqrt(v + 1e-05) * g + b

        def _band_blocks(t, w):
            b, h, s, dh = t.shape
            nb = s // w
            tp = jnp.pad(t, ((0, 0), (0, 0), (w, w), (0, 0))).reshape(b, h, nb + 2, w, dh)
            return jnp.concatenate([tp[:, :, 0:nb], tp[:, :, 1:nb + 1], tp[:, :, 2:nb + 2]], axis=3)

        def _longformer_attn(x, att_mask, Wq, bq, Wk, bk, Wv, bv, Wo, bo, w, gidx):
            b, s, d = x.shape
            dh = d // H
            proj = lambda Wm, bm: (x @ Wm.T + bm).reshape(b, s, H, dh).transpose(0, 2, 1, 3)
            q = proj(Wq, bq) / np.float32(np.sqrt(dh))
            k = proj(Wk, bk)
            v = proj(Wv, bv)
            nb = s // w
            qb = q.reshape(b, H, nb, w, dh)
            kb = _band_blocks(k, w)
            vb = _band_blocks(v, w)
            sb = jnp.einsum('bhnqd,bhnkd->bhnqk', qb, kb)
            i = jnp.arange(w)[:, None]
            jj = jnp.arange(3 * w)[None, :]
            allowed = (jj - i >= 0) & (jj - i <= 2 * w)
            pos = jnp.arange(nb)[:, None] * w - w + jj
            valid = (pos >= 0) & (pos < s)
            key_bias = jnp.where(att_mask != 0, -10000.0, 0.0)
            kbias = jnp.pad(key_bias, ((0, 0), (w, w)), constant_values=-1000000000.0).reshape(b, nb + 2, w)
            kbb = jnp.concatenate([kbias[:, 0:nb], kbias[:, 1:nb + 1], kbias[:, 2:nb + 2]], axis=2)
            bias = jnp.where(allowed[None, None] & valid[None, :, None, :], kbb[:, :, None, :], -1000000000.0)
            sb = sb + bias[:, None]
            sb_flat = sb.reshape(b, H, s, 3 * w)
            g = jnp.asarray(gidx)
            ng = g.shape[0]
            kg = k[:, :, g]
            vg = v[:, :, g]
            sg = jnp.einsum('bhsd,bhgd->bhsg', q, kg)
            probs = jax.nn.softmax(jnp.concatenate([sg, sb_flat], axis=-1), axis=-1)
            pg = probs[..., :ng]
            pb = probs[..., ng:].reshape(b, H, nb, w, 3 * w)
            out = jnp.einsum('bhnqk,bhnkd->bhnqd', pb, vb).reshape(b, H, s, dh)
            out = out + jnp.einsum('bhsg,bhgd->bhsd', pg, vg)
            qg = q[:, :, g]
            sfull = jnp.einsum('bhgd,bhsd->bhgs', qg, k) + jnp.where(att_mask < 0, -10000.0, 0.0)[:, None, None, :]
            og = jnp.einsum('bhgs,bhsd->bhgd', jax.nn.softmax(sfull, axis=-1), v)
            out = out.at[:, :, g].set(og)
            out = out.transpose(0, 2, 1, 3).reshape(b, s, d)
            return out @ Wo.T + bo
        key = jax.random.key(seed)
        ks = jax.random.split(key, 32)
        sc = 0.02
        inp = {'call': jax.random.randint(ks[0], (B, S), 0, V), 'entry': jax.random.randint(ks[1], (B, S), 0, 2), 'time': jax.random.randint(ks[2], (B, S), 0, 250), 'proc': jax.random.randint(ks[3], (B, S), 0, 64), 'pid': jax.random.randint(ks[4], (B, S), 0, 64), 'tid': jax.random.randint(ks[5], (B, S), 0, 64), 'ret': jax.random.randint(ks[6], (B, S), 0, 2), 'pad_mask': jnp.zeros((B, S), dtype=bool), 'chk': 0, 'emb': jax.random.normal(ks[7], (V, D), jnp.float32) * sc, 'Wq': jax.random.normal(ks[8], (L, D, D), jnp.float32) * sc, 'bq': jnp.zeros((L, D), jnp.float32), 'Wk': jax.random.normal(ks[9], (L, D, D), jnp.float32) * sc, 'bk': jnp.zeros((L, D), jnp.float32), 'Wv': jax.random.normal(ks[10], (L, D, D), jnp.float32) * sc, 'bv': jnp.zeros((L, D), jnp.float32), 'Wo': jax.random.normal(ks[11], (L, D, D), jnp.float32) * sc, 'bo': jnp.zeros((L, D), jnp.float32), 'W1': jax.random.normal(ks[12], (L, FF, D), jnp.float32) * sc, 'b1': jnp.zeros((L, FF), jnp.float32), 'W2': jax.random.normal(ks[13], (L, D, FF), jnp.float32) * sc, 'b2': jnp.zeros((L, D), jnp.float32), 'g1': jnp.ones((L, D), jnp.float32), 'beta1': jnp.zeros((L, D), jnp.float32), 'g2': jnp.ones((L, D), jnp.float32), 'beta2': jnp.zeros((L, D), jnp.float32), 'gf': jnp.ones((D,), jnp.float32), 'betaf': jnp.zeros((D,), jnp.float32), 'Wc': jax.random.normal(ks[14], (V, D), jnp.float32) * sc, 'bc': jnp.zeros((V,), jnp.float32)}
        return inp
    _L0_tok_all = _L0_tok_setup()
    _L0_tok_in = {k: v for k, v in _L0_tok_all.items() if k in ('emb', 'Wq', 'bq', 'Wk', 'bk', 'Wv', 'bv', 'Wo', 'bo', 'W1', 'b1', 'W2', 'b2', 'g1', 'beta1', 'g2', 'beta2', 'gf', 'betaf', 'Wc', 'bc')}
    del _L0_tok_all

    def _L0_attn_setup():
        import jax, jax.numpy as jnp
        import numpy as np
        D, NH, FF, M = (128, 8, 512, 128)
        HD = D // NH
        B, N = (8, 1024)

        def _ln(x, g, b):
            mu = jnp.mean(x, axis=-1, keepdims=True)
            var = jnp.var(x, axis=-1, keepdims=True)
            return (x - mu) / jnp.sqrt(var + 1e-05) * g + b

        def _mha(q, k, v, in_w, in_b, out_w, out_b):
            wq, wk, wv = jnp.split(in_w, 3, axis=0)
            bq, bk, bv = jnp.split(in_b, 3)
            qh = (q @ wq.T + bq).reshape(q.shape[0], q.shape[1], NH, HD)
            kh = (k @ wk.T + bk).reshape(k.shape[0], k.shape[1], NH, HD)
            vh = (v @ wv.T + bv).reshape(v.shape[0], v.shape[1], NH, HD)
            scores = jnp.einsum('bqhd,bkhd->bhqk', qh, kh) / jnp.sqrt(jnp.asarray(HD, qh.dtype))
            attn = jax.nn.softmax(scores, axis=-1)
            o = jnp.einsum('bhqk,bkhd->bqhd', attn, vh).reshape(q.shape[0], q.shape[1], D)
            return o @ out_w.T + out_b

        def _mab(q, k, v, p):
            in_w, in_b, out_w, out_b, g1, b1, g2, b2, l1w, l1b, l2w, l2b = p
            x = q + _mha(_ln(q, g1, b1), _ln(k, g1, b1), _ln(v, g1, b1), in_w, in_b, out_w, out_b)
            h = _ln(x, g2, b2)
            ff = jax.nn.gelu(h @ l1w.T + l1b, approximate=False) @ l2w.T + l2b
            return x + ff

        def _block_params(key, scale=0.02):
            ks = jax.random.split(key, 4)
            return dict(in_w=jax.random.normal(ks[0], (3 * D, D), jnp.float32) * scale, in_b=jnp.zeros((3 * D,), jnp.float32), out_w=jax.random.normal(ks[1], (D, D), jnp.float32) * scale, out_b=jnp.zeros((D,), jnp.float32), ln1_g=jnp.ones((D,), jnp.float32), ln1_b=jnp.zeros((D,), jnp.float32), ln2_g=jnp.ones((D,), jnp.float32), ln2_b=jnp.zeros((D,), jnp.float32), l1_w=jax.random.normal(ks[2], (FF, D), jnp.float32) * scale, l1_b=jnp.zeros((FF,), jnp.float32), l2_w=jax.random.normal(ks[3], (D, FF), jnp.float32) * scale, l2_b=jnp.zeros((D,), jnp.float32))
        key = jax.random.key(seed)
        kx, ki, k1, k2 = jax.random.split(key, 4)
        inp = {'x': jax.random.normal(kx, (B, N, D), jnp.float32), 'ind': jax.random.normal(ki, (M, D), jnp.float32)}
        for pref, k in (('a1_', k1), ('a2_', k2)):
            for name, val in _block_params(k).items():
                inp[pref + name] = val
        return inp
    _L0_attn_all = _L0_attn_setup()
    _L0_attn_in = {k: v for k, v in _L0_attn_all.items() if k in ('ind', 'a1_in_w', 'a1_in_b', 'a1_out_w', 'a1_out_b', 'a1_ln1_g', 'a1_ln1_b', 'a1_ln2_g', 'a1_ln2_b', 'a1_l1_w', 'a1_l1_b', 'a1_l2_w', 'a1_l2_b', 'a2_in_w', 'a2_in_b', 'a2_out_w', 'a2_out_b', 'a2_ln1_g', 'a2_ln1_b', 'a2_ln2_g', 'a2_ln2_b', 'a2_l1_w', 'a2_l1_b', 'a2_l2_w', 'a2_l2_b')}
    del _L0_attn_all

    def _L0_ffn_setup():
        import jax, jax.numpy as jnp
        import numpy as np
        B, T, D, H = (2, 256, 128, 512)
        G, E = (4, 8)
        GK, EK = (2, 2)
        EPS = 1e-05
        SCALE = 0.02

        def _layernorm(x, g, b):
            m = jnp.mean(x, axis=-1, keepdims=True)
            xc = x - m
            v = jnp.mean(xc * xc, axis=-1, keepdims=True)
            return xc * jax.lax.rsqrt(v + EPS) * g + b

        def _topk_gate(logits, k, n):
            v, i = jax.lax.top_k(logits, k)
            sc = jax.nn.softmax(v, axis=-1)
            return jnp.sum(jax.nn.one_hot(i, n, dtype=logits.dtype) * sc[..., None], axis=-2)
        key = jax.random.key(seed)
        ks = jax.random.split(key, 6)
        return {'inp': jax.random.normal(ks[0], (B, T, D), jnp.float32), 'ln_g': jnp.ones((D,), jnp.float32), 'ln_b': jnp.zeros((D,), jnp.float32), 'wg_group': jax.random.normal(ks[1], (D, G), jnp.float32) * SCALE, 'wg_inner': jax.random.normal(ks[2], (G, D, E), jnp.float32) * SCALE, 'W1': jax.random.normal(ks[3], (G, E, D, H), jnp.float32) * SCALE, 'b1': jnp.zeros((G, E, H), jnp.float32), 'W2': jax.random.normal(ks[4], (G, E, H, D), jnp.float32) * SCALE, 'b2': jnp.zeros((G, E, D), jnp.float32), 'gln_g': jnp.ones((G, D), jnp.float32), 'gln_b': jnp.zeros((G, D), jnp.float32)}
    _L0_ffn_all = _L0_ffn_setup()
    _L0_ffn_in = {k: v for k, v in _L0_ffn_all.items() if k in ('ln_g', 'ln_b', 'wg_group', 'wg_inner', 'W1', 'b1', 'W2', 'b2', 'gln_g', 'gln_b')}
    del _L0_ffn_all
    return {'x': x, 'mask_BS_i1_0': mask_BS_i1_0, 'itok_BS_0_999': itok_BS_0_999, 'itok_BS_0_63': itok_BS_0_63, 'mask_BS_i0_1': mask_BS_i0_1, 'mask_BS_b0_1': mask_BS_b0_1, 'L0_tok_emb': _L0_tok_in['emb'], 'L0_tok_Wq': _L0_tok_in['Wq'], 'L0_tok_bq': _L0_tok_in['bq'], 'L0_tok_Wk': _L0_tok_in['Wk'], 'L0_tok_bk': _L0_tok_in['bk'], 'L0_tok_Wv': _L0_tok_in['Wv'], 'L0_tok_bv': _L0_tok_in['bv'], 'L0_tok_Wo': _L0_tok_in['Wo'], 'L0_tok_bo': _L0_tok_in['bo'], 'L0_tok_W1': _L0_tok_in['W1'], 'L0_tok_b1': _L0_tok_in['b1'], 'L0_tok_W2': _L0_tok_in['W2'], 'L0_tok_b2': _L0_tok_in['b2'], 'L0_tok_g1': _L0_tok_in['g1'], 'L0_tok_beta1': _L0_tok_in['beta1'], 'L0_tok_g2': _L0_tok_in['g2'], 'L0_tok_beta2': _L0_tok_in['beta2'], 'L0_tok_gf': _L0_tok_in['gf'], 'L0_tok_betaf': _L0_tok_in['betaf'], 'L0_tok_Wc': _L0_tok_in['Wc'], 'L0_tok_bc': _L0_tok_in['bc'], 'L0_attn_ind': _L0_attn_in['ind'], 'L0_attn_a1_in_w': _L0_attn_in['a1_in_w'], 'L0_attn_a1_in_b': _L0_attn_in['a1_in_b'], 'L0_attn_a1_out_w': _L0_attn_in['a1_out_w'], 'L0_attn_a1_out_b': _L0_attn_in['a1_out_b'], 'L0_attn_a1_ln1_g': _L0_attn_in['a1_ln1_g'], 'L0_attn_a1_ln1_b': _L0_attn_in['a1_ln1_b'], 'L0_attn_a1_ln2_g': _L0_attn_in['a1_ln2_g'], 'L0_attn_a1_ln2_b': _L0_attn_in['a1_ln2_b'], 'L0_attn_a1_l1_w': _L0_attn_in['a1_l1_w'], 'L0_attn_a1_l1_b': _L0_attn_in['a1_l1_b'], 'L0_attn_a1_l2_w': _L0_attn_in['a1_l2_w'], 'L0_attn_a1_l2_b': _L0_attn_in['a1_l2_b'], 'L0_attn_a2_in_w': _L0_attn_in['a2_in_w'], 'L0_attn_a2_in_b': _L0_attn_in['a2_in_b'], 'L0_attn_a2_out_w': _L0_attn_in['a2_out_w'], 'L0_attn_a2_out_b': _L0_attn_in['a2_out_b'], 'L0_attn_a2_ln1_g': _L0_attn_in['a2_ln1_g'], 'L0_attn_a2_ln1_b': _L0_attn_in['a2_ln1_b'], 'L0_attn_a2_ln2_g': _L0_attn_in['a2_ln2_g'], 'L0_attn_a2_ln2_b': _L0_attn_in['a2_ln2_b'], 'L0_attn_a2_l1_w': _L0_attn_in['a2_l1_w'], 'L0_attn_a2_l1_b': _L0_attn_in['a2_l1_b'], 'L0_attn_a2_l2_w': _L0_attn_in['a2_l2_w'], 'L0_attn_a2_l2_b': _L0_attn_in['a2_l2_b'], 'L0_ffn_ln_g': _L0_ffn_in['ln_g'], 'L0_ffn_ln_b': _L0_ffn_in['ln_b'], 'L0_ffn_wg_group': _L0_ffn_in['wg_group'], 'L0_ffn_wg_inner': _L0_ffn_in['wg_inner'], 'L0_ffn_W1': _L0_ffn_in['W1'], 'L0_ffn_b1': _L0_ffn_in['b1'], 'L0_ffn_W2': _L0_ffn_in['W2'], 'L0_ffn_b2': _L0_ffn_in['b2'], 'L0_ffn_gln_g': _L0_ffn_in['gln_g'], 'L0_ffn_gln_b': _L0_ffn_in['gln_b']}

def reference(x, mask_BS_i1_0, itok_BS_0_999, itok_BS_0_63, mask_BS_i0_1, mask_BS_b0_1, L0_tok_emb, L0_tok_Wq, L0_tok_bq, L0_tok_Wk, L0_tok_bk, L0_tok_Wv, L0_tok_bv, L0_tok_Wo, L0_tok_bo, L0_tok_W1, L0_tok_b1, L0_tok_W2, L0_tok_b2, L0_tok_g1, L0_tok_beta1, L0_tok_g2, L0_tok_beta2, L0_tok_gf, L0_tok_betaf, L0_tok_Wc, L0_tok_bc, L0_attn_ind, L0_attn_a1_in_w, L0_attn_a1_in_b, L0_attn_a1_out_w, L0_attn_a1_out_b, L0_attn_a1_ln1_g, L0_attn_a1_ln1_b, L0_attn_a1_ln2_g, L0_attn_a1_ln2_b, L0_attn_a1_l1_w, L0_attn_a1_l1_b, L0_attn_a1_l2_w, L0_attn_a1_l2_b, L0_attn_a2_in_w, L0_attn_a2_in_b, L0_attn_a2_out_w, L0_attn_a2_out_b, L0_attn_a2_ln1_g, L0_attn_a2_ln1_b, L0_attn_a2_ln2_g, L0_attn_a2_ln2_b, L0_attn_a2_l1_w, L0_attn_a2_l1_b, L0_attn_a2_l2_w, L0_attn_a2_l2_b, L0_ffn_ln_g, L0_ffn_ln_b, L0_ffn_wg_group, L0_ffn_wg_inner, L0_ffn_W1, L0_ffn_b1, L0_ffn_W2, L0_ffn_b2, L0_ffn_gln_g, L0_ffn_gln_b):
    import jax
    import jax.numpy as jnp

    def _L0_tok_ref(call, entry, time, proc, pid, tid, ret, pad_mask, chk, emb, Wq, bq, Wk, bk, Wv, bv, Wo, bo, W1, b1, W2, b2, g1, beta1, g2, beta2, gf, betaf, Wc, bc):
        import jax, jax.numpy as jnp
        import numpy as np
        B, S, D, H, W, L, V, FF = (8, 1024, 192, 12, 128, 2, 128, 768)
        G_IDX = (0,)

        def _ln(x, g, b):
            m = x.mean(-1, keepdims=True)
            v = ((x - m) ** 2).mean(-1, keepdims=True)
            return (x - m) * jax.lax.rsqrt(v + 1e-05) * g + b

        def _band_blocks(t, w):
            b, h, s, dh = t.shape
            nb = s // w
            tp = jnp.pad(t, ((0, 0), (0, 0), (w, w), (0, 0))).reshape(b, h, nb + 2, w, dh)
            return jnp.concatenate([tp[:, :, 0:nb], tp[:, :, 1:nb + 1], tp[:, :, 2:nb + 2]], axis=3)

        def _longformer_attn(x, att_mask, Wq, bq, Wk, bk, Wv, bv, Wo, bo, w, gidx):
            b, s, d = x.shape
            dh = d // H
            proj = lambda Wm, bm: (x @ Wm.T + bm).reshape(b, s, H, dh).transpose(0, 2, 1, 3)
            q = proj(Wq, bq) / np.float32(np.sqrt(dh))
            k = proj(Wk, bk)
            v = proj(Wv, bv)
            nb = s // w
            qb = q.reshape(b, H, nb, w, dh)
            kb = _band_blocks(k, w)
            vb = _band_blocks(v, w)
            sb = jnp.einsum('bhnqd,bhnkd->bhnqk', qb, kb)
            i = jnp.arange(w)[:, None]
            jj = jnp.arange(3 * w)[None, :]
            allowed = (jj - i >= 0) & (jj - i <= 2 * w)
            pos = jnp.arange(nb)[:, None] * w - w + jj
            valid = (pos >= 0) & (pos < s)
            key_bias = jnp.where(att_mask != 0, -10000.0, 0.0)
            kbias = jnp.pad(key_bias, ((0, 0), (w, w)), constant_values=-1000000000.0).reshape(b, nb + 2, w)
            kbb = jnp.concatenate([kbias[:, 0:nb], kbias[:, 1:nb + 1], kbias[:, 2:nb + 2]], axis=2)
            bias = jnp.where(allowed[None, None] & valid[None, :, None, :], kbb[:, :, None, :], -1000000000.0)
            sb = sb + bias[:, None]
            sb_flat = sb.reshape(b, H, s, 3 * w)
            g = jnp.asarray(gidx)
            ng = g.shape[0]
            kg = k[:, :, g]
            vg = v[:, :, g]
            sg = jnp.einsum('bhsd,bhgd->bhsg', q, kg)
            probs = jax.nn.softmax(jnp.concatenate([sg, sb_flat], axis=-1), axis=-1)
            pg = probs[..., :ng]
            pb = probs[..., ng:].reshape(b, H, nb, w, 3 * w)
            out = jnp.einsum('bhnqk,bhnkd->bhnqd', pb, vb).reshape(b, H, s, dh)
            out = out + jnp.einsum('bhsg,bhgd->bhsd', pg, vg)
            qg = q[:, :, g]
            sfull = jnp.einsum('bhgd,bhsd->bhgs', qg, k) + jnp.where(att_mask < 0, -10000.0, 0.0)[:, None, None, :]
            og = jnp.einsum('bhgs,bhsd->bhgd', jax.nn.softmax(sfull, axis=-1), v)
            out = out.at[:, :, g].set(og)
            out = out.transpose(0, 2, 1, 3).reshape(b, s, d)
            return out @ Wo.T + bo
        x = emb[call]
        g = jnp.asarray(G_IDX)
        att_mask = jnp.zeros((call.shape[0], call.shape[1]), jnp.float32).at[:, g].set(10000.0)
        att_mask = jnp.where(pad_mask, -10000.0, att_mask)
        for l in range(L):
            a = _longformer_attn(x, att_mask, Wq[l], bq[l], Wk[l], bk[l], Wv[l], bv[l], Wo[l], bo[l], W, G_IDX)
            x = _ln(x + a, g1[l], beta1[l])
            h = jax.nn.relu(x @ W1[l].T + b1[l]) @ W2[l].T + b2[l]
            x = _ln(x + h, g2[l], beta2[l])
        x = _ln(x, gf, betaf)
        return x @ Wc.T + bc

    def _L0_attn_ref(x, ind, a1_in_w, a1_in_b, a1_out_w, a1_out_b, a1_ln1_g, a1_ln1_b, a1_ln2_g, a1_ln2_b, a1_l1_w, a1_l1_b, a1_l2_w, a1_l2_b, a2_in_w, a2_in_b, a2_out_w, a2_out_b, a2_ln1_g, a2_ln1_b, a2_ln2_g, a2_ln2_b, a2_l1_w, a2_l1_b, a2_l2_w, a2_l2_b):
        import jax, jax.numpy as jnp
        import numpy as np
        D, NH, FF, M = (128, 8, 512, 128)
        HD = D // NH
        B, N = (8, 1024)

        def _ln(x, g, b):
            mu = jnp.mean(x, axis=-1, keepdims=True)
            var = jnp.var(x, axis=-1, keepdims=True)
            return (x - mu) / jnp.sqrt(var + 1e-05) * g + b

        def _mha(q, k, v, in_w, in_b, out_w, out_b):
            wq, wk, wv = jnp.split(in_w, 3, axis=0)
            bq, bk, bv = jnp.split(in_b, 3)
            qh = (q @ wq.T + bq).reshape(q.shape[0], q.shape[1], NH, HD)
            kh = (k @ wk.T + bk).reshape(k.shape[0], k.shape[1], NH, HD)
            vh = (v @ wv.T + bv).reshape(v.shape[0], v.shape[1], NH, HD)
            scores = jnp.einsum('bqhd,bkhd->bhqk', qh, kh) / jnp.sqrt(jnp.asarray(HD, qh.dtype))
            attn = jax.nn.softmax(scores, axis=-1)
            o = jnp.einsum('bhqk,bkhd->bqhd', attn, vh).reshape(q.shape[0], q.shape[1], D)
            return o @ out_w.T + out_b

        def _mab(q, k, v, p):
            in_w, in_b, out_w, out_b, g1, b1, g2, b2, l1w, l1b, l2w, l2b = p
            x = q + _mha(_ln(q, g1, b1), _ln(k, g1, b1), _ln(v, g1, b1), in_w, in_b, out_w, out_b)
            h = _ln(x, g2, b2)
            ff = jax.nn.gelu(h @ l1w.T + l1b, approximate=False) @ l2w.T + l2b
            return x + ff

        def _block_params(key, scale=0.02):
            ks = jax.random.split(key, 4)
            return dict(in_w=jax.random.normal(ks[0], (3 * D, D), jnp.float32) * scale, in_b=jnp.zeros((3 * D,), jnp.float32), out_w=jax.random.normal(ks[1], (D, D), jnp.float32) * scale, out_b=jnp.zeros((D,), jnp.float32), ln1_g=jnp.ones((D,), jnp.float32), ln1_b=jnp.zeros((D,), jnp.float32), ln2_g=jnp.ones((D,), jnp.float32), ln2_b=jnp.zeros((D,), jnp.float32), l1_w=jax.random.normal(ks[2], (FF, D), jnp.float32) * scale, l1_b=jnp.zeros((FF,), jnp.float32), l2_w=jax.random.normal(ks[3], (D, FF), jnp.float32) * scale, l2_b=jnp.zeros((D,), jnp.float32))
        p1 = (a1_in_w, a1_in_b, a1_out_w, a1_out_b, a1_ln1_g, a1_ln1_b, a1_ln2_g, a1_ln2_b, a1_l1_w, a1_l1_b, a1_l2_w, a1_l2_b)
        p2 = (a2_in_w, a2_in_b, a2_out_w, a2_out_b, a2_ln1_g, a2_ln1_b, a2_ln2_g, a2_ln2_b, a2_l1_w, a2_l1_b, a2_l2_w, a2_l2_b)
        ind_b = jnp.broadcast_to(ind, (x.shape[0], M, D))
        h = _mab(ind_b, x, x, p1)
        return _mab(x, h, h, p2)

    def _L0_ffn_ref(inp, ln_g, ln_b, wg_group, wg_inner, W1, b1, W2, b2, gln_g, gln_b):
        import jax, jax.numpy as jnp
        import numpy as np
        B, T, D, H = (2, 256, 128, 512)
        G, E = (4, 8)
        GK, EK = (2, 2)
        EPS = 1e-05
        SCALE = 0.02

        def _layernorm(x, g, b):
            m = jnp.mean(x, axis=-1, keepdims=True)
            xc = x - m
            v = jnp.mean(xc * xc, axis=-1, keepdims=True)
            return xc * jax.lax.rsqrt(v + EPS) * g + b

        def _topk_gate(logits, k, n):
            v, i = jax.lax.top_k(logits, k)
            sc = jax.nn.softmax(v, axis=-1)
            return jnp.sum(jax.nn.one_hot(i, n, dtype=logits.dtype) * sc[..., None], axis=-2)
        b, t, d = inp.shape
        x = inp.reshape(-1, d)
        gw = _topk_gate(x @ wg_group, GK, G)
        z = _layernorm(x, ln_g, ln_b)
        out = jnp.zeros_like(x)
        for g in range(G):
            iw = _topk_gate(z @ wg_inner[g], EK, E)
            moe = jnp.zeros_like(z)
            for e in range(E):
                h = jax.nn.relu(z @ W1[g, e] + b1[g, e])
                moe = moe + iw[:, e:e + 1] * (h @ W2[g, e] + b2[g, e])
            y = _layernorm(z + moe, gln_g[g], gln_b[g])
            out = out + gw[:, g:g + 1] * y
        return out.reshape(b, t, d) + inp
    h = _L0_tok_ref(x, mask_BS_i1_0, itok_BS_0_999, itok_BS_0_63, itok_BS_0_63, itok_BS_0_63, mask_BS_i0_1, mask_BS_b0_1, 0, L0_tok_emb, L0_tok_Wq, L0_tok_bq, L0_tok_Wk, L0_tok_bk, L0_tok_Wv, L0_tok_bv, L0_tok_Wo, L0_tok_bo, L0_tok_W1, L0_tok_b1, L0_tok_W2, L0_tok_b2, L0_tok_g1, L0_tok_beta1, L0_tok_g2, L0_tok_beta2, L0_tok_gf, L0_tok_betaf, L0_tok_Wc, L0_tok_bc)
    h = h + _L0_attn_ref(_layernorm(h, axis=-1), L0_attn_ind, L0_attn_a1_in_w, L0_attn_a1_in_b, L0_attn_a1_out_w, L0_attn_a1_out_b, L0_attn_a1_ln1_g, L0_attn_a1_ln1_b, L0_attn_a1_ln2_g, L0_attn_a1_ln2_b, L0_attn_a1_l1_w, L0_attn_a1_l1_b, L0_attn_a1_l2_w, L0_attn_a1_l2_b, L0_attn_a2_in_w, L0_attn_a2_in_b, L0_attn_a2_out_w, L0_attn_a2_out_b, L0_attn_a2_ln1_g, L0_attn_a2_ln1_b, L0_attn_a2_ln2_g, L0_attn_a2_ln2_b, L0_attn_a2_l1_w, L0_attn_a2_l1_b, L0_attn_a2_l2_w, L0_attn_a2_l2_b)
    h = h + _L0_ffn_ref(_layernorm(h, axis=-1), L0_ffn_ln_g, L0_ffn_ln_b, L0_ffn_wg_group, L0_ffn_wg_inner, L0_ffn_W1, L0_ffn_b1, L0_ffn_W2, L0_ffn_b2, L0_ffn_gln_g, L0_ffn_gln_b)
    return h

_drawn_inputs = setup_inputs


def setup_inputs(seed=0):
    import zlib

    import numpy as np

    out = dict(_drawn_inputs(seed))
    spreads = {'L0_tok_bq': (0.0, 2.0),
     'L0_tok_bk': (0.0, 2.0),
     'L0_tok_bv': (0.0, 0.1),
     'L0_tok_bo': (0.0, 0.1),
     'L0_tok_b1': (0.0, 0.1),
     'L0_tok_b2': (0.0, 0.1),
     'L0_tok_g1': (1.0, 0.2),
     'L0_tok_beta1': (0.0, 0.1),
     'L0_tok_g2': (1.0, 0.2),
     'L0_tok_beta2': (0.0, 0.1),
     'L0_tok_gf': (1.0, 0.2),
     'L0_tok_betaf': (0.0, 0.1),
     'L0_tok_bc': (0.0, 0.1),
     'L0_attn_a1_in_b': (0.0, 0.8),
     'L0_attn_a1_out_b': (0.0, 0.8),
     'L0_attn_a1_ln1_g': (1.0, 0.6),
     'L0_attn_a1_ln1_b': (0.0, 0.8),
     'L0_attn_a1_ln2_g': (1.0, 0.6),
     'L0_attn_a1_ln2_b': (0.0, 0.8),
     'L0_attn_a1_l1_b': (0.0, 0.8),
     'L0_attn_a1_l2_b': (0.0, 0.8),
     'L0_attn_a2_in_b': (0.0, 0.427),
     'L0_attn_a2_out_b': (0.0, 0.1),
     'L0_attn_a2_ln1_g': (1.0, 0.6),
     'L0_attn_a2_ln1_b': (0.0, 0.8),
     'L0_attn_a2_ln2_g': (1.0, 0.6),
     'L0_attn_a2_ln2_b': (0.0, 0.8),
     'L0_attn_a2_l1_b': (0.0, 0.422),
     'L0_attn_a2_l2_b': (0.0, 0.1),
     'L0_ffn_ln_g': (1.0, 0.2),
     'L0_ffn_ln_b': (0.0, 0.291),
     'L0_ffn_b1': (0.0, 0.8),
     'L0_ffn_b2': (0.0, 0.533),
     'L0_ffn_gln_g': (1.0, 0.2),
     'L0_ffn_gln_b': (0.0, 0.334)}
    factors = {'L0_tok_Wq': 45.763,
     'L0_tok_Wk': 53.052,
     'L0_attn_ind': 8.0,
     'L0_attn_a1_in_w': 8.0,
     'L0_attn_a1_out_w': 8.0,
     'L0_attn_a1_l1_w': 8.0,
     'L0_attn_a1_l2_w': 8.0,
     'L0_attn_a2_in_w': 6.938,
     'L0_attn_a2_out_w': 2.872,
     'L0_ffn_wg_group': 8.0,
     'L0_ffn_wg_inner': 3.325,
     'L0_ffn_W1': 6.372,
     'L0_ffn_W2': 4.673}
    for name, (base, spread) in spreads.items():
        noise = np.random.default_rng([zlib.crc32(name.encode()), seed]).standard_normal(out[name].shape)
        drawn = base * np.exp(spread * noise) if base else spread * noise
        out[name] = jnp.asarray(drawn.astype(out[name].dtype))
    for name, factor in factors.items():
        out[name] = (out[name] * factor).astype(out[name].dtype)
    return out
```

```python
from contextlib import ExitStack

import numpy as np

import concourse.bass as bass
from concourse import mybir

F32, F32R, BF16 = mybir.dt.float32, mybir.dt.float32r, mybir.dt.bfloat16
I32, U8 = mybir.dt.int32, mybir.dt.uint8
ALU, ACT, AX = mybir.AluOpType, mybir.ActivationFunctionType, mybir.AxisListType

P = 128
B, S = 8, 512
NT = S // P
NB = 2
VOCAB = 128
D, H, DH = 192, 12, 16
KT = 2
DP = D // KT
LAYERS, FF = 2, 768
FC = FF // P
E = 128
IH = E // DH
IF = 512 // P
G, X, XH = 4, 8, 512
XC = XH // P
W17 = DH + 1
EPS = 1e-5
NEG = -1e9
X_SLOTS = (LAYERS + 1) * B + NB
KB_SLOTS = LAYERS * B + NB
RING = 6


class Phase:

    def __init__(self, nc, name, ctx, outer, rounds=True):
        self.nc, self.name, self.ctx, self.outer, self.sems = nc, name, ctx, outer, {}
        self.sem_ctx = ctx if rounds else outer
        self.done, self.go, self.seen = (self.lasting(x) for x in ("round_done", "round_go", "round_seen"))

    def sb(self, name, shape, dt=F32):
        return self.ctx.enter_context(self.nc.sbuf_tensor(f"{self.name}_{name}", shape, dt))

    def psum(self, name):
        return self.ctx.enter_context(self.nc.psum_tensor(f"{self.name}_{name}", [P, 512], F32))

    def lasting(self, name):
        return self.outer.enter_context(self.nc.semaphore(f"{self.name}_{name}"))

    def sem(self, name):
        self.sems[name] = self.sem_ctx.enter_context(self.nc.semaphore(f"{self.name}_{name}"))
        return self.sems[name]

    def wait_lasting(self, eng, sem, value):
        eng.wait_ge(sem, value)
        eng.sem_inc(self.seen, 1)

    def end_round(self, eng, i):
        eng.drain().then_inc(self.done, 1)
        eng.wait_ge(self.go, i + 1)
        eng.sem_inc(self.seen, 1)

    def zero_round(self, pool, i):
        pool.drain().then_inc(self.done, 1)
        pool.wait_ge(self.done, i * 5 + 5)
        pool.sem_inc(self.seen, 1)
        for s in self.sems.values():
            pool.sem_clear(s)
        pool.sem_inc(self.go, 1)


class Chain:

    def __init__(self, eng, sem):
        self.eng, self.sem, self.n = eng, sem, 0

    def mark(self, ins):
        self.n += 1
        ins.then_inc(self.sem, 1)
        return self.n

    def after(self, n=None):
        self.eng.wait_ge(self.sem, self.n if n is None else n)


class Tiles:

    def __init__(self, ph, banks, order):
        self.banks, self.number = banks, {key: n for n, key in enumerate(order)}
        assert len(self.number) == len(order)
        self.ring = len(banks)
        self.full = [ph.sem(f"full{b}") for b in range(self.ring)]
        self.free = [ph.sem(f"free{b}") for b in range(self.ring)]

    def claim(self, pe, key):
        n = self.number[key]
        if n >= self.ring:
            pe.wait_ge(self.free[n % self.ring], n // self.ring)
        return self.banks[n % self.ring]

    def filled(self, ins, key):
        ins.then_inc(self.full[self.number[key] % self.ring], 1)

    def take(self, eng, key):
        n = self.number[key]
        eng.wait_ge(self.full[n % self.ring], n // self.ring + 1)
        return self.banks[n % self.ring]

    def copied(self, ins, key):
        ins.then_inc(self.free[self.number[key] % self.ring], 1)

    def wait_copied(self, eng, key):
        n = self.number[key]
        eng.wait_ge(self.free[n % self.ring], n // self.ring + 1)


def embed(nc, a, outer):
    with ExitStack() as ctx:
        ph = Phase(nc, "embed", ctx, outer, rounds=False)
        N = B * S
        HALF = N // 8
        ids, idsf = ph.sb("ids", [P, N], I32), ph.sb("idsf", [P, N])
        onehot = ph.sb("onehot", [P, N])
        emb, vocab = ph.sb("emb", [VOCAB, D]), ph.sb("vocab", [P, 1])
        x = ph.sb("x_rows", [P, N // P, D])
        pad, padf = ph.sb("pad", [B, S], U8), ph.sb("padf", [B, S])
        kb = ph.sb("kb", [B, 2, S + 2])
        banks = [ph.psum(f"bank{b}") for b in range(RING)]
        loaded, pad_in, stored = ph.sem("loaded"), ph.sem("pad_in"), ph.sem("stored")
        casted, hot, biased = ph.sem("casted"), ph.sem("hot"), ph.sem("biased")
        tiles = Tiles(ph, banks, [t for t in range(N // P // 2)])
        block = ctx.enter_context(nc.Block())

        @block.sync
        def _(sp):
            sp.dma_start(emb[:, :], a["emb"]).then_inc(loaded, 16)
            sp.dma_start(vocab[:, :], a["iota"]).then_inc(loaded, 16)
            sp.dma_start(ids[:, :], a["ids"]).then_inc(loaded, 16)
            sp.dma_start(pad[:, :], a["pad"]).then_inc(pad_in, 16)
            sp.wait_ge(biased, 5)
            for slot in range(0, KB_SLOTS, B):
                n = min(B, KB_SLOTS - slot)
                sp.dma_start(a["kb"][slot:slot + n], kb[0:n, :, :]).then_inc(stored, 16)
            for b in range(B):
                for t in (2 * b, 2 * b + 1):
                    tiles.wait_copied(sp, t)
                sp.dma_start(a["x"][b], x[:, NT * b:NT * b + NT, :]).then_inc(stored, 16)
            for b in range(NB):
                sp.dma_start(a["x"][X_SLOTS - NB + b], x[:, NT * b:NT * b + NT, :]).then_inc(stored, 16)
            sp.wait_ge(stored, 16 * (-(-KB_SLOTS // B) + B + NB))

        @block.vector
        def _(dve):
            dve.wait_ge(loaded, 48)
            for c in range(8):
                part = slice(c * HALF, c * HALF + HALF)
                dve.tensor_copy(idsf[:, part], ids[:, part]).then_inc(casted, 1)
                dve.wait_ge(casted, c + 1)
                dve.tensor_scalar(onehot[:, part], idsf[:, part], vocab[:, 0:1], None,
                                  ALU.is_equal).then_inc(hot, 1)
            dve.wait_ge(pad_in, 16)
            dve.tensor_copy(padf[:, :], pad[:, :]).then_inc(biased, 1)
            dve.wait_ge(biased, 1)
            dve.tensor_scalar(padf[:, :], padf[:, :], 0.0, None, ALU.not_equal).then_inc(biased, 1)
            dve.wait_ge(biased, 2)
            dve.memset(kb[:, :, S:S + 2], 0.0)
            dve.tensor_scalar(kb[:, 0, 0:S], padf[:, :], -10000.0, None, ALU.mult)
            dve.tensor_scalar(kb[:, 1, 0:S], padf[:, :], -10000.0, None, ALU.mult).then_inc(biased, 1)
            dve.wait_ge(biased, 3)
            dve.memset(kb[:, 0, 0:1], -10000.0).then_inc(biased, 1)
            dve.memset(kb[:, 0, S + 1:S + 2], NEG).then_inc(biased, 1)

        @block.tensor
        def _(pe):
            for t in range(N // P // 2):
                pe.wait_ge(hot, t // 2 + 1)
                bank = tiles.claim(pe, t)
                for j in range(2):
                    tok = slice((2 * t + j) * P, (2 * t + j + 1) * P)
                    mm = pe.matmul(bank[:, j * D:j * D + D], onehot[:, tok], emb[:, :], start=True, stop=True)
                tiles.filled(mm, t)

        @block.scalar
        def _(act):
            for t in range(N // P // 2):
                bank = tiles.take(act, t)
                tiles.copied(act.activation(x[:, 2 * t:2 * t + 2, :], bank[:, 0:2 * D], ACT.Copy), t)


def tower(nc, a, outer):
    with ExitStack() as ctx:
        ph = Phase(nc, "tower", ctx, outer)
        wqk = ph.sb("wqk", [DP, 2, KT, D])
        wvo = ph.sb("wvo", [DP, 2, KT, D])
        w1, w2 = ph.sb("w1", [DP, KT, FF]), ph.sb("w2", [P, FC, D])
        rows = ph.sb("rows", [P, 5, D])
        rows2 = ph.sb("rows2", [P, 2, D])
        cols = ph.sb("cols", [DP, 4, KT])
        b1c = ph.sb("b1c", [P, FC])
        ident, identb = ph.sb("ident", [P, P]), ph.sb("identb", [P, P], BF16)
        mask = ph.sb("mask", [P, 2, P], BF16)
        onerow = ph.sb("onerow", [1, P], F32R)
        onesr = ph.sb("onesr", [1, S])
        heads = ph.sb("heads", [DP, KT, H])
        headrow = ph.sb("headrow", [H, D])
        ones12 = ph.sb("ones12", [H, 1])
        half = ph.sb("half", [P, NT])
        x = [ph.sb(f"x{s}", [P, NT, D]) for s in range(NB)]
        xb = [ph.sb(f"xb{s}", [P, NT, D]) for s in range(NB)]
        xT = [ph.sb(f"xT{s}", [DP, KT, S]) for s in range(NB)]
        qk = ph.sb("qk", [DP, 4, KT, S], F32R)
        q_st = [ph.sb(f"q_st{s}", [P, H // 2, S], F32R) for s in range(NB)]
        k_st = [ph.sb(f"k_st{s}", [P, H // 2, S + 2], F32R) for s in range(NB)]
        v = [ph.sb(f"v{s}", [P, NT, H, W17]) for s in range(NB)]
        hid = [ph.sb(f"hid{s}", [P, FC, S]) for s in range(NB)]
        v0 = ph.sb("vglob", [P, NB, H, W17])
        padrow = ph.sb("padrow", [1, NB, S], F32R)
        prob = [ph.sb(f"prob{j}", [P, H, 2 + 3 * P]) for j in range(2)]
        probT = [ph.sb(f"probT{j}", [P, 3 * P]) for j in range(4)]
        negmax = ph.sb("negmax", [P, NB, NT * H])
        glob = ph.sb("glob", [P, H, W17])
        oT = ph.sb("oT", [P, 2, H // 4 * P])
        osum = ph.sb("osum", [P, H, W17])
        orec = ph.sb("orec", [P, H])
        qg = ph.sb("qg", [DP, 2, KT, P], F32R)
        pg = ph.sb("pg", [H, NB, S])
        pgst = ph.sb("pgst", [H, NB, 4])
        pgT = ph.sb("pgT", [P, NT, H])
        ogm = ph.sb("ogm", [H, D])
        st6, mv = ph.sb("st6", [P, NB, NT, 6]), ph.sb("mv", [P, NB, NT, 2])
        rstd = ph.sb("rstd", [P, NB, NT])
        banks = [ph.psum(f"bank{b}") for b in range(RING)]
        obank = [ph.psum(f"obank{b}") for b in range(2)]
        BV, BO, G1, BE1, B2 = range(5)
        G2, BE2 = range(2)

        STEPS = NT * H
        LAG_T, LAG_V = 2, 4
        LAG_R = 2
        QUERY_TILES = (1, 0, 2, 3)
        AT_T, AT_O, AT_1 = 8, 16, 34

        def step(k):
            place, h = divmod(k, H)
            return place, QUERY_TILES[place], h

        def row_tile(k):
            i, rest = divmod(k - LAG_V - LAG_R + 1, H)
            return i - 1 if i > 0 and rest == 0 else None

        order = []
        for s in range(NB):
            order += [("xT", s, k) for k in range(KT)]
        for s in range(NB):
            order += [("qk", s, w, m) for w in range(2) for m in range(KT)]
            order += [("v", s, t) for t in range(2)]
            order += [("v0", s), ("sg", s)]
        for s in range(NB):
            for k in range(STEPS + LAG_V + LAG_R):
                if k < STEPS:
                    order.append(("s", s, k))
                if k == AT_T:
                    order.append(("pgT", s))
                if k == AT_O:
                    order.append(("og", s))
                if k == AT_1:
                    order.append(("og1", s))
                if LAG_T <= k < STEPS + LAG_T:
                    order.append(("pT", s, k - LAG_T))
                if row_tile(k) is not None:
                    order.append(("rows", s, row_tile(k)))
        for s in range(NB):
            order += [("oT", s, k) for k in range(KT)]
        for s in range(NB):
            order += [("o", s, t) for t in range(2)]
        for s in range(NB):
            order += [("x1T", s, k) for k in range(KT)]
        for s in range(NB):
            order += [("up", s, c) for c in range(FC)]
        for s in range(NB):
            order += [("down", s, t) for t in range(2)]
        tiles = Tiles(ph, banks, order)
        o_full, o_free = ph.sem("o_full"), ph.sem("o_free")
        o_clear = ph.lasting("o_clear")

        weights_in, consts_in = ph.lasting("weights_in"), ph.lasting("consts_in")
        ones_in = ph.lasting("ones_in")
        consts_set, wq_scaled = ph.lasting("consts_set"), ph.lasting("wq_scaled")
        x_in, kb_in, pad_in = ph.lasting("x_in"), ph.lasting("kb_in"), ph.lasting("pad_in")
        x_out, x_stored, rows2_in = ph.lasting("x_out"), ph.sem("x_stored"), ph.lasting("rows2_in")
        split_hi = ph.sem("split_hi")
        qk_out, stacked = ph.sem("qk_out"), ph.sem("stacked")
        kglob = ph.sem("kglob")
        xb_ready, xb2_ready = ph.sem("xb_ready"), ph.sem("xb2_ready")
        qg_ready, rowmax = ph.sem("qg_ready"), ph.sem("rowmax")
        glob_ready, o_tok = ph.sem("glob_ready"), ph.sem("o_tok")
        pg_max, pg_norm = ph.sem("pg_max"), ph.sem("pg_norm")
        normed, moments, roots = ph.sem("normed"), ph.sem("moments"), ph.sem("roots")
        dve_chain, pool_chain = ph.sem("dve_chain"), ph.sem("pool_chain")
        x_final = ph.sem("x_final")
        block = ctx.enter_context(nc.Block())
        ROUNDS = B // NB
        LAST = LAYERS * ROUNDS
        NW = 7 * 16

        def blocks(i):
            return range(max(i - 1, 0), min(i + 2, NT))

        def stack(buf, h):
            return buf[64 * (h % 2):64 * (h % 2) + 3 * DH + 1, h // 2, :]

        @block.sync
        def _(sp):
            for dst, src in ((ident, "ident"), (identb, "identb"), (heads, "heads"), (headrow, "headrow")):
                sp.dma_start(dst[:], a[src]).then_inc(consts_in, 16)
            sp.dma_start(mask[:, :, :], a["mask"]).then_inc(consts_in, 16)
            sp.wait_ge(consts_set, 1)
            for s in range(NB):
                for par in range(2):
                    p = 64 * par + 3 * DH
                    for c in range(H // 2):
                        sp.dma_start(q_st[s][p:p + 1, c, :].bitcast(F32), onesr[:, :]).then_inc(ones_in, 16)

            def slot(t, n):
                return t[n:n + 1] if isinstance(n, int) else t[bass.ds(n, 1)]

            def load_weights(layer):
                for dst, src in ((wqk, "wqk"), (wvo, "wvo"), (w1, "w1"), (w2, "w2"), (rows, "rows"),
                                 (cols, "cols"), (b1c, "b1c")):
                    sp.dma_start(dst[:], a[src][layer]).then_inc(weights_in, 16)

            def load_rows2(layer):
                sp.dma_start(rows2[:], a["rows2"][layer]).then_inc(rows2_in, 16)

            def load_sequences(i):
                for s in range(NB):
                    sp.dma_start(xb[s][:, :, :], slot(a["x"], i * NB + s).rearrange("o p t d -> (o p) t d"))\
                        .then_inc(x_in, 16)
                for s in range(NB):
                    for par in range(2):
                        p = 64 * par + 3 * DH
                        sp.dma_start(k_st[s][p:p + 1, :, :].bitcast(F32),
                                     slot(a["kb"], i * NB + s)[:, 0:1, :].broadcast_to([1, H // 2, S + 2]))\
                            .then_inc(kb_in, 16)
                    sp.dma_start(padrow[:, s, :].bitcast(F32), slot(a["kb"], i * NB + s)[:, 1, 0:S])\
                        .then_inc(pad_in, 16)

            def store_sequences(i):
                for s in range(NB):
                    sp.wait_ge(x_final, s + 1)
                    dst = slot(a["x"], (i - 1 + ROUNDS) * NB + s)
                    sp.dma_start(dst.rearrange("o p t d -> (o p) t d"), x[s][:, :, :]).then_inc(x_out, 16)

            def round_(i, first=False, new_layer=None):
                for s in range(NB):
                    for w in range(2):
                        for m in range(KT):
                            tiles.wait_copied(sp, ("qk", s, w, m))
                    for w in range(4):
                        sp.dma_start(a["qk"][s, w].rearrange("(m p) q -> p m q", p=DP),
                                     qk[:, w, :, :].bitcast(F32)).then_inc(qk_out, 16)
                    sp.wait_ge(qk_out, 64 * (s + 1))
                    for buf, parts in ((q_st[s], (0, 1, 0)), (k_st[s], (2, 2, 3))):
                        for row, w in enumerate(parts):
                            src = a["qk"][s, w].rearrange("(c par d) q -> par d c q", par=2, d=DH)
                            for par in range(2):
                                p = 64 * par + DH * row
                                sp.dma_start(buf[p:p + DH, :, 0:S].bitcast(F32), src[par])\
                                    .then_inc(stacked, 16)
                if not first:
                    store_sequences(i)
                    ph.wait_lasting(sp, x_out, 16 * NB * i)
                sp.sem_inc(x_stored, 1)
                if new_layer is not None:
                    load_rows2(new_layer)
                    sp.wait_ge(rows2_in, 16 * (new_layer + 1))
                for s in range(NB):
                    for t in range(2):
                        tiles.wait_copied(sp, ("down", s, t))
                load_sequences(i + 1)
                ph.end_round(sp, i)

            load_sequences(0)
            for layer in range(LAYERS):
                first = layer * ROUNDS
                load_weights(layer)
                if layer == 0:
                    load_rows2(0)
                round_(first, first=layer == 0, new_layer=layer if layer else None)
                with sp.Fori(first + 1, first + ROUNDS) as i:
                    round_(i)
            store_sequences(LAST)
            sp.wait_ge(x_out, 16 * NB * LAST)
            sp.wait_ge(x_in, 16 * NB * (LAST + 1))
            sp.wait_ge(kb_in, 16 * 2 * NB * (LAST + 1))
            sp.wait_ge(pad_in, 16 * NB * (LAST + 1))
            ph.end_round(sp, LAST)

        @block.gpsimd
        def _(pool):
            pool.memset(onesr[:, :], 1.0).then_inc(consts_set, 1)
            pool.memset(half[:, :], -0.5).then_inc(consts_set, 1)
            pool.memset(ones12[:, :], 1.0).then_inc(consts_set, 1)
            pool.memset(onerow[:, :].bitcast(F32), 1.0).then_inc(consts_set, 1)
            pool.memset(qg[:, :, :, :].bitcast(F32), 0.0).then_inc(consts_set, 1)
            for s in range(NB):
                pool.memset(v[s][:, :, :, DH:W17], 1.0).then_inc(consts_set, 1)
                pool.memset(x[s][:, :, :], 0.0).then_inc(consts_set, 1)
            pool.wait_ge(consts_in, 80)
            pool.wait_ge(rows2_in, 16)

            def root(ch, n, s):
                pool.wait_ge(moments, n + 1)
                ch.mark(pool.tensor_scalar(rstd[:, s, :], mv[:, s, :, 1], EPS, None, ALU.add))
                ch.after()
                pool.tensor_tensor(rstd[:, s, :], rstd[:, s, :], half[:, :], ALU.pow).then_inc(roots, 1)

            def finish(ch, s):
                pool.wait_ge(normed, s + 1)
                ch.mark(pool.tensor_tensor(x[s][:, :, :], x[s][:, :, :],
                                           rows2[:, G2:G2 + 1, :].broadcast_to([P, NT, D]), ALU.mult))
                ch.after()
                pool.tensor_tensor(x[s][:, :, :], x[s][:, :, :],
                                   rows2[:, BE2:BE2 + 1, :].broadcast_to([P, NT, D]), ALU.add)\
                    .then_inc(x_final, 1)

            with pool.Fori(0, LAYERS) as layer:
                with pool.Fori(0, ROUNDS) as r:
                    pool.wait_ge(consts_set, 5 + 2 * NB)
                    ch = Chain(pool, pool_chain)
                    ph.wait_lasting(pool, weights_in, NW * (layer + 1))
                    ph.wait_lasting(pool, x_in, 16 * NB * (layer * ROUNDS + r + 1))
                    for s in range(NB):
                        root(ch, s, s)
                    for s in range(NB):
                        for m in range(KT):
                            tiles.wait_copied(pool, ("qk", s, 0, m))
                        if s:
                            tiles.take(pool, ("sg", s - 1))
                        for w in range(2):
                            for m in range(KT):
                                pool.tensor_scalar(qg[:, w, m, 0:H], heads[:, m, :],
                                                   qk[:, w, m, 0:1].bitcast(F32), None, ALU.mult)\
                                    .then_inc(qg_ready, 1)
                        finish(ch, s)
                    for s in range(NB):
                        for k in range(KT):
                            tiles.take(pool, ("xT", s, k))
                        pool.tensor_tensor(xb[s][:, :, :], xb[s][:, :, :],
                                           rows[:, BO:BO + 1, :].broadcast_to([P, NT, D]), ALU.add)\
                            .then_inc(xb_ready, 1)
                    for s in range(NB):
                        pool.wait_ge(stacked, 16 * 12 * (s + 1))
                        pool.wait_ge(qg_ready, 4 * NB)
                        for par in range(2):
                            for j in range(2):
                                if s + par + j:
                                    pool.wait_ge(kglob, 4 * s + 2 * par + j)
                                pool.tensor_copy(
                                    k_st[s][64 * par:64 * par + 3 * DH, :, S + j:S + j + 1],
                                    k_st[s][64 * par:64 * par + 3 * DH, :, 0:1].bitcast(F32)).then_inc(kglob, 1)
                    for s in range(NB):
                        for i in range(NT):
                            n = s * NT + i
                            pool.wait_ge(kglob, 4 * NB)
                            tiles.wait_copied(pool, ("v0", s))
                            tiles.wait_copied(pool, ("s", s, i * H + H - 1))
                            if n:
                                tiles.wait_copied(pool, ("rows", (n - 1) // NT, (n - 1) % NT))
                            pool.tensor_tensor(glob[:, :, :], v0[:, s, :, :],
                                               prob[i % 2][:, :, 0:1].broadcast_to([P, H, W17]), ALU.mult)\
                                .then_inc(glob_ready, 1)
                    for s in range(NB):
                        root(ch, NB + s, s)
                    for s in range(NB):
                        pool.wait_ge(normed, NB + s + 1)
                        for row, op in ((G1, ALU.mult), (BE1, ALU.add), (B2, ALU.add)):
                            ins = pool.tensor_tensor(xb[s][:, :, :], (x if row == G1 else xb)[s][:, :, :],
                                                     rows[:, row:row + 1, :].broadcast_to([P, NT, D]), op)
                            if row == B2:
                                ins.then_inc(xb2_ready, 1)
                            else:
                                ch.mark(ins)
                                ch.after()
                    ph.zero_round(pool, layer * ROUNDS + r)
            ch = Chain(pool, pool_chain)
            for s in range(NB):
                root(ch, s, s)
            for s in range(NB):
                finish(ch, s)
            ph.zero_round(pool, LAST)

        @block.tensor
        def _(pe):
            pe.wait_ge(consts_in, 80)
            pe.wait_ge(ones_in, 16 * NB * H)
            pe.wait_ge(consts_set, 5 + 2 * NB)
            pe.wait_ge(o_clear, 2)

            def transposes(key, src, tile_of, n):
                bank = tiles.claim(pe, key)
                for t in range(n):
                    mm = pe.transpose(bank[0:DP, t * P:t * P + P], tile_of(src, t), ident[:, :])
                tiles.filled(mm, key)

            def rows_product(key, lhs, rhs, kts, width):
                _, s, t2 = key
                bank = tiles.claim(pe, key)
                for j in range(2):
                    t = 2 * t2 + j
                    for k in range(kts):
                        mm = pe.matmul(bank[:, j * width:(j + 1) * width], lhs[:, k, t * P:t * P + P],
                                       rhs[:, k, :], start=(k == 0), stop=(k == kts - 1))
                tiles.filled(mm, key)

            with pe.Fori(0, LAYERS) as layer:
                with pe.Fori(0, ROUNDS) as r:
                    ph.wait_lasting(pe, weights_in, NW * (layer + 1))
                    ph.wait_lasting(pe, wq_scaled, layer + 1)
                    ph.wait_lasting(pe, x_in, 16 * NB * (layer * ROUNDS + r + 1))
                    for s in range(NB):
                        for k in range(KT):
                            transposes(("xT", s, k), xb[s], lambda b_, t, k=k: b_[:, t, k * DP:k * DP + DP], NT)
                    for s in range(NB):
                        for k in range(KT):
                            tiles.wait_copied(pe, ("xT", s, k))
                        for w in range(2):
                            for m in range(KT):
                                key = ("qk", s, w, m)
                                bank = tiles.claim(pe, key)
                                for k in range(KT):
                                    mm = pe.matmul(bank[0:DP, :], wqk[:, w, k, m * DP:m * DP + DP],
                                                   xT[s][:, k, :], start=(k == 0), stop=(k == KT - 1))
                                tiles.filled(mm, key)
                        for t in range(2):
                            rows_product(("v", s, t), xT[s], wvo[:, 0, :, :], KT, D)
                        tiles.wait_copied(pe, ("v", s, 0))
                        tiles.wait_copied(pe, ("v", s, 1))
                        bank = tiles.claim(pe, ("v0", s))
                        mm = pe.matmul(bank[:, 0:H * W17], onesr[0:1, 0:P],
                                       v[s][0:1, 0, :, :].rearrange("p h w -> p (h w)"), start=True, stop=True)
                        tiles.filled(mm, ("v0", s))
                        bank = tiles.claim(pe, ("sg", s))
                        pe.wait_ge(qg_ready, 4 * (s + 1))
                        ph.wait_lasting(pe, pad_in, 16 * NB * (layer * ROUNDS + r + 1))
                        n = 0
                        for m in range(KT):
                            for w, kw in ((0, 2), (1, 2), (0, 3)):
                                pe.matmul(bank[:, :], qg[:, w, m, :], qk[:, kw, m, :], start=(n == 0), stop=False)
                                n += 1
                        mm = pe.matmul(bank[:, :], onerow[:, :], padrow[:, s, :], start=False, stop=True)
                        tiles.filled(mm, ("sg", s))
                    for s in range(NB):
                        pe.wait_ge(stacked, 16 * 12 * (s + 1))
                        pe.wait_ge(kglob, 4 * (s + 1))
                        ph.wait_lasting(pe, kb_in, 16 * 2 * NB * (layer * ROUNDS + r + 1))
                        for k in range(STEPS + LAG_V + LAG_R):
                            if k < STEPS:
                                _, i, h = step(k)
                                bl = blocks(i)
                                key = ("s", s, k)
                                bank = tiles.claim(pe, key)
                                q, kk = stack(q_st[s], h)[:, i * P:i * P + P], stack(k_st[s], h)
                                pe.matmul(bank[:, 0:2], q, kk[:, S:S + 2], start=True, stop=True)
                                todo = [(2, 2 + len(bl) * P, q, kk[:, bl[0] * P:(bl[-1] + 1) * P])]
                                if i > 0:
                                    todo.append((2, 2 + P, identb[:, :], mask[:, 0, :]))
                                if i < NT - 1:
                                    e_ = 2 + len(bl) * P
                                    todo.append((e_ - P, e_, identb[:, :], mask[:, 1, :]))
                                for n, (c0, c1, lhs, rhs) in enumerate(todo):
                                    mm = pe.matmul(bank[:, c0:c1], lhs, rhs, start=(n == 0),
                                                   stop=(n == len(todo) - 1), skip_group_check=True)
                                tiles.filled(mm, key)
                            if k == AT_T:
                                pe.wait_ge(pg_norm, s + 1)
                                bank = tiles.claim(pe, ("pgT", s))
                                for t in range(NT):
                                    mm = pe.transpose(bank[:, t * H:t * H + H], pg[:, s, t * P:t * P + P], ident[0:H, 0:H])
                                tiles.filled(mm, ("pgT", s))
                            if k == AT_O:
                                tiles.wait_copied(pe, ("pgT", s))
                                bank = tiles.claim(pe, ("og", s))
                                for t in range(NT):
                                    mm = pe.matmul(bank[0:H, 0:D], pgT[:, t, :], v[s][:, t, :, 0:DH],
                                                   start=(t == 0), stop=(t == NT - 1))
                                tiles.filled(mm, ("og", s))
                            if k == AT_1:
                                tiles.wait_copied(pe, ("og", s))
                                bank = tiles.claim(pe, ("og1", s))
                                tiles.filled(pe.matmul(bank[0:1, 0:D], ones12[:, :], ogm[:, :], start=True, stop=True),
                                             ("og1", s))
                            if LAG_T <= k < STEPS + LAG_T:
                                kt = k - LAG_T
                                place, i, h = step(kt)
                                key = ("pT", s, kt)
                                bank = tiles.claim(pe, key)
                                tiles.wait_copied(pe, ("s", s, kt))
                                for j in range(len(blocks(i))):
                                    mm = pe.transpose(bank[:, j * P:j * P + P],
                                                      prob[place % 2][:, h, 2 + j * P:2 + j * P + P], ident[:, :])
                                tiles.filled(mm, key)
                            if LAG_V <= k < STEPS + LAG_V:
                                kv = k - LAG_V
                                place, i, h = step(kv)
                                n = s * NT + place
                                tiles.wait_copied(pe, ("pT", s, kv))
                                if h == 0 and n >= 2:
                                    pe.wait_ge(o_free, n - 1)
                                bl = blocks(i)
                                p, c = 32 * (h % 4), h // 4 * P
                                for j, t in enumerate(bl):
                                    mm = pe.matmul(obank[n % 2][p:p + W17, c:c + P], v[s][:, t, h, :],
                                                   probT[kv % 4][:, j * P:j * P + P],
                                                   start=(j == 0), stop=(j == len(bl) - 1))
                                if h == H - 1:
                                    mm.then_inc(o_full, 1)
                            if row_tile(k) is not None:
                                n = s * NT + row_tile(k)
                                key = ("rows", s, row_tile(k))
                                bank = tiles.claim(pe, key)
                                pe.wait_ge(o_free, n + 1)
                                for c in range(H // 4):
                                    mm = pe.transpose(bank[:, c * P:c * P + P], oT[:, n % 2, c * P:c * P + P],
                                                      ident[:, :])
                                tiles.filled(mm, key)
                    for s in range(NB):
                        pe.wait_ge(o_tok, NT * (s + 1))
                        tiles.wait_copied(pe, ("og1", s))
                        for k in range(KT):
                            transposes(("oT", s, k), x[s], lambda b_, t, k=k: b_[:, t, k * DP:k * DP + DP], NT)
                    for s in range(NB):
                        for k in range(KT):
                            tiles.wait_copied(pe, ("oT", s, k))
                        for t in range(2):
                            rows_product(("o", s, t), xT[s], wvo[:, 1, :, :], KT, D)
                    for s in range(NB):
                        pe.wait_ge(normed, NB + s + 1)
                        for k in range(KT):
                            transposes(("x1T", s, k), x[s], lambda b_, t, k=k: b_[:, t, k * DP:k * DP + DP], NT)
                    for s in range(NB):
                        for k in range(KT):
                            tiles.wait_copied(pe, ("x1T", s, k))
                        for c in range(FC):
                            key = ("up", s, c)
                            bank = tiles.claim(pe, key)
                            for k in range(KT):
                                mm = pe.matmul(bank[:, :], w1[:, k, c * P:c * P + P], xT[s][:, k, :],
                                               start=(k == 0), stop=(k == KT - 1))
                            tiles.filled(mm, key)
                    for s in range(NB):
                        for c in range(FC):
                            tiles.wait_copied(pe, ("up", s, c))
                        for t in range(2):
                            rows_product(("down", s, t), hid[s], w2, FC, D)
                    ph.end_round(pe, layer * ROUNDS + r)
            ph.end_round(pe, LAST)

        @block.scalar
        def _(act):
            with act.Fori(0, LAYERS) as layer:
                with act.Fori(0, ROUNDS) as r:
                    ph.wait_lasting(act, weights_in, NW * (layer + 1))
                    ph.wait_lasting(act, wq_scaled, layer + 1)
                    for s in range(NB):
                        bank = tiles.take(act, ("xT", s, 0))
                        tiles.copied(act.activation(xT[s][:, 0, :], bank[0:DP, :], ACT.Copy), ("xT", s, 0))
                    for s in range(NB):
                        for w in range(2):
                            for m in range(KT):
                                bank = tiles.take(act, ("qk", s, w, m))
                                if s:
                                    act.wait_ge(qk_out, 64 * s)
                                    tiles.take(act, ("sg", s - 1))
                                act.activation(qk[:, 2 * w, m, :], bank[0:DP, :], ACT.Identity,
                                               bias=cols[:, w, m:m + 1]).then_inc(split_hi, 1)
                        bank = tiles.take(act, ("sg", s))
                        act.wait_ge(pg_max, s + 1)
                        tiles.copied(act.activation(pg[:, s, :], bank[0:H, :], ACT.Exp, bias=pgst[:, s, 0:1],
                                                    accum_out=pgst[:, s, 1:2]), ("sg", s))
                    for s in range(NB):
                        for k in range(STEPS + LAG_V + 1):
                            if k < STEPS:
                                place, i, h = step(k)
                                n = s * NT + place
                                if h == 0 and n >= 2:
                                    act.wait_ge(glob_ready, n - 1)
                                    tiles.take(act, ("pT", (n - 2) // NT, ((n - 2) % NT) * H + H - 1))
                                bank = tiles.take(act, ("s", s, k))
                                act.wait_ge(rowmax, s * STEPS + k + 1)
                                w_ = 2 + len(blocks(i)) * P
                                tiles.copied(act.activation(prob[place % 2][:, h, 0:w_], bank[:, 0:w_], ACT.Exp,
                                                            bias=negmax[:, s, k:k + 1]), ("s", s, k))
                            if LAG_T <= k < STEPS + LAG_T and (k - LAG_T) % 2:
                                kt = k - LAG_T
                                bank = tiles.take(act, ("pT", s, kt))
                                w_ = len(blocks(step(kt)[1])) * P
                                tiles.copied(act.activation(probT[kt % 4][:, 0:w_], bank[:, 0:w_], ACT.Copy),
                                             ("pT", s, kt))
                            if k > LAG_V and (k - LAG_V) % H == 0:
                                n = s * NT + (k - LAG_V) // H - 1
                                if n >= 2:
                                    tiles.take(act, ("rows", (n - 2) // NT, (n - 2) % NT))
                                act.wait_ge(o_full, n + 1)
                                act.activation(oT[:, n % 2, :], obank[n % 2][:, 0:H // 4 * P], ACT.Copy)\
                                    .then_inc(o_free, 1)
                    for s in range(NB):
                        bank = tiles.take(act, ("oT", s, 0))
                        tiles.copied(act.activation(xT[s][:, 0, :], bank[0:DP, :], ACT.Copy), ("oT", s, 0))
                    for s in range(NB):
                        bank = tiles.take(act, ("x1T", s, 0))
                        tiles.copied(act.activation(xT[s][:, 0, :], bank[0:DP, :], ACT.Identity,
                                                    scale=cols[:, 2, 0:1], bias=cols[:, 3, 0:1]), ("x1T", s, 0))
                    for s in range(NB):
                        for c in range(0, FC, 2):
                            bank = tiles.take(act, ("up", s, c))
                            tiles.copied(act.activation(hid[s][:, c, :], bank[:, :], ACT.Relu,
                                                        bias=b1c[:, c:c + 1]), ("up", s, c))
                    ph.end_round(act, layer * ROUNDS + r)
            ph.end_round(act, LAST)

        @block.vector
        def _(dve):
            for bank in obank:
                dve.memset(bank[:, :], 0.0).then_inc(o_clear, 1)
            dve.wait_ge(consts_set, 5 + 2 * NB)

            def statistics(ch, s):
                for t in range(NT):
                    ins = dve.bn_stats(st6[:, s, t, :], x[s][:, t, :])
                ch.mark(ins)
                ch.after()
                for t in range(NT):
                    ins = dve.bn_aggr(mv[:, s, t, :], st6[:, s, t, :])
                ins.then_inc(moments, 1)

            def normalise(n, s):
                dve.wait_ge(moments, n + 1)
                dve.wait_ge(roots, n + 1)
                for t in range(NT):
                    ins = dve.tensor_scalar(x[s][:, t, :], x[s][:, t, :], mv[:, s, t, 0:1],
                                            rstd[:, s, t:t + 1], ALU.subtract, ALU.mult)
                ins.then_inc(normed, 1)

            with dve.Fori(0, LAYERS) as layer:
                ph.wait_lasting(dve, weights_in, NW * (layer + 1))
                dve.tensor_scalar(wqk[:, 0, :, :], wqk[:, 0, :, :], DH ** -0.5, None, ALU.mult)
                dve.tensor_scalar(cols[:, 0, :], cols[:, 0, :], DH ** -0.5, None, ALU.mult).then_inc(wq_scaled, 1)
                with dve.Fori(0, ROUNDS) as r:
                    ph.wait_lasting(dve, wq_scaled, layer + 1)
                    ch = Chain(dve, dve_chain)
                    for s in range(NB):
                        bank = tiles.take(dve, ("xT", s, 1))
                        tiles.copied(dve.tensor_copy(xT[s][:, 1, :], bank[0:DP, :]), ("xT", s, 1))
                    for s in range(NB):
                        statistics(ch, s)
                    for s in range(NB):
                        for w in range(2):
                            for m in range(KT):
                                dve.wait_ge(split_hi, s * 4 + w * KT + m + 1)
                                key = ("qk", s, w, m)
                                bank = tiles.take(dve, key)
                                tiles.copied(dve.scalar_tensor_tensor(
                                    qk[:, 2 * w + 1, m, :], bank[0:DP, :], cols[:, w, m:m + 1],
                                    qk[:, 2 * w, m, :].bitcast(F32), ALU.add, ALU.subtract), key)
                        normalise(s, s)
                        for t in range(2):
                            bank = tiles.take(dve, ("v", s, t))
                            tiles.copied(dve.tensor_tensor(
                                v[s][:, 2 * t:2 * t + 2, :, 0:DH],
                                bank[:, 0:2 * D].rearrange("p (t h d) -> p t h d", t=2, d=DH),
                                rows[:, BV:BV + 1, :].broadcast_to([P, 2, D])
                                .rearrange("p t (h d) -> p t h d", d=DH), ALU.add), ("v", s, t))
                        bank = tiles.take(dve, ("v0", s))
                        tiles.copied(dve.tensor_copy(v0[:, s, :, :].rearrange("p h w -> p (h w)"),
                                                     bank[:, 0:H * W17]), ("v0", s))
                        bank = tiles.take(dve, ("sg", s))
                        dve.tensor_reduce(pgst[:, s, 0:1], bank[0:H, :], AX.X, ALU.max, negate=True)\
                            .then_inc(pg_max, 1)
                        tiles.wait_copied(dve, ("sg", s))
                        ch.mark(dve.reciprocal(pgst[:, s, 2:3], pgst[:, s, 1:2]))
                        ch.after()
                        dve.tensor_scalar(pg[:, s, :], pg[:, s, :], pgst[:, s, 2:3], None, ALU.mult)\
                            .then_inc(pg_norm, 1)
                    for s in range(NB):
                        def gather(i):
                            n = s * NT + i
                            dve.wait_ge(glob_ready, n + 1)
                            bank = tiles.take(dve, ("rows", s, i))
                            tiles.copied(dve.tensor_tensor(
                                osum[:, :, :], bank[:, 0:H * 32].rearrange("p (h w) -> p h w", w=32)[:, :, 0:W17],
                                glob[:, :, :], ALU.add), ("rows", s, i))
                            tiles.wait_copied(dve, ("rows", s, i))
                            ch.mark(dve.reciprocal(orec[:, :], osum[:, :, DH]))
                            ch.after()
                            dve.wait_ge(x_stored, 1)
                            dve.tensor_tensor(x[s][:, QUERY_TILES[i], :].rearrange("p (h d) -> p h d", d=DH),
                                              osum[:, :, 0:DH],
                                              orec[:, :, None].broadcast_to([P, H, DH]), ALU.mult)\
                                .then_inc(o_tok, 1)

                        for k in range(STEPS + LAG_V + LAG_R + 1):
                            if k < STEPS:
                                bank = tiles.take(dve, ("s", s, k))
                                w_ = 2 + len(blocks(step(k)[1])) * P
                                dve.tensor_reduce(negmax[:, s, k:k + 1], bank[:, 0:w_], AX.X, ALU.max,
                                                  negate=True).then_inc(rowmax, 1)
                            if k == AT_T + 1:
                                bank = tiles.take(dve, ("pgT", s))
                                tiles.copied(dve.tensor_copy(pgT[:, :, :].rearrange("p t h -> p (t h)"),
                                                             bank[:, 0:NT * H]), ("pgT", s))
                            if k == AT_O + 1:
                                bank = tiles.take(dve, ("og", s))
                                tiles.copied(dve.tensor_tensor(ogm[:, :], bank[0:H, 0:D], headrow[:, :], ALU.mult),
                                             ("og", s))
                            if k == AT_1 + 1:
                                dve.wait_ge(o_tok, s * NT + QUERY_TILES.index(0) + 1)
                                bank = tiles.take(dve, ("og1", s))
                                tiles.copied(dve.tensor_copy(x[s][0:1, 0, :], bank[0:1, 0:D]), ("og1", s))
                            if LAG_T <= k < STEPS + LAG_T and (k - LAG_T) % 2 == 0:
                                kt = k - LAG_T
                                bank = tiles.take(dve, ("pT", s, kt))
                                w_ = len(blocks(step(kt)[1])) * P
                                tiles.copied(dve.tensor_copy(probT[kt % 4][:, 0:w_], bank[:, 0:w_]), ("pT", s, kt))
                            if row_tile(k - 1) is not None:
                                gather(row_tile(k - 1))

                    def residual(ln, key, base_sem, s):
                        for t in range(2):
                            bank = tiles.take(dve, (key, s, t))
                            if t == 0:
                                dve.wait_ge(base_sem, s + 1)
                                tiles.take(dve, (("oT", "x1T")[ln], s, KT - 1))
                                if ln:
                                    dve.wait_ge(xb2_ready, s + 1)
                            tiles.copied(dve.tensor_tensor(
                                x[s][:, 2 * t:2 * t + 2, :].rearrange("p t d -> p (t d)"), bank[:, 0:2 * D],
                                xb[s][:, 2 * t:2 * t + 2, :].rearrange("p t d -> p (t d)"), ALU.add), (key, s, t))
                        for t in range(2):
                            tiles.wait_copied(dve, (key, s, t))
                    for s in range(NB):
                        bank = tiles.take(dve, ("oT", s, 1))
                        tiles.copied(dve.tensor_copy(xT[s][:, 1, :], bank[0:DP, :]), ("oT", s, 1))
                    for s in range(NB):
                        residual(0, "o", xb_ready, s)
                        statistics(ch, s)
                    for s in range(NB):
                        normalise(NB + s, s)
                    for s in range(NB):
                        bank = tiles.take(dve, ("x1T", s, 1))
                        tiles.copied(dve.tensor_scalar(xT[s][:, 1, :], bank[0:DP, :], cols[:, 2, 1:2],
                                                       cols[:, 3, 1:2], ALU.mult, ALU.add), ("x1T", s, 1))
                    for s in range(NB):
                        for c in range(1, FC, 2):
                            bank = tiles.take(dve, ("up", s, c))
                            tiles.copied(dve.tensor_scalar(hid[s][:, c, :], bank[:, :], b1c[:, c:c + 1], 0.0,
                                                           ALU.add, ALU.max), ("up", s, c))
                    for s in range(NB):
                        residual(1, "down", xb2_ready, s)
                    ph.end_round(dve, layer * ROUNDS + r)
            ch = Chain(dve, dve_chain)
            for s in range(NB):
                statistics(ch, s)
            for s in range(NB):
                normalise(s, s)
            ph.end_round(dve, LAST)


def induce(nc, a, outer):
    with ExitStack() as ctx:
        ph = Phase(nc, "induce", ctx, outer)
        wc = ph.sb("wc", [DP, KT, E])
        fcols = ph.sb("fcols", [DP, 2, KT])
        bc = ph.sb("bc", [P, E])
        win = ph.sb("win", [E, 2, 3, E])
        wout = ph.sb("wout", [E, 2, E])
        l1, l2 = ph.sb("l1", [E, 2, 512]), ph.sb("l2", [P, 2, IF, E])
        ecols = ph.sb("ecols", [E, 2, 6])
        l1b = ph.sb("l1b", [P, 2, IF])
        erows = ph.sb("erows", [P, 2, 3, E])
        gcols, grows = ph.sb("gcols", [E, 2]), ph.sb("grows", [P, 2, E])
        wgate = ph.sb("wgate", [E, G + G * X])
        ind = ph.sb("ind", [P, 1, E])
        ident = ph.sb("ident", [P, P])
        half = ph.sb("half", [P, NT])
        rank = ph.sb("rank", [P, X])
        indT, q1 = ph.sb("indT", [E, P]), ph.sb("q1", [E, 2, P], F32R)
        q1_st = ph.sb("q1_st", [P, IH // 2, P], F32R)
        indb = ph.sb("indb", [P, E])

        def two(name, shape, dt=F32):
            return [ph.sb(f"{name}{s}", shape, dt) for s in range(NB)]

        x, xT = two("x", [P, NT, D]), two("xT", [DP, KT, S])
        h, x2, x3 = two("h", [P, NT, E]), two("x2", [P, NT, E]), two("x3", [P, NT, E])
        x2b = two("x2b", [P, NT, E])
        u1T, u2T = two("u1T", [E, S]), two("u2T", [E, S])
        kq = two("kq", [E, 4, S], F32R)
        k1_st, q2_st = two("k1_st", [P, IH // 2, S], F32R), two("q2_st", [P, IH // 2, S], F32R)
        k2, k2_st = two("k2", [E, 2, P], F32R), two("k2_st", [P, IH // 2, P], F32R)
        v1, v2 = two("v1", [P, NT, IH, W17]), two("v2", [P, IH, W17])
        o1, y1, y1b = two("o1", [P, E]), two("y1", [P, 1, E]), two("y1b", [P, E])
        t1, h1 = two("t1", [E, P]), two("h1", [P, 1, E])
        hid1, ukT = two("hid1", [P, IF, P]), two("ukT", [E, P])
        y2, y2b = two("y2", [P, NT, E]), two("y2b", [P, NT, E])
        hid2 = two("hid2", [P, IF, S])
        h2, x5, z = two("h2", [P, NT, E]), two("x5", [P, NT, E]), two("z", [P, NT, E])
        base = two("base", [P, NT, E])
        gates = two("gates", [P, NT * (G + 1), X])
        giT = two("giT", [G * X, S])
        prob = [ph.sb(f"prob{j}", [P, S]) for j in range(4)]
        probT = [ph.sb(f"probT{j}", [P, S]) for j in range(4)]
        rmax = ph.sb("rmax", [P, NB * IH, NT])
        orec = ph.sb("orec", [P, 2, IH])
        ga, gb, gc = (ph.sb(f"g{c}", [P, NT * (G + 1), X]) for c in "abc")
        gs = ph.sb("gs", [P, 6, NT * (G + 1)])
        st6, mv = ph.sb("st6", [P, NB, NT, 6]), ph.sb("mv", [P, NB, NT, 2])
        rstd = ph.sb("rstd", [P, NB, NT])
        banks = [ph.psum(f"bank{b}") for b in range(RING)]
        obank = [ph.psum(f"obank{b}") for b in range(2)]

        LAG_T, LAG_V = 2, 4
        AT_ROWS = 2
        seqs = range(NB)
        att = {1: [], 2: []}
        for at in (1, 2):
            for s in seqs:
                for k in range(IH + LAG_V):
                    if k < IH:
                        att[at].append((f"s{at}", s, k))
                    if LAG_T <= k < IH + LAG_T:
                        att[at].append((f"p{at}T", s, k - LAG_T))
                    if s and k == AT_ROWS:
                        att[at] += [(f"o{at}R", s - 1, c) for c in range(at)]
                if s == NB - 1:
                    att[at] += [(f"o{at}R", s, c) for c in range(at)]

        def each(*names):
            return [(n, s) for s in seqs for n in names]

        order = ([("xT", s, k) for s in seqs for k in range(KT)] + each("logits") + each("u")
                 + each("k1", "q2", "v1") + att[1] + each("o1T") + each("y1") + each("t1") + each("up1")
                 + each("down1") + each("uk") + each("k2", "v2") + att[2] + each("o2T") + each("y2") + each("t2")
                 + [("up2", s, c) for s in seqs for c in range(IF)] + each("down2") + each("x5T") + each("zT")
                 + each("gate") + each("giT"))
        tiles = Tiles(ph, banks, order)
        LNS = {(n, s): i * NB + s for i, n in enumerate(
            ("final", "x2", "x3", "y1", "h1", "y2", "x5", "z")) for s in seqs}
        ROWS = {"y1": 1, "h1": 1}

        weights_in, points = ph.lasting("weights_in"), ph.lasting("points")
        consts_set, scaled = ph.lasting("consts_set"), ph.lasting("scaled")
        q1_out, q1_in = ph.lasting("q1_out"), ph.lasting("q1_in")
        x_in, split_hi = ph.lasting("x_in"), ph.sem("split_hi")
        kq_out, stacked = ph.sem("kq_out"), ph.sem("stacked")
        k2_out, stacked2 = ph.sem("k2_out"), ph.sem("stacked2")
        rowmax, expd2 = ph.sem("rowmax"), ph.sem("expd2")
        o1_full, o1_free, o2_full, o2_free = (ph.sem(n) for n in ("o1_full", "o1_free", "o2_full", "o2_free"))
        o_clear = ph.lasting("o_clear")
        moments, roots, normed = ph.sem("moments"), ph.sem("roots"), ph.sem("normed")
        x2b_ready, y1b_ready, y2b_ready = ph.sem("x2b_ready"), ph.sem("y1b_ready"), ph.sem("y2b_ready")
        base_ready, z_ready = ph.sem("base_ready"), ph.sem("z_ready")
        gexp_in, gexp_out, gates_set = ph.sem("gexp_in"), ph.sem("gexp_out"), ph.sem("gates_set")
        dve_chain, pool_chain = ph.sem("dve_chain"), ph.sem("pool_chain")
        stored = ph.sem("stored")
        block = ctx.enter_context(nc.Block())
        ROUNDS = B // NB
        BQ, BK, LG1, LB1, LG2, LB2 = range(6)
        BV, BOUT, BL2 = range(3)
        loads = ((wc, "wc"), (fcols, "fcols"), (bc, "bc"), (win, "win"), (wout, "wout"), (l1, "l1"), (l2, "l2"),
                 (ecols, "ecols"), (l1b, "l1b"), (erows, "erows"), (gcols, "gcols"), (grows, "grows"),
                 (wgate, "wgate"), (ind, "ind"), (ident, "ident"), (rank, "rank"))
        NLOADS = 16 * len(loads)

        def stack(buf, head):
            return buf[64 * (head % 2):64 * (head % 2) + 3 * DH, head // 2, :]

        def restack(sp, buf, src_of, sem):
            for row in range(3):
                src = src_of(row).rearrange("(c par d) q -> par d c q", par=2, d=DH)
                for par in range(2):
                    p = 64 * par + DH * row
                    sp.dma_start(buf[p:p + DH, :, :].bitcast(F32), src[par]).then_inc(sem, 16)

        @block.sync
        def _(sp):
            for dst, src in loads:
                sp.dma_start(dst[:], a[src]).then_inc(weights_in, 16)
            sp.wait_ge(points, 10)
            for w in range(2):
                sp.dma_start(a["q1"][w], q1[:, w, :].bitcast(F32)).then_inc(q1_out, 16)
            sp.wait_ge(q1_out, 32)
            restack(sp, q1_st, lambda row: a["q1"][(0, 1, 0)[row]], q1_in)
            def load_x(r):
                for s in seqs:
                    n = LAYERS * B + r * NB + s
                    src = a["x"][n:n + 1] if isinstance(n, int) else a["x"][bass.ds(n, 1)]
                    sp.dma_start(x[s][:, :, :], src.rearrange("o p t d -> (o p) t d")).then_inc(x_in, 16)

            load_x(0)
            with sp.Fori(0, ROUNDS) as r:
                def seq(t, s):
                    return t[bass.ds(r * NB + s, 1)]
                for s in seqs:
                    for k in range(KT):
                        tiles.take(sp, ("xT", s, k))
                load_x(r + 1)
                for s in seqs:
                    for key in ("k1", "q2"):
                        tiles.wait_copied(sp, (key, s))
                    sp.dma_start(a["kq"][s].rearrange("w p q -> p w q"), kq[s][:, :, :].bitcast(F32))\
                        .then_inc(kq_out, 16)
                    sp.wait_ge(kq_out, 16 * (s + 1))
                    restack(sp, k1_st[s], lambda row, s=s: a["kq"][s, (0, 0, 1)[row]], stacked)
                    restack(sp, q2_st[s], lambda row, s=s: a["kq"][s, (2, 3, 2)[row]], stacked)
                for s in seqs:
                    tiles.wait_copied(sp, ("k2", s))
                    sp.dma_start(a["k2"][s].rearrange("w p q -> p w q"), k2[s][:, :, :].bitcast(F32))\
                        .then_inc(k2_out, 16)
                    sp.wait_ge(k2_out, 16 * (s + 1))
                    restack(sp, k2_st[s], lambda row, s=s: a["k2"][s, (0, 0, 1)[row]], stacked2)
                for s in seqs:
                    sp.wait_ge(base_ready, s + 1)
                    sp.dma_start(seq(a["base"], s).rearrange("o p t d -> (o p) t d"), base[s][:, :, :])\
                        .then_inc(stored, 16)
                    sp.wait_ge(z_ready, s + 1)
                    sp.dma_start(seq(a["z"], s).rearrange("o p t d -> (o p) t d"), z[s][:, :, :])\
                        .then_inc(stored, 16)
                for s in seqs:
                    tiles.wait_copied(sp, ("zT", s))
                    sp.dma_start(seq(a["zT"], s).rearrange("o p q -> (o p) q"), hid2[s][:, 1, :])\
                        .then_inc(stored, 16)
                for s in seqs:
                    sp.wait_ge(gates_set, s + 1)
                    sp.dma_start(seq(a["gates"], s).rearrange("o p t d -> (o p) t d"), gates[s][:, :, :])\
                        .then_inc(stored, 16)
                for s in seqs:
                    tiles.wait_copied(sp, ("giT", s))
                    sp.dma_start(seq(a["giT"], s).rearrange("o p q -> (o p) q"), giT[s][:, :]).then_inc(stored, 16)
                sp.wait_ge(stored, 16 * 5 * NB)
                ph.end_round(sp, r)
            sp.wait_ge(x_in, 16 * NB * (ROUNDS + 1))

        @block.gpsimd
        def _(pool):
            pool.memset(half[:, :], -0.5).then_inc(consts_set, 1)
            for s in seqs:
                pool.memset(v1[s][:, :, :, DH:W17], 1.0).then_inc(consts_set, 1)
                pool.memset(v2[s][:, :, DH:W17], 1.0).then_inc(consts_set, 1)
            pool.wait_ge(consts_set, 1 + 2 * NB)
            pool.wait_ge(points, 2)
            pool.tensor_scalar(rstd[:, 0, 0:1], mv[:, 0, 0:1, 1], EPS, None, ALU.add).then_inc(points, 1)
            pool.wait_ge(points, 3)
            pool.tensor_tensor(rstd[:, 0, 0:1], rstd[:, 0, 0:1], half[:, 0:1], ALU.pow).then_inc(points, 1)
            with pool.Fori(0, ROUNDS) as r:
                ch = Chain(pool, pool_chain)

                def root(name):
                    n = ROWS.get(name, NT)
                    for s in seqs:
                        pool.wait_ge(moments, LNS[name, s] + 1)
                        ch.mark(pool.tensor_scalar(rstd[:, s, 0:n], mv[:, s, 0:n, 1], EPS, None, ALU.add))
                        ch.after()
                        pool.tensor_tensor(rstd[:, s, 0:n], rstd[:, s, 0:n], half[:, 0:n], ALU.pow)\
                            .then_inc(roots, 1)

                root("final")
                root("x2")
                root("x3")
                for s in seqs:
                    pool.wait_ge(normed, LNS["x2", s] + 1)
                    pool.tensor_tensor(x2b[s][:, :, :], x2[s][:, :, :],
                                       erows[:, 1, BOUT:BOUT + 1, :].broadcast_to([P, NT, E]), ALU.add)\
                        .then_inc(x2b_ready, 1)
                root("y1")
                for s in seqs:
                    pool.wait_ge(normed, LNS["y1", s] + 1)
                    pool.tensor_tensor(y1b[s][:, :], y1[s][:, 0, :], erows[:, 0, BL2, :], ALU.add)\
                        .then_inc(y1b_ready, 1)
                root("h1")
                root("y2")
                for s in seqs:
                    pool.wait_ge(normed, LNS["y2", s] + 1)
                    ch.mark(pool.tensor_tensor(y2b[s][:, :, :], y2[s][:, :, :],
                                               erows[:, 1, BL2:BL2 + 1, :].broadcast_to([P, NT, E]), ALU.add))
                    ch.after()
                    pool.tensor_tensor(y2b[s][:, :, :], y2b[s][:, :, :], h[s][:, :, :], ALU.add)\
                        .then_inc(y2b_ready, 1)
                root("x5")
                root("z")
                for s in seqs:
                    pool.wait_ge(normed, LNS["x5", s] + 1)
                    pool.tensor_tensor(base[s][:, :, :], h2[s][:, :, :], x5[s][:, :, :], ALU.add)\
                        .then_inc(base_ready, 1)
                for s in seqs:
                    pool.wait_ge(normed, LNS["z", s] + 1)
                    ch.mark(pool.tensor_tensor(z[s][:, :, :], x3[s][:, :, :],
                                               grows[:, 0:1, :].broadcast_to([P, NT, E]), ALU.mult))
                    ch.after()
                    pool.tensor_tensor(z[s][:, :, :], z[s][:, :, :],
                                       grows[:, 1:2, :].broadcast_to([P, NT, E]), ALU.add).then_inc(z_ready, 1)
                ph.zero_round(pool, r)

        @block.tensor
        def _(pe):
            pe.wait_ge(weights_in, NLOADS)
            pe.wait_ge(consts_set, 1 + 2 * NB)
            pe.wait_ge(scaled, 3)
            pe.wait_ge(points, 5)
            pe.transpose(obank[0][:, 0:P], ind[:, 0, :], ident[:, :]).then_inc(points, 1)
            pe.wait_ge(points, 7)
            pe.matmul(obank[0][:, 0:P], win[:, 0, 0, :], indT[:, :], start=True, stop=True).then_inc(points, 1)
            pe.wait_ge(q1_in, 16 * 6)
            with pe.Fori(0, ROUNDS) as r:

                def turn(key, src, n=NT):
                    bank = tiles.claim(pe, key)
                    for t in range(n):
                        mm = pe.transpose(bank[:, t * P:t * P + P], src[:, t, :], ident[:, :])
                    tiles.filled(mm, key)

                def by_rows(key, lhs, rhs, n=NT):
                    bank = tiles.claim(pe, key)
                    for t in range(n):
                        mm = pe.matmul(bank[:, t * E:t * E + E], lhs[:, t * P:t * P + P], rhs, start=True, stop=True)
                    tiles.filled(mm, key)

                def by_features(key, w, rhs):
                    bank = tiles.claim(pe, key)
                    tiles.filled(pe.matmul(bank[:, 0:rhs.shape[1]], w, rhs, start=True, stop=True), key)

                def normalised(name, s):
                    pe.wait_ge(normed, LNS[name, s] + 1)

                for s in seqs:
                    normalised("final", s)
                    for k in range(KT):
                        bank = tiles.claim(pe, ("xT", s, k))
                        for t in range(NT):
                            mm = pe.transpose(bank[0:DP, t * P:t * P + P], x[s][:, t, k * DP:k * DP + DP], ident[:, :])
                        tiles.filled(mm, ("xT", s, k))
                for s in seqs:
                    for k in range(KT):
                        tiles.wait_copied(pe, ("xT", s, k))
                    bank = tiles.claim(pe, ("logits", s))
                    for t in range(NT):
                        for k in range(KT):
                            mm = pe.matmul(bank[:, t * E:t * E + E], xT[s][:, k, t * P:t * P + P], wc[:, k, :],
                                           start=(k == 0), stop=(k == KT - 1))
                    tiles.filled(mm, ("logits", s))
                for s in seqs:
                    normalised("x3", s)
                    turn(("u", s), x3[s])
                for s in seqs:
                    tiles.wait_copied(pe, ("u", s))
                    by_features(("k1", s), win[:, 0, 1, :], u1T[s][:, :])
                    by_features(("q2", s), win[:, 1, 0, :], u2T[s][:, :])
                    by_rows(("v1", s), u1T[s], win[:, 0, 2, :])
                pe.wait_ge(o_clear, 2)

                def turn_outputs(at, s):
                    pe.wait_ge((o1_free, o2_free)[at - 1], at * (s + 1))
                    for c in range(at):
                        key = (f"o{at}R", s, c)
                        bank = tiles.claim(pe, key)
                        for j in range(2 if at == 1 else NT):
                            src = hid1[s][:, j, :] if at == 1 else hid2[s][:, c, j * P:j * P + P]
                            mm = pe.transpose(bank[:, j * P:j * P + P], src, ident[:, :])
                        tiles.filled(mm, key)

                for at in (1, 2):
                    for s in seqs:
                        if at == 1:
                            pe.wait_ge(stacked, 16 * 12 * (s + 1))
                            tiles.wait_copied(pe, ("v1", s))
                        else:
                            pe.wait_ge(stacked2, 16 * 6 * (s + 1))
                            tiles.wait_copied(pe, ("v2", s))
                        for k in range(IH + LAG_V):
                            if k < IH:
                                key = (f"s{at}", s, k)
                                bank = tiles.claim(pe, key)
                                if at == 1:
                                    mm = pe.matmul(bank[:, :], stack(q1_st, k), stack(k1_st[s], k),
                                                   start=True, stop=True)
                                else:
                                    q = stack(q2_st[s], k)
                                    for t in range(NT):
                                        mm = pe.matmul(bank[:, t * P:t * P + P], q[:, t * P:t * P + P],
                                                       stack(k2_st[s], k), start=True, stop=True)
                                tiles.filled(mm, key)
                            if LAG_T <= k < IH + LAG_T:
                                kt = k - LAG_T
                                n = s * IH + kt
                                if at == 1:
                                    tiles.wait_copied(pe, ("s1", s, kt))
                                else:
                                    pe.wait_ge(expd2, n + 1)
                                key = (f"p{at}T", s, kt)
                                bank = tiles.claim(pe, key)
                                for t in range(NT):
                                    mm = pe.transpose(bank[:, t * P:t * P + P], prob[n % 4][:, t * P:t * P + P],
                                                      ident[:, :])
                                tiles.filled(mm, key)
                            if k >= LAG_V:
                                kv = k - LAG_V
                                n = s * IH + kv
                                tiles.wait_copied(pe, (f"p{at}T", s, kv))
                                if kv == 0:
                                    if at == 1 and s:
                                        pe.wait_ge(o1_free, s)
                                    if at == 2:
                                        pe.wait_ge(o1_free, NB)
                                        if s:
                                            pe.wait_ge(o2_free, 2 * s)
                                p, c = 32 * (kv % 4), kv // 4
                                if at == 1:
                                    for t in range(NT):
                                        mm = pe.matmul(obank[0][p:p + W17, c * P:c * P + P], v1[s][:, t, kv, :],
                                                       probT[n % 4][:, t * P:t * P + P],
                                                       start=(t == 0), stop=(t == NT - 1))
                                else:
                                    mm = pe.matmul(obank[c][p:p + W17, :], v2[s][:, kv, :], probT[n % 4][:, :],
                                                   start=True, stop=True)
                                if kv == IH - 1:
                                    mm.then_inc(o1_full if at == 1 else o2_full, 1)
                            if s and k == AT_ROWS:
                                turn_outputs(at, s - 1)
                        if s == NB - 1:
                            turn_outputs(at, s)
                    if at == 1:
                        for s in seqs:
                            tiles.wait_copied(pe, ("o1R", s, 0))
                            bank = tiles.claim(pe, ("o1T", s))
                            tiles.filled(pe.transpose(bank[:, 0:P], o1[s][:, :], ident[:, :]), ("o1T", s))
                        for s in seqs:
                            tiles.wait_copied(pe, ("o1T", s))
                            by_rows(("y1", s), t1[s], wout[:, 0, :], 1)
                        for s in seqs:
                            normalised("y1", s)
                            bank = tiles.claim(pe, ("t1", s))
                            tiles.filled(pe.transpose(bank[:, 0:P], h1[s][:, 0, :], ident[:, :]), ("t1", s))
                        for s in seqs:
                            tiles.wait_copied(pe, ("t1", s))
                            bank = tiles.claim(pe, ("up1", s))
                            for c in range(IF):
                                mm = pe.matmul(bank[:, c * P:c * P + P], l1[:, 0, c * P:c * P + P], t1[s][:, :],
                                               start=True, stop=True)
                            tiles.filled(mm, ("up1", s))
                        for s in seqs:
                            tiles.wait_copied(pe, ("up1", s))
                            bank = tiles.claim(pe, ("down1", s))
                            for c in range(IF):
                                mm = pe.matmul(bank[:, 0:E], hid1[s][:, c, :], l2[:, 0, c, :],
                                               start=(c == 0), stop=(c == IF - 1))
                            tiles.filled(mm, ("down1", s))
                        for s in seqs:
                            normalised("h1", s)
                            turn(("uk", s), y1[s], 1)
                        for s in seqs:
                            tiles.wait_copied(pe, ("uk", s))
                            by_features(("k2", s), win[:, 1, 1, :], ukT[s][:, :])
                            by_rows(("v2", s), ukT[s], win[:, 1, 2, :], 1)
                for s in seqs:
                    for c in range(2):
                        tiles.wait_copied(pe, ("o2R", s, c))
                    turn(("o2T", s), x3[s])
                for s in seqs:
                    tiles.wait_copied(pe, ("o2T", s))
                    by_rows(("y2", s), u1T[s], wout[:, 1, :])
                for s in seqs:
                    normalised("y2", s)
                    turn(("t2", s), x3[s])
                for s in seqs:
                    tiles.wait_copied(pe, ("t2", s))
                    for c in range(IF):
                        by_features(("up2", s, c), l1[:, 1, c * P:c * P + P], u2T[s][:, :])
                for s in seqs:
                    for c in range(IF):
                        tiles.wait_copied(pe, ("up2", s, c))
                    bank = tiles.claim(pe, ("down2", s))
                    for t in range(NT):
                        for c in range(IF):
                            mm = pe.matmul(bank[:, t * E:t * E + E], hid2[s][:, c, t * P:t * P + P], l2[:, 1, c, :],
                                           start=(c == 0), stop=(c == IF - 1))
                    tiles.filled(mm, ("down2", s))
                for s in seqs:
                    normalised("x5", s)
                    turn(("x5T", s), x5[s])
                for s in seqs:
                    normalised("z", s)
                    turn(("zT", s), x3[s])
                for s in seqs:
                    tiles.wait_copied(pe, ("x5T", s))
                    tiles.wait_copied(pe, ("zT", s))
                    bank = tiles.claim(pe, ("gate", s))
                    for t in range(NT):
                        c = t * (G + 1) * X
                        rows = slice(t * P, t * P + P)
                        pe.matmul(bank[:, c:c + G * X], hid2[s][:, 1, rows], wgate[:, G:], start=True, stop=True)
                        mm = pe.matmul(bank[:, c + G * X:c + G * X + G], hid2[s][:, 0, rows], wgate[:, 0:G],
                                       start=True, stop=True)
                    tiles.filled(mm, ("gate", s))
                for s in seqs:
                    pe.wait_ge(gates_set, s + 1)
                    bank = tiles.claim(pe, ("giT", s))
                    for t in range(NT):
                        mm = pe.transpose(bank[0:G * X, t * P:t * P + P],
                                          gates[s][:, t * (G + 1):t * (G + 1) + G, :]
                                          .rearrange("p g x -> p (g x)"), ident[:, :])
                    tiles.filled(mm, ("giT", s))
                ph.end_round(pe, r)

        @block.scalar
        def _(act):
            act.wait_ge(weights_in, NLOADS)
            act.wait_ge(scaled, 3)
            act.wait_ge(points, 6)
            act.activation(indT[:, :], obank[0][:, 0:P], ACT.Identity, scale=ecols[:, 0, LG1:LG1 + 1],
                           bias=ecols[:, 0, LB1:LB1 + 1]).then_inc(points, 1)
            act.wait_ge(points, 8)
            act.activation(q1[:, 0, :], obank[0][:, 0:P], ACT.Identity, bias=ecols[:, 0, BQ:BQ + 1])\
                .then_inc(points, 1)
            with act.Fori(0, ROUNDS) as r:
                def affine(dst, src, g, b):
                    return act.activation(dst, src, ACT.Identity, scale=g, bias=b)

                for s in seqs:
                    bank = tiles.take(act, ("xT", s, 0))
                    tiles.copied(affine(xT[s][:, 0, :], bank[0:DP, :], fcols[:, 0, 0:1], fcols[:, 1, 0:1]),
                                 ("xT", s, 0))
                for s in seqs:
                    bank = tiles.take(act, ("u", s))
                    affine(u1T[s][:, :], bank[:, :], ecols[:, 0, LG1:LG1 + 1], ecols[:, 0, LB1:LB1 + 1])
                    tiles.copied(affine(u2T[s][:, :], bank[:, :], ecols[:, 1, LG1:LG1 + 1],
                                        ecols[:, 1, LB1:LB1 + 1]), ("u", s))
                for s in seqs:
                    for key, blk, bias, w in (("k1", 0, BK, 0), ("q2", 1, BQ, 2)):
                        bank = tiles.take(act, (key, s))
                        act.activation(kq[s][:, w, :], bank[:, :], ACT.Identity, bias=ecols[:, blk, bias:bias + 1])\
                            .then_inc(split_hi, 1)
                for at in (1, 2):
                    for s in seqs:
                        for k in range(IH + LAG_T):
                            if k < IH:
                                n = s * IH + k
                                if n >= 4:
                                    tiles.take(act, (f"p{at}T", (n - 4) // IH, (n - 4) % IH))
                                if at == 1:
                                    bank = tiles.take(act, ("s1", s, k))
                                    act.wait_ge(rowmax, n + 1)
                                    tiles.copied(act.activation(prob[n % 4][:, :], bank[:, :], ACT.Exp,
                                                                bias=rmax[:, n, 0:1]), ("s1", s, k))
                                else:
                                    tiles.wait_copied(act, ("s2", s, k))
                                    act.activation(prob[n % 4][:, :], prob[n % 4][:, :], ACT.Exp).then_inc(expd2, 1)
                            if k >= LAG_T and (k - LAG_T) % 2:
                                n = s * IH + k - LAG_T
                                key = (f"p{at}T", s, k - LAG_T)
                                bank = tiles.take(act, key)
                                tiles.copied(act.activation(probT[n % 4][:, :], bank[:, :], ACT.Copy), key)
                        if at == 1:
                            act.wait_ge(o1_full, s + 1)
                            act.activation(hid1[s][:, 0:2, :].rearrange("p c d -> p (c d)"), obank[0][:, 0:2 * P],
                                           ACT.Copy).then_inc(o1_free, 1)
                        else:
                            act.wait_ge(o2_full, s + 1)
                            act.activation(hid2[s][:, 0, :], obank[0][:, :], ACT.Copy).then_inc(o2_free, 1)
                    if at == 1:
                        for s in seqs:
                            bank = tiles.take(act, ("o1T", s))
                            tiles.copied(act.activation(t1[s][:, :], bank[:, 0:P], ACT.Copy), ("o1T", s))
                        for s in seqs:
                            bank = tiles.take(act, ("t1", s))
                            tiles.copied(affine(t1[s][:, :], bank[:, 0:P], ecols[:, 0, LG2:LG2 + 1],
                                                ecols[:, 0, LB2:LB2 + 1]), ("t1", s))
                        for s in seqs:
                            bank = tiles.take(act, ("up1", s))
                            for c in range(IF):
                                ins = act.activation(hid1[s][:, c, :], bank[:, c * P:c * P + P], ACT.Gelu,
                                                     bias=l1b[:, 0, c:c + 1])
                            tiles.copied(ins, ("up1", s))
                        for s in seqs:
                            bank = tiles.take(act, ("uk", s))
                            tiles.copied(affine(ukT[s][:, :], bank[:, 0:P], ecols[:, 1, LG1:LG1 + 1],
                                                ecols[:, 1, LB1:LB1 + 1]), ("uk", s))
                        for s in seqs:
                            bank = tiles.take(act, ("k2", s))
                            act.activation(k2[s][:, 0, :], bank[:, 0:P], ACT.Identity, bias=ecols[:, 1, BK:BK + 1])\
                                .then_inc(split_hi, 1)
                for s in seqs:
                    bank = tiles.take(act, ("o2T", s))
                    tiles.copied(act.activation(u1T[s][:, :], bank[:, :], ACT.Copy), ("o2T", s))
                for s in seqs:
                    bank = tiles.take(act, ("t2", s))
                    tiles.copied(affine(u2T[s][:, :], bank[:, :], ecols[:, 1, LG2:LG2 + 1],
                                        ecols[:, 1, LB2:LB2 + 1]), ("t2", s))
                for s in seqs:
                    for c in range(IF):
                        bank = tiles.take(act, ("up2", s, c))
                        tiles.copied(act.activation(hid2[s][:, c, :], bank[:, :], ACT.Gelu, bias=l1b[:, 1, c:c + 1]),
                                     ("up2", s, c))
                for s in seqs:
                    bank = tiles.take(act, ("x5T", s))
                    tiles.copied(act.activation(hid2[s][:, 0, :], bank[:, :], ACT.Copy), ("x5T", s))
                for s in seqs:
                    bank = tiles.take(act, ("zT", s))
                    tiles.copied(affine(hid2[s][:, 1, :], bank[:, :], gcols[:, 0:1], gcols[:, 1:2]), ("zT", s))
                for s in seqs:
                    act.wait_ge(gexp_in, s + 1)
                    act.activation(gs[:, 3, :], gs[:, 2, :], ACT.Exp).then_inc(gexp_out, 1)
                for s in seqs:
                    bank = tiles.take(act, ("giT", s))
                    tiles.copied(act.activation(giT[s][:, :], bank[0:G * X, :], ACT.Copy), ("giT", s))
                ph.end_round(act, r)

        @block.vector
        def _(dve):
            dve.wait_ge(weights_in, NLOADS)
            dve.bn_stats(st6[:, 0, 0, :], ind[:, 0, :]).then_inc(points, 1)
            dve.tensor_scalar(win[:, :, 0, :], win[:, :, 0, :], DH ** -0.5, None, ALU.mult).then_inc(scaled, 1)
            dve.tensor_scalar(ecols[:, :, BQ], ecols[:, :, BQ], DH ** -0.5, None, ALU.mult).then_inc(scaled, 1)
            dve.tensor_tensor(indb[:, :], ind[:, 0, :], erows[:, 0, BOUT, :], ALU.add).then_inc(scaled, 1)
            dve.wait_ge(points, 1)
            dve.bn_aggr(mv[:, 0, 0, :], st6[:, 0, 0, :]).then_inc(points, 1)
            dve.wait_ge(scaled, 3)
            dve.wait_ge(points, 4)
            dve.tensor_scalar(ind[:, 0, :], ind[:, 0, :], mv[:, 0, 0, 0:1], rstd[:, 0, 0:1],
                              ALU.subtract, ALU.mult).then_inc(points, 1)
            dve.wait_ge(points, 9)
            dve.scalar_tensor_tensor(q1[:, 1, :], obank[0][:, 0:P], ecols[:, 0, BQ:BQ + 1],
                                     q1[:, 0, :].bitcast(F32), ALU.add, ALU.subtract).then_inc(points, 1)
            dve.wait_ge(points, 10)
            for bank in obank:
                dve.memset(bank[:, :], 0.0).then_inc(o_clear, 1)
            with dve.Fori(0, ROUNDS) as r:
                ch = Chain(dve, dve_chain)

                def wide(t):
                    return t[:, :, :].rearrange("p t d -> p (t d)")

                def layernorm(name, src, dst):
                    n = ROWS.get(name, NT)
                    for s in seqs:
                        for t in range(n):
                            ins = dve.bn_stats(st6[:, s, t, :], src[s][:, t, :])
                        ch.mark(ins)
                        ch.after()
                        for t in range(n):
                            ins = dve.bn_aggr(mv[:, s, t, :], st6[:, s, t, :])
                        ins.then_inc(moments, 1)
                    for s in seqs:
                        dve.wait_ge(moments, LNS[name, s] + 1)
                        dve.wait_ge(roots, LNS[name, s] + 1)
                        for t in range(n):
                            ins = dve.tensor_scalar(dst[s][:, t, :], src[s][:, t, :], mv[:, s, t, 0:1],
                                                    rstd[:, s, t:t + 1], ALU.subtract, ALU.mult)
                        ins.then_inc(normed, 1)
                    for s in seqs:
                        dve.wait_ge(normed, LNS[name, s] + 1)

                def low(key, dst, high, bias, n, width=S):
                    dve.wait_ge(split_hi, n)
                    bank = tiles.take(dve, key)
                    tiles.copied(dve.scalar_tensor_tensor(dst, bank[:, 0:width], bias, high.bitcast(F32),
                                                          ALU.add, ALU.subtract), key)

                def values(key, dst, row, n):
                    bank = tiles.take(dve, key)
                    tiles.copied(dve.tensor_tensor(
                        dst, bank[:, 0:n * E].rearrange("p (t h d) -> p t h d", t=n, d=DH),
                        row.broadcast_to([P, n, E]).rearrange("p t (h d) -> p t h d", d=DH), ALU.add), key)

                ph.wait_lasting(dve, x_in, 16 * NB * (r + 1))
                layernorm("final", x, x)
                for s in seqs:
                    bank = tiles.take(dve, ("xT", s, 1))
                    tiles.copied(dve.tensor_scalar(xT[s][:, 1, :], bank[0:DP, :], fcols[:, 0, 1:2], fcols[:, 1, 1:2],
                                                   ALU.mult, ALU.add), ("xT", s, 1))
                for s in seqs:
                    bank = tiles.take(dve, ("logits", s))
                    tiles.copied(dve.tensor_tensor(h[s][:, :, :], bank[:, :].rearrange("p (t d) -> p t d", d=E),
                                                   bc[:, None, :].broadcast_to([P, NT, E]), ALU.add), ("logits", s))
                for s in seqs:
                    tiles.wait_copied(dve, ("logits", s))
                layernorm("x2", h, x2)
                layernorm("x3", x2, x3)
                for s in seqs:
                    low(("k1", s), kq[s][:, 1, :], kq[s][:, 0, :], ecols[:, 0, BK:BK + 1], 2 * s + 1)
                    low(("q2", s), kq[s][:, 3, :], kq[s][:, 2, :], ecols[:, 1, BQ:BQ + 1], 2 * s + 2)
                    values(("v1", s), v1[s][:, :, :, 0:DH], erows[:, 0, BV:BV + 1, :], NT)

                def rows_of(at, s):
                    for c in range(at):
                        bank = tiles.take(dve, (f"o{at}R", s, c))
                        if at == 1:
                            o = bank[:, 0:IH * 32].rearrange("p (h w) -> p h w", w=32)
                            dst, rec, shape = o1[s][:, :].rearrange("p (h d) -> p h d", d=DH), orec[:, 0, :], [P, IH, DH]
                            total = o[:, :, DH]
                        else:
                            o = bank[:, :].rearrange("p (t h w) -> p t h w", t=NT, w=32)
                            dst = x3[s][:, :, c * 4 * DH:(c + 1) * 4 * DH].rearrange("p t (h d) -> p t h d", d=DH)
                            rec, shape = orec[:, :, :].rearrange("p a h -> p (a h)"), [P, NT, 4, DH]
                            rec = rec.rearrange("p (t h) -> p t h", t=NT)
                            total = o[:, :, :, DH]
                            if c:
                                tiles.wait_copied(dve, ("o2R", s, c - 1))
                        ch.mark(dve.reciprocal(rec, total))
                        ch.after()
                        o = o[:, :, 0:DH] if at == 1 else o[:, :, :, 0:DH]
                        rec = rec[:, :, None] if at == 1 else rec[:, :, :, None]
                        tiles.copied(dve.tensor_tensor(dst, o, rec.broadcast_to(shape), ALU.mult),
                                     (f"o{at}R", s, c))

                for at in (1, 2):
                    for s in seqs:
                        for k in range(IH + LAG_T):
                            if k < IH:
                                n = s * IH + k
                                key = (f"s{at}", s, k)
                                bank = tiles.take(dve, key)
                                if at == 1:
                                    dve.tensor_reduce(rmax[:, n, 0:1], bank[:, :], AX.X, ALU.max, negate=True)\
                                        .then_inc(rowmax, 1)
                                else:
                                    if n >= 4:
                                        tiles.take(dve, ("p2T", (n - 4) // IH, (n - 4) % IH))
                                    view = bank[:, :].rearrange("p (t d) -> p t d", d=P)
                                    ch.mark(dve.tensor_reduce(rmax[:, n, :], view, AX.X, ALU.max))
                                    ch.after()
                                    tiles.copied(dve.tensor_tensor(
                                        prob[n % 4][:, :].rearrange("p (t d) -> p t d", d=P), view,
                                        rmax[:, n, :, None].broadcast_to([P, NT, P]), ALU.subtract), key)
                            if k >= LAG_T and (k - LAG_T) % 2 == 0:
                                n = s * IH + k - LAG_T
                                key = (f"p{at}T", s, k - LAG_T)
                                bank = tiles.take(dve, key)
                                tiles.copied(dve.tensor_copy(probT[n % 4][:, :], bank[:, :]), key)
                            if s and k == AT_ROWS + 1:
                                rows_of(at, s - 1)
                        if at == 2:
                            dve.wait_ge(o2_full, s + 1)
                            dve.tensor_copy(hid2[s][:, 1, :], obank[1][:, :]).then_inc(o2_free, 1)
                        if s == NB - 1:
                            rows_of(at, s)
                    if at == 1:
                        for s in seqs:
                            bank = tiles.take(dve, ("y1", s))
                            tiles.copied(dve.tensor_tensor(y1[s][:, 0, :], bank[:, 0:E], indb[:, :], ALU.add),
                                         ("y1", s))
                        for s in seqs:
                            tiles.wait_copied(dve, ("y1", s))
                        layernorm("y1", y1, h1)
                        for s in seqs:
                            bank = tiles.take(dve, ("down1", s))
                            dve.wait_ge(y1b_ready, s + 1)
                            tiles.copied(dve.tensor_tensor(h1[s][:, 0, :], bank[:, 0:E], y1b[s][:, :], ALU.add),
                                         ("down1", s))
                        for s in seqs:
                            tiles.wait_copied(dve, ("down1", s))
                        layernorm("h1", h1, y1)
                        for s in seqs:
                            low(("k2", s), k2[s][:, 1, :], k2[s][:, 0, :], ecols[:, 1, BK:BK + 1], 2 * NB + s + 1, P)
                            values(("v2", s), v2[s][:, None, :, 0:DH], erows[:, 1, BV:BV + 1, :], 1)
                for s in seqs:
                    bank = tiles.take(dve, ("y2", s))
                    dve.wait_ge(x2b_ready, s + 1)
                    tiles.copied(dve.tensor_tensor(wide(y2[s]), bank[:, :], wide(x2b[s]), ALU.add), ("y2", s))
                for s in seqs:
                    tiles.wait_copied(dve, ("y2", s))
                layernorm("y2", y2, x3)
                for s in seqs:
                    bank = tiles.take(dve, ("down2", s))
                    dve.wait_ge(y2b_ready, s + 1)
                    tiles.copied(dve.tensor_tensor(wide(h2[s]), bank[:, :], wide(y2b[s]), ALU.add), ("down2", s))
                for s in seqs:
                    tiles.wait_copied(dve, ("down2", s))
                layernorm("x5", h2, x5)
                layernorm("z", x5, x3)
                N5 = NT * (G + 1)

                def row(j):
                    return gs[:, j, :]

                def spread(j):
                    return gs[:, j, :, None].broadcast_to([P, N5, X])

                for s in seqs:
                    if s:
                        dve.wait_ge(gates_set, s)
                    bank = tiles.take(dve, ("gate", s))
                    ch.mark(dve.memset(gates[s][:, G:N5:G + 1, G:X], -3e30))
                    ch.after()
                    b4 = bank[:, 0:N5 * X].rearrange("p (t c) -> p t c", t=NT)
                    g4 = gates[s][:, :, :].rearrange("p (t g) x -> p t (g x)", t=NT)
                    tiles.copied(dve.tensor_copy(g4[:, :, 0:G * X + G], b4[:, :, 0:G * X + G]), ("gate", s))
                    tiles.wait_copied(dve, ("gate", s))
                    lg = gates[s][:, :, :]

                    def step(ins):
                        ch.mark(ins)
                        ch.after()

                    def first(src, m, hot):
                        step(dve.tensor_reduce(row(m), src, AX.X, ALU.max))
                        step(dve.tensor_tensor(hot, src, spread(m), ALU.is_equal))
                        step(dve.tensor_tensor(hot, hot, rank[:, None, :].broadcast_to([P, N5, X]), ALU.mult))
                        step(dve.tensor_reduce(row(5), hot, AX.X, ALU.max))
                        step(dve.tensor_tensor(hot, hot, spread(5), ALU.is_equal))

                    first(lg, 0, ga[:, :, :])
                    step(dve.scalar_tensor_tensor(gc[:, :, :], ga[:, :, :], -1e30, lg, ALU.mult, ALU.add))
                    first(gc[:, :, :], 1, gb[:, :, :])
                    dve.tensor_tensor(row(2), row(1), row(0), ALU.subtract).then_inc(gexp_in, 1)
                    dve.wait_ge(gexp_out, s + 1)
                    step(dve.tensor_scalar(row(4), row(3), 1.0, None, ALU.add))
                    step(dve.reciprocal(row(4), row(4)))
                    step(dve.tensor_tensor(row(3), row(3), row(4), ALU.mult))
                    step(dve.tensor_tensor(ga[:, :, :], ga[:, :, :], spread(4), ALU.mult))
                    step(dve.tensor_tensor(gb[:, :, :], gb[:, :, :], spread(3), ALU.mult))
                    dve.tensor_tensor(lg, ga[:, :, :], gb[:, :, :], ALU.add).then_inc(gates_set, 1)
                ph.end_round(dve, r)


def experts(nc, a, outer):
    with ExitStack() as ctx:
        ph = Phase(nc, "experts", ctx, outer)
        N = B * S
        NG = 4
        ident, ident_in = ph.sb("ident", [P, P]), ph.lasting("ident_in")
        NCH, NTT, TC = N // 512, N // P, 512 // P
        zT, accT = ph.sb("zT", [E, N]), ph.sb("accT", [E, N])
        zhi, zlo = ph.sb("zhi", [E, N], F32R), ph.sb("zlo", [E, N], F32R)
        out = ph.sb("out", [P, NTT, E])
        gates, gw = ph.sb("gates", [P, NTT, G + 1, X]), ph.sb("gw", [P, NTT, 1])
        giT, b2g = ph.sb("giT", [G * X, N]), ph.sb("b2g", [G * X, E])
        w1, w2 = ph.sb("w1", [E, 2, XH]), ph.sb("w2", [P, 2, XC, E])
        w1s, w2s = ph.sb("w1s", [E, 2, 2, XH], F32R), ph.sb("w2s", [P, 2, 2, XC, E], F32R)
        b1c, glrows = ph.sb("b1c", [P, X, XC]), ph.sb("glrows", [P, 2, E])
        relu = [ph.sb(f"relu{j}", [P, 512]) for j in range(XC)]
        hhi = [ph.sb(f"hhi{j}", [P, XC, 512], F32R) for j in range(2)]
        hlo = [ph.sb(f"hlo{j}", [P, XC, 512], F32R) for j in range(2)]
        gate = [ph.sb(f"gate{j}", [P, 512]) for j in range(NG)]
        gated = [ph.sb(f"gated{j}", [P, 512]) for j in range(2)]
        half = ph.sb("half", [P, TC])
        st6, mv, rstd = ph.sb("st6", [P, 2, TC, 6]), ph.sb("mv", [P, 2, TC, 2]), ph.sb("rstd", [P, 2, TC])
        y = [ph.sb(f"y{j}", [P, TC, E]) for j in range(2)]
        banks = [ph.psum(f"bank{b}") for b in range(8)]

        CH = X * NCH
        LAST = CH - NCH
        STEPS = CH + 5

        def ending(q, lag):
            c = q - lag - LAST
            return c if 0 <= c < NCH else None

        order = [("init", c) for c in range(NCH)]
        for q in range(STEPS):
            if q < CH:
                order += [("up", q, k) for k in range(XC)]
            if 1 <= q <= CH:
                order.append(("down", q - 1))
            if ending(q, 2) is not None:
                order.append(("turned", ending(q, 2)))
        tiles = Tiles(ph, banks, order)
        loaded, half_set = ph.lasting("loaded"), ph.lasting("half_set")
        z_in, z_hi, z_lo = ph.lasting("z_in"), ph.lasting("z_hi"), ph.lasting("z_lo")
        stored = ph.lasting("stored")
        group_in, gate_set = ph.sem("group_in"), ph.sem("gate_set")
        w_in, w_hi, w_lo = [ph.sem("w_in0"), ph.sem("w_in1")], ph.sem("w_hi"), ph.sem("w_lo")
        gate_in = [ph.sem(f"gate_in{j}") for j in range(NG)]
        h_lo, summed = ph.sem("h_lo"), ph.sem("summed")
        moments, roots, shifted = (ph.sem(n) for n in ("moments", "roots", "shifted"))
        added, dve_chain, pool_chain = ph.sem("added"), ph.sem("dve_chain"), ph.sem("pool_chain")
        block = ctx.enter_context(nc.Block())
        NLOADS = 16 * 3 * B

        @block.sync
        def _(sp):
            for b in range(B):
                sp.dma_start(zT[:, b * 512:b * 512 + 512], a["zT"][b]).then_inc(z_in, 16)
            for b in range(B):
                tt = slice(TC * b, TC * b + TC)
                sp.dma_start(out[:, tt, :], a["base"][b]).then_inc(loaded, 16)
                sp.dma_start(gates[:, tt, :, :], a["gates"][b].rearrange("p (t g) x -> p t g x", t=TC))\
                    .then_inc(loaded, 16)
                sp.dma_start(giT[:, b * 512:b * 512 + 512], a["giT"][b]).then_inc(loaded, 16)
            with sp.Fori(0, G) as g:
                grp = bass.ds(g, 1)
                sp.dma_start(b1c[:, :, :], a["eb1"][grp].rearrange("o p x k -> (o p) x k")).then_inc(group_in, 16)
                sp.dma_start(b2g[:, :], a["eb2"][grp].rearrange("o x d -> (o x) d")).then_inc(group_in, 16)
                sp.dma_start(glrows[:, :, :], a["glrows"][grp].rearrange("o p r d -> (o p) r d"))\
                    .then_inc(group_in, 16)

                def load_weights(e):
                    if e >= 2:
                        sp.wait_ge(w_lo, 2 * (e - 1))
                    sp.dma_start(w1[:, e % 2, :], a["ew1"][grp, e].rearrange("o p n -> (o p) n"))\
                        .then_inc(w_in[e % 2], 16)
                    sp.dma_start(w2[:, e % 2, :, :], a["ew2"][grp, e].rearrange("o p k n -> (o p) k n"))\
                        .then_inc(w_in[e % 2], 16)

                load_weights(0)
                for q in range(CH):
                    e, c = divmod(q, NCH)
                    if c == 0 and e + 1 < X:
                        load_weights(e + 1)
                    if q >= NG:
                        tiles.wait_copied(sp, ("down", q - NG))
                    sp.dma_start(gate[q % NG][:, :], a["giT"][c, bass.ds(g * X + e, 1), :].broadcast_to([P, 512]))\
                        .then_inc(gate_in[q % NG], 16)
                ph.end_round(sp, g)
            for b in range(B):
                sp.dma_start(a["out"][b].rearrange("(t p) d -> p t d", p=P), out[:, TC * b:TC * b + TC, :])\
                    .then_inc(stored, 16)
            sp.wait_ge(stored, 16 * B)

        def weights_arrived(eng, e):
            eng.wait_ge(w_in[e % 2], 32 * (e // 2 + 1))

        @block.gpsimd
        def _(pool):
            pool.memset(half[:, :], -0.5).then_inc(half_set, 1)
            pool.wait_ge(half_set, 1)
            with pool.Fori(0, G) as g:
                ch = Chain(pool, pool_chain)

                def split_weights(e):
                    weights_arrived(pool, e)
                    if e >= 2:
                        tiles.take(pool, ("down", (e - 1) * NCH - 1))
                    pool.tensor_copy(w1s[:, e % 2, 0, :], w1[:, e % 2, :]).then_inc(w_hi, 1)
                    pool.tensor_copy(w2s[:, e % 2, 0, :, :], w2[:, e % 2, :, :]).then_inc(w_hi, 1)

                pool.wait_ge(group_in, 48)
                split_weights(0)
                for q in range(1, STEPS):
                    if q < CH and q % NCH == 2 and q // NCH + 1 < X:
                        split_weights(q // NCH + 1)
                    if q <= CH:
                        c = (q - 1) % NCH
                        tiles.wait_copied(pool, ("down", q - 1))
                        if q > NCH:
                            pool.wait_ge(summed, q - NCH)
                        else:
                            tiles.wait_copied(pool, ("init", c))
                        part = accT[:, c * 512:c * 512 + 512]
                        pool.tensor_tensor(part, part, gated[(q - 1) % 2][:, :], ALU.add).then_inc(summed, 1)
                    if (c := ending(q, 2)) is not None:
                        pool.wait_ge(moments, c + 1)
                        ch.mark(pool.tensor_scalar(rstd[:, c % 2, :], mv[:, c % 2, :, 1], EPS, None, ALU.add))
                        ch.after()
                        pool.tensor_tensor(rstd[:, c % 2, :], rstd[:, c % 2, :], half[:, :], ALU.pow)\
                            .then_inc(roots, 1)
                    if (c := ending(q, 3)) is not None:
                        tiles.wait_copied(pool, ("turned", c))
                        yc = y[c % 2][:, :, :]
                        ch.mark(pool.tensor_tensor(yc, yc, glrows[:, 0:1, :].broadcast_to([P, TC, E]), ALU.mult))
                        ch.after()
                        pool.tensor_tensor(yc, yc, glrows[:, 1:2, :].broadcast_to([P, TC, E]), ALU.add)\
                            .then_inc(shifted, 1)
                ph.zero_round(pool, g)

        @block.tensor
        def _(pe):
            pe.wait_ge(ident_in, 16)
            pe.wait_ge(loaded, NLOADS)
            pe.wait_ge(z_lo, B)
            with pe.Fori(0, G) as g:
                pe.wait_ge(group_in, 48)
                for c in range(NCH):
                    bank = tiles.claim(pe, ("init", c))
                    tiles.filled(pe.matmul(bank[:, :], b2g[:, :], giT[:, c * 512:c * 512 + 512],
                                           start=True, stop=True), ("init", c))
                for q in range(STEPS):
                    if q < CH:
                        e, c = divmod(q, NCH)
                        if c == 0:
                            pe.wait_ge(w_lo, 2 * (e + 1))
                        zc = slice(c * 512, c * 512 + 512)
                        for k in range(XC):
                            bank = tiles.claim(pe, ("up", q, k))
                            hi, lo = (w1s[:, e % 2, part, k * P:k * P + P] for part in range(2))
                            pe.matmul(bank[:, :], hi, zhi[:, zc], start=True, stop=False)
                            pe.matmul(bank[:, :], hi, zlo[:, zc], start=False, stop=False)
                            mm = pe.matmul(bank[:, :], lo, zhi[:, zc], start=False, stop=True)
                            tiles.filled(mm, ("up", q, k))
                    if 1 <= q <= CH:
                        q1 = q - 1
                        bank = tiles.claim(pe, ("down", q1))
                        for k in range(XC):
                            pe.wait_ge(h_lo, XC * q1 + k + 1)
                            hi, lo = (w2s[:, (q1 // NCH) % 2, part, k, :] for part in range(2))
                            pe.matmul(bank[:, :], hi, hhi[q1 % 2][:, k, :], start=(k == 0), stop=False)
                            pe.matmul(bank[:, :], hi, hlo[q1 % 2][:, k, :], start=False, stop=False)
                            mm = pe.matmul(bank[:, :], lo, hhi[q1 % 2][:, k, :], start=False, stop=(k == XC - 1))
                        tiles.filled(mm, ("down", q1))
                    if (c := ending(q, 2)) is not None:
                        bank = tiles.claim(pe, ("turned", c))
                        pe.wait_ge(summed, LAST + c + 1)
                        for t in range(TC):
                            col = (c * TC + t) * P
                            mm = pe.transpose(bank[:, t * P:t * P + P], accT[:, col:col + P], ident[:, :])
                        tiles.filled(mm, ("turned", c))
                ph.end_round(pe, g)

        @block.scalar
        def _(act):
            act.dma_start(ident[:, :], a["ident"]).then_inc(ident_in, 16)
            act.wait_ge(z_in, 16 * B)
            for b in range(B):
                act.activation(zhi[:, b * 512:b * 512 + 512], zT[:, b * 512:b * 512 + 512], ACT.Copy)\
                    .then_inc(z_hi, 1)
            with act.Fori(0, G) as g:
                act.wait_ge(group_in, 48)
                for q in range(CH):
                    for k in range(XC):
                        bank = tiles.take(act, ("up", q, k))
                        if q:
                            act.wait_ge(h_lo, XC * (q - 1) + k + 1)
                        if q >= 2:
                            tiles.take(act, ("down", q - 2))
                        bias = b1c[:, q // NCH, k:k + 1]
                        act.activation(relu[k][:, :], bank[:, :], ACT.Relu, bias=bias)
                        tiles.copied(act.activation(hhi[q % 2][:, k, :], bank[:, :], ACT.Relu, bias=bias),
                                     ("up", q, k))
                ph.end_round(act, g)

        @block.vector
        def _(dve):
            for b in range(B):
                dve.wait_ge(z_hi, b + 1)
                part = slice(b * 512, b * 512 + 512)
                dve.tensor_tensor(zlo[:, part], zT[:, part], zhi[:, part].bitcast(F32), ALU.subtract)\
                    .then_inc(z_lo, 1)
            dve.wait_ge(loaded, NLOADS)
            with dve.Fori(0, G) as g:
                ch = Chain(dve, dve_chain)

                def split_weights(e):
                    dve.wait_ge(w_hi, 2 * e + 1)
                    dve.tensor_tensor(w1s[:, e % 2, 1, :], w1[:, e % 2, :], w1s[:, e % 2, 0, :].bitcast(F32),
                                      ALU.subtract).then_inc(w_lo, 1)
                    dve.wait_ge(w_hi, 2 * e + 2)
                    dve.tensor_tensor(w2s[:, e % 2, 1, :, :], w2[:, e % 2, :, :],
                                      w2s[:, e % 2, 0, :, :].bitcast(F32), ALU.subtract).then_inc(w_lo, 1)

                split_weights(0)
                dve.tensor_copy(gw[:, :, :], gates[:, :, G, bass.ds(g, 1)]).then_inc(gate_set, 1)
                for c in range(NCH):
                    bank = tiles.take(dve, ("init", c))
                    part = slice(c * 512, c * 512 + 512)
                    tiles.copied(dve.tensor_tensor(accT[:, part], bank[:, :], zT[:, part], ALU.add), ("init", c))
                dve.wait_ge(gate_set, 1)
                for q in range(STEPS):
                    if q < CH:
                        if q % NCH == 2 and q // NCH + 1 < X:
                            split_weights(q // NCH + 1)
                        for k in range(XC):
                            tiles.wait_copied(dve, ("up", q, k))
                            dve.tensor_tensor(hlo[q % 2][:, k, :], relu[k][:, :], hhi[q % 2][:, k, :].bitcast(F32),
                                              ALU.subtract).then_inc(h_lo, 1)
                    if 1 <= q <= CH:
                        q1 = q - 1
                        bank = tiles.take(dve, ("down", q1))
                        dve.wait_ge(gate_in[q1 % NG], 16 * (q1 // NG + 1))
                        if q1 >= 2:
                            dve.wait_ge(summed, q1 - 1)
                        tiles.copied(dve.tensor_tensor(gated[q1 % 2][:, :], bank[:, :], gate[q1 % NG][:, :],
                                                       ALU.mult), ("down", q1))
                    if (c := ending(q, 3)) is not None:
                        bank = banks[tiles.number["turned", c] % 8]
                        dve.wait_ge(roots, c + 1)
                        if c >= 2:
                            dve.wait_ge(added, c - 1)
                        for t in range(TC):
                            ins = dve.tensor_scalar(y[c % 2][:, t, :], bank[:, t * P:t * P + P], mv[:, c % 2, t, 0:1],
                                                    rstd[:, c % 2, t:t + 1], ALU.subtract, ALU.mult)
                        tiles.copied(ins, ("turned", c))
                    if (c := ending(q, 2)) is not None:
                        bank = tiles.take(dve, ("turned", c))
                        for t in range(TC):
                            ins = dve.bn_stats(st6[:, c % 2, t, :], bank[:, t * P:t * P + P])
                        ch.mark(ins)
                        ch.after()
                        for t in range(TC):
                            ins = dve.bn_aggr(mv[:, c % 2, t, :], st6[:, c % 2, t, :])
                        ins.then_inc(moments, 1)
                    if (c := ending(q, 4)) is not None:
                        dve.wait_ge(shifted, c + 1)
                        for t in range(TC):
                            row = out[:, c * TC + t, :]
                            ins = dve.scalar_tensor_tensor(row, y[c % 2][:, t, :], gw[:, c * TC + t, :],
                                                           row, ALU.mult, ALU.add)
                        ins.then_inc(added, 1)
                ph.end_round(dve, g)


def pack_tower(inp):
    def arr(n):
        return np.asarray(inp["L0_tok_" + n])

    def by_in(w, p):
        n_layers, out, inn = w.shape
        return w.transpose(0, 2, 1).reshape(n_layers, inn // p, p, out).transpose(0, 2, 1, 3)

    def by_feature(v, p):
        return v.reshape(v.shape[0], -1, p).transpose(0, 2, 1)

    def on_all(v):
        return np.broadcast_to(v[:, None, :], (v.shape[0], P, v.shape[1]))

    return {
        "wqk": np.stack([by_in(arr("Wq"), DP), by_in(arr("Wk"), DP)], 2),
        "wvo": np.stack([by_in(arr("Wv"), DP), by_in(arr("Wo"), DP)], 2),
        "w1": by_in(arr("W1"), DP),
        "w2": by_in(arr("W2"), P),
        "rows": np.stack([on_all(arr(n)) for n in ("bv", "bo", "g1", "beta1", "b2")], 2),
        "rows2": np.stack([on_all(arr(n)) for n in ("g2", "beta2")], 2),
        "cols": np.stack([by_feature(arr(n), DP) for n in ("bq", "bk", "g1", "beta1")], 2),
        "b1c": by_feature(arr("b1"), P),
        "emb": arr("emb"),
        "ids": np.broadcast_to(np.asarray(inp["x"]).reshape(1, B * S), (P, B * S)),
        "pad": np.asarray(inp["mask_BS_b0_1"]),
    }


def pack_induce(inp):
    def arr(n):
        return np.asarray(inp["L0_" + n])

    def both(f, axis=1):
        return np.stack([f("attn_a1_"), f("attn_a2_")], axis)

    def on_all(v):
        return np.broadcast_to(v[None], (P,) + v.shape)

    def cols(*names):
        return np.stack([arr(n) for n in names], 1)

    ln = ("ln1_g", "ln1_b", "ln2_g", "ln2_b")
    return {
        "wc": arr("tok_Wc").T.reshape(KT, DP, E).transpose(1, 0, 2),
        "fcols": np.stack([arr("tok_gf").reshape(KT, DP).T, arr("tok_betaf").reshape(KT, DP).T], 1),
        "bc": on_all(arr("tok_bc")),
        "win": both(lambda p: arr(p + "in_w").T.reshape(E, 3, E)),
        "wout": both(lambda p: arr(p + "out_w").T),
        "l1": both(lambda p: arr(p + "l1_w").T),
        "l2": both(lambda p: arr(p + "l2_w").T.reshape(IF, P, E).transpose(1, 0, 2)),
        "ecols": both(lambda p: np.concatenate([arr(p + "in_b").reshape(3, E)[0:2].T, cols(*(p + n for n in ln))], 1)),
        "l1b": both(lambda p: arr(p + "l1_b").reshape(IF, P).T),
        "erows": both(lambda p: on_all(np.stack([arr(p + "in_b")[2 * E:], arr(p + "out_b"), arr(p + "l2_b")]))),
        "gcols": cols("ffn_ln_g", "ffn_ln_b"),
        "grows": on_all(np.stack([arr("ffn_ln_g"), arr("ffn_ln_b")])),
        "wgate": np.concatenate([arr("ffn_wg_group"), arr("ffn_wg_inner").transpose(1, 0, 2).reshape(E, G * X)], 1),
        "ind": arr("attn_ind")[:, None, :],
        "rank": np.broadcast_to(np.arange(X, 0, -1, dtype=np.float32), (P, X)),
    }


def pack_experts(inp):
    def arr(n):
        return np.asarray(inp["L0_ffn_" + n])

    own = np.zeros((G, G, X, E), np.float32)
    own[np.arange(G), np.arange(G)] = arr("b2")
    gl = np.stack([arr("gln_g"), arr("gln_b")], 1)
    return {
        "ew1": arr("W1"),
        "ew2": arr("W2").reshape(G, X, XC, P, E).transpose(0, 1, 3, 2, 4),
        "eb1": arr("b1").reshape(G, X, XC, P).transpose(0, 3, 1, 2),
        "eb2": own.reshape(G, G * X, E),
        "glrows": np.broadcast_to(gl[:, None], (G, P, 2, E)),
    }


def constants():
    r, c = np.arange(P)[:, None], np.arange(P)[None, :]
    feature = np.arange(D)
    heads = (feature[:, None] // DH == np.arange(H)[None, :]).astype(np.float32)
    return {
        "ident": np.eye(P, dtype=np.float32),
        "identb": np.eye(P, dtype=mybir.dt.np(BF16)),
        "mask": np.stack([np.where(c >= r, 0.0, NEG), np.where(c <= r, 0.0, NEG)], 1).astype(mybir.dt.np(BF16)),
        "heads": heads.reshape(KT, DP, H).transpose(1, 0, 2).copy(),
        "headrow": heads.T.copy(),
        "iota": np.arange(P, dtype=np.float32)[:, None].copy(),
    }


SCRATCH = {
    "x": (X_SLOTS, P, NT, D), "kb": (KB_SLOTS, 2, S + 2), "qk": (NB, 4, D, S),
    "q1": (2, E, P), "kq": (NB, 4, E, S), "k2": (NB, 2, E, P),
    "base": (B, P, NT, E), "z": (B, P, NT, E), "zT": (B, E, S), "gates": (B, P, NT * (G + 1), X),
    "giT": (B, G * X, S),
}


def build(nc, a):
    for name, shape in SCRATCH.items():
        if name not in a:
            a[name] = nc.dram_tensor(f"scratch_{name}", shape, F32, kind="Internal").ap()
    with ExitStack() as outer:
        embed(nc, a, outer)
        tower(nc, a, outer)
        induce(nc, a, outer)
        experts(nc, a, outer)


def kernel(**inputs):
    import concourse.bacc as bacc
    from concourse.bass_utils import run_bass_kernel_spmd

    arrays = {**pack_tower(inputs), **pack_induce(inputs), **pack_experts(inputs), **constants()}
    arrays = {n: np.ascontiguousarray(v) for n, v in arrays.items()}
    nc = bacc.Bacc("TRN2", target_bir_lowering=False, num_devices=1)
    a = {n: nc.dram_tensor(n, v.shape, mybir.dt.from_np(v.dtype), kind="ExternalInput").ap()
         for n, v in arrays.items()}
    a["out"] = nc.dram_tensor("out", (B, S, E), F32, kind="ExternalOutput").ap()
    build(nc, a)
    r = run_bass_kernel_spmd(nc, [arrays], core_ids=[0])
    return r.results[0]["out"]
```

```python
from contextlib import ExitStack

import numpy as np

import concourse.bass as bass
from concourse import mybir

F32, F32R, BF16 = mybir.dt.float32, mybir.dt.float32r, mybir.dt.bfloat16
I32, U8 = mybir.dt.int32, mybir.dt.uint8
ALU, ACT, AX = mybir.AluOpType, mybir.ActivationFunctionType, mybir.AxisListType

P = 128
B, S = 8, 512
NT = S // P
NB = 2
VOCAB = 128
D, H, DH = 192, 12, 16
KT = 2
DP = D // KT
LAYERS, FF = 2, 768
FC = FF // P
E = 128
IH = E // DH
IF = 512 // P
G, X, XH = 4, 8, 512
XC = XH // P
W17 = DH + 1
EPS = 1e-5
NEG = -1e9
X_SLOTS = (LAYERS + 1) * B + NB
KB_SLOTS = LAYERS * B + NB
RING = 6


class Phase:

    def __init__(self, nc, name, ctx, outer, rounds=True):
        self.nc, self.name, self.ctx, self.outer, self.sems = nc, name, ctx, outer, {}
        self.sem_ctx = ctx if rounds else outer
        self.done, self.go, self.seen = (self.lasting(x) for x in ("round_done", "round_go", "round_seen"))

    def sb(self, name, shape, dt=F32):
        return self.ctx.enter_context(self.nc.sbuf_tensor(f"{self.name}_{name}", shape, dt))

    def psum(self, name):
        return self.ctx.enter_context(self.nc.psum_tensor(f"{self.name}_{name}", [P, 512], F32))

    def lasting(self, name):
        return self.outer.enter_context(self.nc.semaphore(f"{self.name}_{name}"))

    def sem(self, name):
        self.sems[name] = self.sem_ctx.enter_context(self.nc.semaphore(f"{self.name}_{name}"))
        return self.sems[name]

    def wait_lasting(self, eng, sem, value):
        eng.wait_ge(sem, value)
        eng.sem_inc(self.seen, 1)

    def end_round(self, eng, i):
        eng.drain().then_inc(self.done, 1)
        eng.wait_ge(self.go, i + 1)
        eng.sem_inc(self.seen, 1)

    def zero_round(self, pool, i):
        pool.drain().then_inc(self.done, 1)
        pool.wait_ge(self.done, i * 5 + 5)
        pool.sem_inc(self.seen, 1)
        for s in self.sems.values():
            pool.sem_clear(s)
        pool.sem_inc(self.go, 1)


class Chain:

    def __init__(self, eng, sem):
        self.eng, self.sem, self.n = eng, sem, 0

    def mark(self, ins):
        self.n += 1
        ins.then_inc(self.sem, 1)
        return self.n

    def after(self, n=None):
        self.eng.wait_ge(self.sem, self.n if n is None else n)


class Tiles:

    def __init__(self, ph, banks, order, name=""):
        self.banks, self.number = banks, {key: n for n, key in enumerate(order)}
        assert len(self.number) == len(order)
        self.ring = len(banks)
        self.full = [ph.sem(f"{name}full{b}") for b in range(self.ring)]
        self.free = [ph.sem(f"{name}free{b}") for b in range(self.ring)]

    def claim(self, pe, key):
        n = self.number[key]
        if n >= self.ring:
            pe.wait_ge(self.free[n % self.ring], n // self.ring)
        return self.banks[n % self.ring]

    def filled(self, ins, key):
        ins.then_inc(self.full[self.number[key] % self.ring], 1)

    def take(self, eng, key):
        n = self.number[key]
        eng.wait_ge(self.full[n % self.ring], n // self.ring + 1)
        return self.banks[n % self.ring]

    def copied(self, ins, key):
        ins.then_inc(self.free[self.number[key] % self.ring], 1)

    def wait_copied(self, eng, key):
        n = self.number[key]
        eng.wait_ge(self.free[n % self.ring], n // self.ring + 1)


def embed(nc, a, outer):
    with ExitStack() as ctx:
        ph = Phase(nc, "embed", ctx, outer, rounds=False)
        N = B * S
        HALF = N // 8
        ids, idsf = ph.sb("ids", [P, N], I32), ph.sb("idsf", [P, N])
        onehot = ph.sb("onehot", [P, N])
        emb, vocab = ph.sb("emb", [VOCAB, D]), ph.sb("vocab", [P, 1])
        x = ph.sb("x_rows", [P, N // P, D])
        pad, padf = ph.sb("pad", [B, S], U8), ph.sb("padf", [B, S])
        kb = ph.sb("kb", [B, 2, S + 2])
        banks = [ph.psum(f"bank{b}") for b in range(RING)]
        loaded, pad_in, stored = ph.sem("loaded"), ph.sem("pad_in"), ph.sem("stored")
        casted, hot, biased = ph.sem("casted"), ph.sem("hot"), ph.sem("biased")
        tiles = Tiles(ph, banks, [t for t in range(N // P // 2)])
        block = ctx.enter_context(nc.Block())

        @block.sync
        def _(sp):
            sp.dma_start(emb[:, :], a["emb"]).then_inc(loaded, 16)
            sp.dma_start(vocab[:, :], a["iota"]).then_inc(loaded, 16)
            sp.dma_start(ids[:, :], a["ids"]).then_inc(loaded, 16)
            sp.dma_start(pad[:, :], a["pad"]).then_inc(pad_in, 16)
            sp.wait_ge(biased, 5)
            for slot in range(0, KB_SLOTS, B):
                n = min(B, KB_SLOTS - slot)
                sp.dma_start(a["kb"][slot:slot + n], kb[0:n, :, :]).then_inc(stored, 16)
            for b in range(B):
                for t in (2 * b, 2 * b + 1):
                    tiles.wait_copied(sp, t)
                sp.dma_start(a["x"][b], x[:, NT * b:NT * b + NT, :]).then_inc(stored, 16)
            for b in range(NB):
                sp.dma_start(a["x"][X_SLOTS - NB + b], x[:, NT * b:NT * b + NT, :]).then_inc(stored, 16)
            sp.wait_ge(stored, 16 * (-(-KB_SLOTS // B) + B + NB))

        @block.vector
        def _(dve):
            dve.wait_ge(loaded, 48)
            for c in range(8):
                part = slice(c * HALF, c * HALF + HALF)
                dve.tensor_copy(idsf[:, part], ids[:, part]).then_inc(casted, 1)
                dve.wait_ge(casted, c + 1)
                dve.tensor_scalar(onehot[:, part], idsf[:, part], vocab[:, 0:1], None,
                                  ALU.is_equal).then_inc(hot, 1)
            dve.wait_ge(pad_in, 16)
            dve.tensor_copy(padf[:, :], pad[:, :]).then_inc(biased, 1)
            dve.wait_ge(biased, 1)
            dve.tensor_scalar(padf[:, :], padf[:, :], 0.0, None, ALU.not_equal).then_inc(biased, 1)
            dve.wait_ge(biased, 2)
            dve.memset(kb[:, :, S:S + 2], 0.0)
            dve.tensor_scalar(kb[:, 0, 0:S], padf[:, :], -10000.0, None, ALU.mult)
            dve.tensor_scalar(kb[:, 1, 0:S], padf[:, :], -10000.0, None, ALU.mult).then_inc(biased, 1)
            dve.wait_ge(biased, 3)
            dve.memset(kb[:, 0, 0:1], -10000.0).then_inc(biased, 1)
            dve.memset(kb[:, 0, S + 1:S + 2], NEG).then_inc(biased, 1)

        @block.tensor
        def _(pe):
            for t in range(N // P // 2):
                pe.wait_ge(hot, t // 2 + 1)
                bank = tiles.claim(pe, t)
                for j in range(2):
                    tok = slice((2 * t + j) * P, (2 * t + j + 1) * P)
                    mm = pe.matmul(bank[:, j * D:j * D + D], onehot[:, tok], emb[:, :], start=True, stop=True)
                tiles.filled(mm, t)

        @block.scalar
        def _(act):
            for t in range(N // P // 2):
                bank = tiles.take(act, t)
                tiles.copied(act.activation(x[:, 2 * t:2 * t + 2, :], bank[:, 0:2 * D], ACT.Copy), t)


def tower(nc, a, outer):
    with ExitStack() as ctx:
        ph = Phase(nc, "tower", ctx, outer)
        wqk = ph.sb("wqk", [DP, 2, KT, D])
        wvo = ph.sb("wvo", [DP, 2, KT, D])
        w1, w2 = ph.sb("w1", [DP, KT, FF]), ph.sb("w2", [P, FC, D])
        rows = ph.sb("rows", [P, 5, D])
        rows2 = ph.sb("rows2", [P, 2, D])
        cols = ph.sb("cols", [DP, 4, KT])
        b1c = ph.sb("b1c", [P, FC])
        ident, identb = ph.sb("ident", [P, P]), ph.sb("identb", [P, P], BF16)
        mask = ph.sb("mask", [P, 2, P], BF16)
        onerow = ph.sb("onerow", [1, P], F32R)
        onesr = ph.sb("onesr", [1, S])
        heads = ph.sb("heads", [DP, KT, H])
        headrow = ph.sb("headrow", [H, D])
        ones12 = ph.sb("ones12", [H, 1])
        half = ph.sb("half", [P, NT])
        x = [ph.sb(f"x{s}", [P, NT, D]) for s in range(NB)]
        xb = [ph.sb(f"xb{s}", [P, NT, D]) for s in range(NB)]
        xT = [ph.sb(f"xT{s}", [DP, KT, S]) for s in range(NB)]
        qk = ph.sb("qk", [DP, 4, KT, S], F32R)
        q_st = [ph.sb(f"q_st{s}", [P, H // 2, S], F32R) for s in range(NB)]
        k_st = [ph.sb(f"k_st{s}", [P, H // 2, S + 2], F32R) for s in range(NB)]
        v = [ph.sb(f"v{s}", [P, NT, H, W17]) for s in range(NB)]
        hid = [ph.sb(f"hid{s}", [P, FC, S]) for s in range(NB)]
        v0 = ph.sb("vglob", [P, NB, H, W17])
        padrow = ph.sb("padrow", [1, NB, S], F32R)
        prob = [ph.sb(f"prob{j}", [P, H, 2 + 3 * P]) for j in range(2)]
        probT = [ph.sb(f"probT{j}", [P, 3 * P]) for j in range(4)]
        negmax = ph.sb("negmax", [P, NB, NT * H])
        glob = ph.sb("glob", [P, H, W17])
        oT = ph.sb("oT", [P, 2, H // 4 * P])
        osum = ph.sb("osum", [P, H, W17])
        orec = ph.sb("orec", [P, H])
        qg = ph.sb("qg", [DP, 2, KT, P], F32R)
        pg = ph.sb("pg", [H, NB, S])
        pgst = ph.sb("pgst", [H, NB, 4])
        pgT = ph.sb("pgT", [P, NT, H])
        ogm = ph.sb("ogm", [H, D])
        st6, mv = ph.sb("st6", [P, NB, NT, 6]), ph.sb("mv", [P, NB, NT, 2])
        rstd = ph.sb("rstd", [P, NB, NT])
        banks = [ph.psum(f"bank{b}") for b in range(RING)]
        obank = [ph.psum(f"obank{b}") for b in range(2)]
        BV, BO, G1, BE1, B2 = range(5)
        G2, BE2 = range(2)

        STEPS = NT * H
        LAG_T, LAG_V = 2, 4
        LAG_R = 3
        QUERY_TILES = (1, 0, 3, 2)
        AT_T, AT_O, AT_1 = 6, 17, 38

        AT_OT, AT_OP, AT_N, AT_X = 2, 6, 14, 18

        def step(k):
            place, j = divmod(k, H)
            return place, QUERY_TILES[place], 2 * (j % (H // 2)) + j // (H // 2)

        def row_tile(k):
            i, rest = divmod(k - LAG_V - LAG_R + 1, H)
            return i - 1 if i > 0 and rest == 0 else None

        order = []
        for s in range(NB):
            order += [("xT", s, k) for k in range(KT)]
        for s in range(NB):
            order += [("qk", s, w, m) for w in range(2) for m in range(KT)]
            order += [("v", s, t) for t in range(2)]
            order += [("v0", s), ("sg", s)]
        for s in range(NB):
            for k in range(STEPS + LAG_V + LAG_R):
                if k < STEPS:
                    order.append(("s", s, k))
                if k == AT_T:
                    order.append(("pgT", s))
                if k == AT_O:
                    order.append(("og", s))
                if k == AT_1:
                    order.append(("og1", s))
                if LAG_T <= k < STEPS + LAG_T:
                    order.append(("pT", s, k - LAG_T))
                if row_tile(k) is not None:
                    order.append(("rows", s, row_tile(k)))
                if s and k == AT_OT:
                    order += [("oT", 0, m) for m in range(KT)]
                if s and k == AT_OP:
                    order += [("o", 0, t) for t in range(2)]
                if s and k == AT_X:
                    order += [("x1T", 0, m) for m in range(KT)]

        def up(s, *chunks):
            return [("up", s, c) for c in chunks]

        order += up(0, 0, 1, 2) + [("oT", 1, m) for m in range(KT)] + up(0, 3) + [("o", 1, t) for t in range(2)]
        order += up(0, *range(4, FC)) + [("down", 0, t) for t in range(2)] + [("x1T", 1, m) for m in range(KT)]
        order += up(1, *range(FC)) + [("down", 1, t) for t in range(2)]
        tiles = Tiles(ph, banks, order)
        o_full, o_free = ph.sem("o_full"), ph.sem("o_free")
        o_clear = ph.lasting("o_clear")

        weights_in, consts_in = ph.lasting("weights_in"), ph.lasting("consts_in")
        ones_in, ffn_in = ph.lasting("ones_in"), ph.lasting("ffn_in")
        consts_set, wq_scaled = ph.lasting("consts_set"), ph.lasting("wq_scaled")
        x_in, kb_in, pad_in = ph.lasting("x_in"), ph.lasting("kb_in"), ph.lasting("pad_in")
        x_out, x_stored, rows2_in = ph.lasting("x_out"), ph.sem("x_stored"), ph.lasting("rows2_in")
        split_hi = ph.sem("split_hi")
        qk_out, stacked = ph.sem("qk_out"), [ph.sem("stacked_even"), ph.sem("stacked_odd")]
        kglob = ph.sem("kglob")
        xb_ready, xb2_ready = ph.sem("xb_ready"), ph.sem("xb2_ready")
        qg_ready, rowmax = ph.sem("qg_ready"), ph.sem("rowmax")
        glob_ready, o_tok = ph.sem("glob_ready"), ph.sem("o_tok")
        pg_max, pg_norm = ph.sem("pg_max"), ph.sem("pg_norm")
        normed, moments, roots = ph.sem("normed"), ph.sem("moments"), ph.sem("roots")
        dve_chain, pool_chain = ph.sem("dve_chain"), ph.sem("pool_chain")
        x_final = ph.sem("x_final")
        block = ctx.enter_context(nc.Block())
        ROUNDS = B // NB
        LAST = LAYERS * ROUNDS
        NW, NFF = 4 * 16, 3 * 16

        def blocks(i):
            return range(max(i - 1, 0), min(i + 2, NT))

        def stack(buf, h):
            return buf[64 * (h % 2):64 * (h % 2) + 3 * DH + 1, h // 2, :]

        @block.sync
        def _(sp):
            def slot(t, n):
                return t[n:n + 1] if isinstance(n, int) else t[bass.ds(n, 1)]

            def load_weights(layer):
                for dst, src in ((wqk, "wqk"), (cols, "cols"), (rows, "rows"), (wvo, "wvo")):
                    sp.dma_start(dst[:], a[src][layer]).then_inc(weights_in, 16)
                for dst, src in ((w1, "w1"), (w2, "w2"), (b1c, "b1c")):
                    sp.dma_start(dst[:], a[src][layer]).then_inc(ffn_in, 16)

            def load_rows2(layer):
                sp.dma_start(rows2[:], a["rows2"][layer]).then_inc(rows2_in, 16)

            def load_tokens(i, s):
                sp.dma_start(xb[s][:, :, :], slot(a["x"], i * NB + s).rearrange("o p t d -> (o p) t d"))\
                    .then_inc(x_in, 16)

            def load_biases(i):
                for s in range(NB):
                    for par in range(2):
                        p = 64 * par + 3 * DH
                        sp.dma_start(k_st[s][p:p + 1, :, :].bitcast(F32),
                                     slot(a["kb"], i * NB + s)[:, 0:1, :].broadcast_to([1, H // 2, S + 2]))\
                            .then_inc(kb_in, 16)
                    sp.dma_start(padrow[:, s, :].bitcast(F32), slot(a["kb"], i * NB + s)[:, 1, 0:S])\
                        .then_inc(pad_in, 16)

            def store_sequences(i):
                for s in range(NB):
                    sp.wait_ge(x_final, s + 1)
                    dst = slot(a["x"], (i - 1 + ROUNDS) * NB + s)
                    sp.dma_start(dst.rearrange("o p t d -> (o p) t d"), x[s][:, :, :]).then_inc(x_out, 16)

            def round_(i, first=False, new_layer=None):
                for s in range(NB):
                    for w in range(2):
                        for m in range(KT):
                            tiles.wait_copied(sp, ("qk", s, w, m))
                    for w in range(4):
                        sp.dma_start(a["qk"][s, w].rearrange("(m p) q -> p m q", p=DP),
                                     qk[:, w, :, :].bitcast(F32)).then_inc(qk_out, 16)
                    sp.wait_ge(qk_out, 64 * (s + 1))
                    for par in range(2):
                        for buf, parts in ((q_st[s], (0, 1, 0)), (k_st[s], (2, 2, 3))):
                            for row, w in enumerate(parts):
                                src = a["qk"][s, w].rearrange("(c par d) q -> par d c q", par=2, d=DH)
                                p = 64 * par + DH * row
                                sp.dma_start(buf[p:p + DH, :, 0:S].bitcast(F32), src[par])\
                                    .then_inc(stacked[par], 16)
                if not first:
                    store_sequences(i)
                    ph.wait_lasting(sp, x_out, 16 * NB * i)
                sp.sem_inc(x_stored, 1)
                if new_layer is not None:
                    load_rows2(new_layer)
                    sp.wait_ge(rows2_in, 16 * (new_layer + 1))
                tiles.take(sp, ("s", NB - 1, STEPS - 1))
                load_biases(i + 1)
                for s in range(NB):
                    for t in range(2):
                        tiles.wait_copied(sp, ("down", s, t))
                    load_tokens(i + 1, s)
                ph.end_round(sp, i)

            for s in range(NB):
                load_tokens(0, s)
            for dst, src in ((ident, "ident"), (identb, "identb"), (heads, "heads"), (headrow, "headrow")):
                sp.dma_start(dst[:], a[src]).then_inc(consts_in, 16)
            sp.dma_start(mask[:, :, :], a["mask"]).then_inc(consts_in, 16)
            for layer in range(LAYERS):
                first = layer * ROUNDS
                load_weights(layer)
                if layer == 0:
                    load_rows2(0)
                    load_biases(0)
                round_(first, first=layer == 0, new_layer=layer if layer else None)
                with sp.Fori(first + 1, first + ROUNDS) as i:
                    round_(i)
            store_sequences(LAST)
            sp.wait_ge(x_out, 16 * NB * LAST)
            sp.wait_ge(x_in, 16 * NB * (LAST + 1))
            sp.wait_ge(kb_in, 16 * 2 * NB * (LAST + 1))
            sp.wait_ge(pad_in, 16 * NB * (LAST + 1))
            ph.end_round(sp, LAST)

        @block.gpsimd
        def _(pool):
            pool.memset(onesr[:, :], 1.0).then_inc(consts_set, 1)
            pool.memset(half[:, :], -0.5).then_inc(consts_set, 1)
            pool.memset(ones12[:, :], 1.0).then_inc(consts_set, 1)
            pool.memset(onerow[:, :].bitcast(F32), 1.0).then_inc(consts_set, 1)
            pool.memset(qg[:, :, :, :].bitcast(F32), 0.0).then_inc(consts_set, 1)
            for s in range(NB):
                pool.memset(v[s][:, :, :, DH:W17], 1.0).then_inc(consts_set, 1)
                pool.memset(x[s][:, :, :], 0.0).then_inc(consts_set, 1)
            pool.wait_ge(consts_in, 80)
            pool.wait_ge(rows2_in, 16)

            def root(ch, n, s):
                pool.wait_ge(moments, n + 1)
                ch.mark(pool.tensor_scalar(rstd[:, s, :], mv[:, s, :, 1], EPS, None, ALU.add))
                ch.after()
                pool.tensor_tensor(rstd[:, s, :], rstd[:, s, :], half[:, :], ALU.pow).then_inc(roots, 1)

            def after_attention(ch, s):
                root(ch, NB + s, s)
                pool.wait_ge(normed, NB + s + 1)
                for row, op in ((G1, ALU.mult), (BE1, ALU.add), (B2, ALU.add)):
                    ins = pool.tensor_tensor(xb[s][:, :, :], (x if row == G1 else xb)[s][:, :, :],
                                             rows[:, row:row + 1, :].broadcast_to([P, NT, D]), op)
                    if row == B2:
                        ins.then_inc(xb2_ready, 1)
                    else:
                        ch.mark(ins)
                        ch.after()

            def global_key(s):
                pool.wait_ge(qg_ready, 4 * NB)
                for par in range(2):
                    pool.wait_ge(stacked[par], 16 * 6 * (s + 1))
                    part = k_st[s][64 * par:64 * par + 3 * DH, :, :]
                    pool.tensor_copy(part[:, :, S:S + 2],
                                     part[:, :, 0:1].bitcast(F32).broadcast_to([3 * DH, H // 2, 2]))\
                        .then_inc(kglob, 1)
                    pool.wait_ge(kglob, 2 * s + par + 1)

            def finish(ch, s):
                pool.wait_ge(normed, s + 1)
                ch.mark(pool.tensor_tensor(x[s][:, :, :], x[s][:, :, :],
                                           rows2[:, G2:G2 + 1, :].broadcast_to([P, NT, D]), ALU.mult))
                ch.after()
                pool.tensor_tensor(x[s][:, :, :], x[s][:, :, :],
                                   rows2[:, BE2:BE2 + 1, :].broadcast_to([P, NT, D]), ALU.add)\
                    .then_inc(x_final, 1)

            with pool.Fori(0, LAYERS) as layer:
                with pool.Fori(0, ROUNDS) as r:
                    pool.wait_ge(consts_set, 5 + 2 * NB)
                    ch = Chain(pool, pool_chain)
                    ph.wait_lasting(pool, weights_in, NW * (layer + 1))
                    ph.wait_lasting(pool, x_in, 16 * NB * (layer * ROUNDS + r + 1))
                    for s in range(NB):
                        root(ch, s, s)
                    for s in range(NB):
                        for m in range(KT):
                            tiles.wait_copied(pool, ("qk", s, 0, m))
                        if s:
                            tiles.take(pool, ("sg", s - 1))
                        for w in range(2):
                            for m in range(KT):
                                pool.tensor_scalar(qg[:, w, m, 0:H], heads[:, m, :],
                                                   qk[:, w, m, 0:1].bitcast(F32), None, ALU.mult)\
                                    .then_inc(qg_ready, 1)
                    global_key(0)
                    for s in range(NB):
                        finish(ch, s)
                    for s in range(NB):
                        for k in range(KT):
                            tiles.take(pool, ("xT", s, k))
                        pool.tensor_tensor(xb[s][:, :, :], xb[s][:, :, :],
                                           rows[:, BO:BO + 1, :].broadcast_to([P, NT, D]), ALU.add)\
                            .then_inc(xb_ready, 1)
                    global_key(1)
                    for s in range(NB):
                        for i in range(NT):
                            n = s * NT + i
                            pool.wait_ge(kglob, 2 * NB)
                            tiles.wait_copied(pool, ("v0", s))
                            tiles.wait_copied(pool, ("s", s, i * H + H - 1))
                            if n:
                                tiles.wait_copied(pool, ("rows", (n - 1) // NT, (n - 1) % NT))
                            pool.tensor_tensor(glob[:, :, :], v0[:, s, :, :],
                                               prob[i % 2][:, :, 0:1].broadcast_to([P, H, W17]), ALU.mult)\
                                .then_inc(glob_ready, 1)
                            if n == NT:
                                after_attention(ch, 0)
                    after_attention(ch, NB - 1)
                    ph.zero_round(pool, layer * ROUNDS + r)
            ch = Chain(pool, pool_chain)
            for s in range(NB):
                root(ch, s, s)
            for s in range(NB):
                finish(ch, s)
            ph.zero_round(pool, LAST)

        @block.tensor
        def _(pe):
            pe.wait_ge(consts_in, 80)
            pe.wait_ge(consts_set, 5 + 2 * NB)
            pe.wait_ge(o_clear, 2)

            def transposes(key, src, tile_of, n):
                bank = tiles.claim(pe, key)
                for t in range(n):
                    mm = pe.transpose(bank[0:DP, t * P:t * P + P], tile_of(src, t), ident[:, :])
                tiles.filled(mm, key)

            def rows_product(key, lhs, rhs, kts, width):
                _, s, t2 = key
                bank = tiles.claim(pe, key)
                for j in range(2):
                    t = 2 * t2 + j
                    for k in range(kts):
                        mm = pe.matmul(bank[:, j * width:(j + 1) * width], lhs[:, k, t * P:t * P + P],
                                       rhs[:, k, :], start=(k == 0), stop=(k == kts - 1))
                tiles.filled(mm, key)

            def turned(name, src, s):
                for k in range(KT):
                    transposes((name, s, k), src, lambda b_, t, k=k: b_[:, t, k * DP:k * DP + DP], NT)

            def outputs_turned(s):
                pe.wait_ge(o_tok, NT * (s + 1))
                tiles.wait_copied(pe, ("og1", s))
                turned("oT", x[s], s)

            def output_product(s):
                for k in range(KT):
                    tiles.wait_copied(pe, ("oT", s, k))
                for t in range(2):
                    rows_product(("o", s, t), xT[s], wvo[:, 1, :, :], KT, D)

            def shifted_turned(s):
                pe.wait_ge(normed, NB + s + 1)
                turned("x1T", x[s], s)

            def up_chunk(s, c):
                for k in range(KT):
                    tiles.wait_copied(pe, ("x1T", s, k))
                bank = tiles.claim(pe, ("up", s, c))
                for k in range(KT):
                    mm = pe.matmul(bank[:, :], w1[:, k, c * P:c * P + P], xT[s][:, k, :],
                                   start=(k == 0), stop=(k == KT - 1))
                tiles.filled(mm, ("up", s, c))

            def down_product(s):
                for c in range(FC):
                    tiles.wait_copied(pe, ("up", s, c))
                for t in range(2):
                    rows_product(("down", s, t), hid[s], w2, FC, D)

            with pe.Fori(0, LAYERS) as layer:
                with pe.Fori(0, ROUNDS) as r:
                    ph.wait_lasting(pe, weights_in, NW * (layer + 1))
                    ph.wait_lasting(pe, wq_scaled, layer + 1)
                    ph.wait_lasting(pe, x_in, 16 * NB * (layer * ROUNDS + r + 1))
                    for s in range(NB):
                        for k in range(KT):
                            transposes(("xT", s, k), xb[s], lambda b_, t, k=k: b_[:, t, k * DP:k * DP + DP], NT)
                    for s in range(NB):
                        for k in range(KT):
                            tiles.wait_copied(pe, ("xT", s, k))
                        for w in range(2):
                            for m in range(KT):
                                key = ("qk", s, w, m)
                                bank = tiles.claim(pe, key)
                                for k in range(KT):
                                    mm = pe.matmul(bank[0:DP, :], wqk[:, w, k, m * DP:m * DP + DP],
                                                   xT[s][:, k, :], start=(k == 0), stop=(k == KT - 1))
                                tiles.filled(mm, key)
                        for t in range(2):
                            rows_product(("v", s, t), xT[s], wvo[:, 0, :, :], KT, D)
                        tiles.wait_copied(pe, ("v", s, 0))
                        tiles.wait_copied(pe, ("v", s, 1))
                        bank = tiles.claim(pe, ("v0", s))
                        mm = pe.matmul(bank[:, 0:H * W17], onesr[0:1, 0:P],
                                       v[s][0:1, 0, :, :].rearrange("p h w -> p (h w)"), start=True, stop=True)
                        tiles.filled(mm, ("v0", s))
                        bank = tiles.claim(pe, ("sg", s))
                        pe.wait_ge(qg_ready, 4 * (s + 1))
                        ph.wait_lasting(pe, pad_in, 16 * NB * (layer * ROUNDS + r + 1))
                        n = 0
                        for m in range(KT):
                            for w, kw in ((0, 2), (1, 2), (0, 3)):
                                pe.matmul(bank[:, :], qg[:, w, m, :], qk[:, kw, m, :], start=(n == 0), stop=False)
                                n += 1
                        mm = pe.matmul(bank[:, :], onerow[:, :], padrow[:, s, :], start=False, stop=True)
                        tiles.filled(mm, ("sg", s))
                    for s in range(NB):
                        pe.wait_ge(ones_in, 16 * NB * 2)
                        ph.wait_lasting(pe, kb_in, 16 * 2 * NB * (layer * ROUNDS + r + 1))
                        for k in range(STEPS + LAG_V + LAG_R):
                            if k < STEPS:
                                _, i, h = step(k)
                                if k in (0, H // 2):
                                    pe.wait_ge(stacked[h % 2], 16 * 6 * (s + 1))
                                    pe.wait_ge(kglob, 2 * s + h % 2 + 1)
                                bl = blocks(i)
                                key = ("s", s, k)
                                bank = tiles.claim(pe, key)
                                q, kk = stack(q_st[s], h)[:, i * P:i * P + P], stack(k_st[s], h)
                                pe.matmul(bank[:, 0:2], q, kk[:, S:S + 2], start=True, stop=True)
                                todo = [(2, 2 + len(bl) * P, q, kk[:, bl[0] * P:(bl[-1] + 1) * P])]
                                if i > 0:
                                    todo.append((2, 2 + P, identb[:, :], mask[:, 0, :]))
                                if i < NT - 1:
                                    e_ = 2 + len(bl) * P
                                    todo.append((e_ - P, e_, identb[:, :], mask[:, 1, :]))
                                for n, (c0, c1, lhs, rhs) in enumerate(todo):
                                    mm = pe.matmul(bank[:, c0:c1], lhs, rhs, start=(n == 0),
                                                   stop=(n == len(todo) - 1), skip_group_check=True)
                                tiles.filled(mm, key)
                            if k == AT_T:
                                pe.wait_ge(pg_norm, s + 1)
                                bank = tiles.claim(pe, ("pgT", s))
                                for t in range(NT):
                                    mm = pe.transpose(bank[:, t * H:t * H + H], pg[:, s, t * P:t * P + P], ident[0:H, 0:H])
                                tiles.filled(mm, ("pgT", s))
                            if k == AT_O:
                                tiles.wait_copied(pe, ("pgT", s))
                                bank = tiles.claim(pe, ("og", s))
                                for t in range(NT):
                                    mm = pe.matmul(bank[0:H, 0:D], pgT[:, t, :], v[s][:, t, :, 0:DH],
                                                   start=(t == 0), stop=(t == NT - 1))
                                tiles.filled(mm, ("og", s))
                            if k == AT_1:
                                tiles.wait_copied(pe, ("og", s))
                                bank = tiles.claim(pe, ("og1", s))
                                tiles.filled(pe.matmul(bank[0:1, 0:D], ones12[:, :], ogm[:, :], start=True, stop=True),
                                             ("og1", s))
                            if LAG_T <= k < STEPS + LAG_T:
                                kt = k - LAG_T
                                place, i, h = step(kt)
                                key = ("pT", s, kt)
                                bank = tiles.claim(pe, key)
                                tiles.wait_copied(pe, ("s", s, kt))
                                for j in range(len(blocks(i))):
                                    mm = pe.transpose(bank[:, j * P:j * P + P],
                                                      prob[place % 2][:, h, 2 + j * P:2 + j * P + P], ident[:, :])
                                tiles.filled(mm, key)
                            if LAG_V <= k < STEPS + LAG_V:
                                kv = k - LAG_V
                                place, i, h = step(kv)
                                n = s * NT + place
                                tiles.wait_copied(pe, ("pT", s, kv))
                                if h == 0 and n >= 2:
                                    pe.wait_ge(o_free, n - 1)
                                bl = blocks(i)
                                p, c = 32 * (h % 4), h // 4 * P
                                for j, t in enumerate(bl):
                                    mm = pe.matmul(obank[n % 2][p:p + W17, c:c + P], v[s][:, t, h, :],
                                                   probT[kv % 4][:, j * P:j * P + P],
                                                   start=(j == 0), stop=(j == len(bl) - 1))
                                if h == H - 1:
                                    mm.then_inc(o_full, 1)
                            if row_tile(k) is not None:
                                n = s * NT + row_tile(k)
                                key = ("rows", s, row_tile(k))
                                bank = tiles.claim(pe, key)
                                pe.wait_ge(o_free, n + 1)
                                for c in range(H // 4):
                                    mm = pe.transpose(bank[:, c * P:c * P + P], oT[:, n % 2, c * P:c * P + P],
                                                      ident[:, :])
                                tiles.filled(mm, key)
                            if s and k == AT_OT:
                                outputs_turned(0)
                            if s and k == AT_OP:
                                output_product(0)
                            if s and k == AT_X:
                                shifted_turned(0)
                    ph.wait_lasting(pe, ffn_in, NFF * (layer + 1))
                    for c in range(3):
                        up_chunk(0, c)
                    outputs_turned(1)
                    up_chunk(0, 3)
                    output_product(1)
                    for c in range(4, FC):
                        up_chunk(0, c)
                    down_product(0)
                    shifted_turned(1)
                    for c in range(FC):
                        up_chunk(1, c)
                    down_product(1)
                    ph.end_round(pe, layer * ROUNDS + r)
            ph.end_round(pe, LAST)

        @block.scalar
        def _(act):
            act.wait_ge(consts_set, 1)
            for s in range(NB):
                for par in range(2):
                    p = 64 * par + 3 * DH
                    act.dma_start(q_st[s][p:p + 1, :, :].bitcast(F32),
                                  onesr[:, None, :].broadcast_to([1, H // 2, S])).then_inc(ones_in, 16)

            def outputs_turned(s):
                bank = tiles.take(act, ("oT", s, 0))
                tiles.copied(act.activation(xT[s][:, 0, :], bank[0:DP, :], ACT.Copy), ("oT", s, 0))

            def shifted_turned(s):
                bank = tiles.take(act, ("x1T", s, 0))
                tiles.copied(act.activation(xT[s][:, 0, :], bank[0:DP, :], ACT.Identity,
                                            scale=cols[:, 2, 0:1], bias=cols[:, 3, 0:1]), ("x1T", s, 0))

            def relu(s, c):
                bank = tiles.take(act, ("up", s, c))
                tiles.copied(act.activation(hid[s][:, c, :], bank[:, :], ACT.Relu, bias=b1c[:, c:c + 1]),
                             ("up", s, c))

            with act.Fori(0, LAYERS) as layer:
                with act.Fori(0, ROUNDS) as r:
                    ph.wait_lasting(act, weights_in, NW * (layer + 1))
                    ph.wait_lasting(act, wq_scaled, layer + 1)
                    for s in range(NB):
                        bank = tiles.take(act, ("xT", s, 0))
                        tiles.copied(act.activation(xT[s][:, 0, :], bank[0:DP, :], ACT.Copy), ("xT", s, 0))
                    for s in range(NB):
                        for w in range(2):
                            for m in range(KT):
                                bank = tiles.take(act, ("qk", s, w, m))
                                if s:
                                    act.wait_ge(qk_out, 64 * s)
                                    tiles.take(act, ("sg", s - 1))
                                act.activation(qk[:, 2 * w, m, :], bank[0:DP, :], ACT.Identity,
                                               bias=cols[:, w, m:m + 1]).then_inc(split_hi, 1)
                        bank = tiles.take(act, ("sg", s))
                        act.wait_ge(pg_max, s + 1)
                        tiles.copied(act.activation(pg[:, s, :], bank[0:H, :], ACT.Exp, bias=pgst[:, s, 0:1],
                                                    accum_out=pgst[:, s, 1:2]), ("sg", s))
                    for s in range(NB):
                        for k in range(STEPS + LAG_V + 1):
                            if k < STEPS:
                                place, i, h = step(k)
                                n = s * NT + place
                                if h == 0 and n >= 2:
                                    act.wait_ge(glob_ready, n - 1)
                                    tiles.take(act, ("pT", (n - 2) // NT, ((n - 2) % NT) * H + H - 1))
                                bank = tiles.take(act, ("s", s, k))
                                act.wait_ge(rowmax, s * STEPS + k + 1)
                                w_ = 2 + len(blocks(i)) * P
                                tiles.copied(act.activation(prob[place % 2][:, h, 0:w_], bank[:, 0:w_], ACT.Exp,
                                                            bias=negmax[:, s, k:k + 1]), ("s", s, k))
                            if LAG_T <= k < STEPS + LAG_T and (k - LAG_T) % 2:
                                kt = k - LAG_T
                                bank = tiles.take(act, ("pT", s, kt))
                                w_ = len(blocks(step(kt)[1])) * P
                                tiles.copied(act.activation(probT[kt % 4][:, 0:w_], bank[:, 0:w_], ACT.Copy),
                                             ("pT", s, kt))
                            if s and k == AT_OT + 1:
                                outputs_turned(0)
                            if s and k == AT_X + 1:
                                shifted_turned(0)
                            if k > LAG_V and (k - LAG_V) % H == 0:
                                n = s * NT + (k - LAG_V) // H - 1
                                if n >= 2:
                                    tiles.take(act, ("rows", (n - 2) // NT, (n - 2) % NT))
                                act.wait_ge(o_full, n + 1)
                                act.activation(oT[:, n % 2, :], obank[n % 2][:, 0:H // 4 * P], ACT.Copy)\
                                    .then_inc(o_free, 1)
                    relu(0, 0)
                    relu(0, 2)
                    outputs_turned(1)
                    relu(0, 4)
                    shifted_turned(1)
                    for c in range(0, FC, 2):
                        relu(1, c)
                    ph.end_round(act, layer * ROUNDS + r)
            ph.end_round(act, LAST)

        @block.vector
        def _(dve):
            for bank in obank:
                dve.memset(bank[:, :], 0.0).then_inc(o_clear, 1)
            dve.wait_ge(consts_set, 5 + 2 * NB)

            def statistics(ch, s):
                for t in range(NT):
                    ins = dve.bn_stats(st6[:, s, t, :], x[s][:, t, :])
                ch.mark(ins)
                ch.after()
                for t in range(NT):
                    ins = dve.bn_aggr(mv[:, s, t, :], st6[:, s, t, :])
                ins.then_inc(moments, 1)

            def normalise(n, s):
                dve.wait_ge(moments, n + 1)
                dve.wait_ge(roots, n + 1)
                for t in range(NT):
                    ins = dve.tensor_scalar(x[s][:, t, :], x[s][:, t, :], mv[:, s, t, 0:1],
                                            rstd[:, s, t:t + 1], ALU.subtract, ALU.mult)
                ins.then_inc(normed, 1)

            def residual(ln, key, base_sem, s):
                for t in range(2):
                    bank = tiles.take(dve, (key, s, t))
                    if t == 0:
                        dve.wait_ge(base_sem, s + 1)
                        tiles.take(dve, (("oT", "x1T")[ln], s, KT - 1))
                        if ln:
                            dve.wait_ge(xb2_ready, s + 1)
                    tiles.copied(dve.tensor_tensor(
                        x[s][:, 2 * t:2 * t + 2, :].rearrange("p t d -> p (t d)"), bank[:, 0:2 * D],
                        xb[s][:, 2 * t:2 * t + 2, :].rearrange("p t d -> p (t d)"), ALU.add), (key, s, t))
                for t in range(2):
                    tiles.wait_copied(dve, (key, s, t))
            def outputs_turned(s):
                bank = tiles.take(dve, ("oT", s, 1))
                tiles.copied(dve.tensor_copy(xT[s][:, 1, :], bank[0:DP, :]), ("oT", s, 1))

            def shifted_turned(s):
                bank = tiles.take(dve, ("x1T", s, 1))
                tiles.copied(dve.tensor_scalar(xT[s][:, 1, :], bank[0:DP, :], cols[:, 2, 1:2],
                                               cols[:, 3, 1:2], ALU.mult, ALU.add), ("x1T", s, 1))

            def relu(s, c):
                bank = tiles.take(dve, ("up", s, c))
                tiles.copied(dve.tensor_scalar(hid[s][:, c, :], bank[:, :], b1c[:, c:c + 1], 0.0,
                                               ALU.add, ALU.max), ("up", s, c))

            with dve.Fori(0, LAYERS) as layer:
                ph.wait_lasting(dve, weights_in, NW * (layer + 1))
                dve.tensor_scalar(wqk[:, 0, :, :], wqk[:, 0, :, :], DH ** -0.5, None, ALU.mult)
                dve.tensor_scalar(cols[:, 0, :], cols[:, 0, :], DH ** -0.5, None, ALU.mult).then_inc(wq_scaled, 1)
                with dve.Fori(0, ROUNDS) as r:
                    ph.wait_lasting(dve, wq_scaled, layer + 1)
                    ch = Chain(dve, dve_chain)
                    for s in range(NB):
                        bank = tiles.take(dve, ("xT", s, 1))
                        tiles.copied(dve.tensor_copy(xT[s][:, 1, :], bank[0:DP, :]), ("xT", s, 1))
                    for s in range(NB):
                        statistics(ch, s)
                    for s in range(NB):
                        for w in range(2):
                            for m in range(KT):
                                dve.wait_ge(split_hi, s * 4 + w * KT + m + 1)
                                key = ("qk", s, w, m)
                                bank = tiles.take(dve, key)
                                tiles.copied(dve.scalar_tensor_tensor(
                                    qk[:, 2 * w + 1, m, :], bank[0:DP, :], cols[:, w, m:m + 1],
                                    qk[:, 2 * w, m, :].bitcast(F32), ALU.add, ALU.subtract), key)
                        normalise(s, s)
                        for t in range(2):
                            bank = tiles.take(dve, ("v", s, t))
                            tiles.copied(dve.tensor_tensor(
                                v[s][:, 2 * t:2 * t + 2, :, 0:DH],
                                bank[:, 0:2 * D].rearrange("p (t h d) -> p t h d", t=2, d=DH),
                                rows[:, BV:BV + 1, :].broadcast_to([P, 2, D])
                                .rearrange("p t (h d) -> p t h d", d=DH), ALU.add), ("v", s, t))
                        bank = tiles.take(dve, ("v0", s))
                        tiles.copied(dve.tensor_copy(v0[:, s, :, :].rearrange("p h w -> p (h w)"),
                                                     bank[:, 0:H * W17]), ("v0", s))
                        bank = tiles.take(dve, ("sg", s))
                        dve.tensor_reduce(pgst[:, s, 0:1], bank[0:H, :], AX.X, ALU.max, negate=True)\
                            .then_inc(pg_max, 1)
                        tiles.wait_copied(dve, ("sg", s))
                        ch.mark(dve.reciprocal(pgst[:, s, 2:3], pgst[:, s, 1:2]))
                        ch.after()
                        dve.tensor_scalar(pg[:, s, :], pg[:, s, :], pgst[:, s, 2:3], None, ALU.mult)\
                            .then_inc(pg_norm, 1)
                    for s in range(NB):
                        def gather(i):
                            n = s * NT + i
                            dve.wait_ge(glob_ready, n + 1)
                            bank = tiles.take(dve, ("rows", s, i))
                            tiles.copied(dve.tensor_tensor(
                                osum[:, :, :], bank[:, 0:H * 32].rearrange("p (h w) -> p h w", w=32)[:, :, 0:W17],
                                glob[:, :, :], ALU.add), ("rows", s, i))
                            tiles.wait_copied(dve, ("rows", s, i))
                            ch.mark(dve.reciprocal(orec[:, :], osum[:, :, DH]))
                            ch.after()
                            dve.wait_ge(x_stored, 1)
                            dve.tensor_tensor(x[s][:, QUERY_TILES[i], :].rearrange("p (h d) -> p h d", d=DH),
                                              osum[:, :, 0:DH],
                                              orec[:, :, None].broadcast_to([P, H, DH]), ALU.mult)\
                                .then_inc(o_tok, 1)

                        for k in range(STEPS + LAG_V + LAG_R + 1):
                            if k < STEPS:
                                bank = tiles.take(dve, ("s", s, k))
                                w_ = 2 + len(blocks(step(k)[1])) * P
                                dve.tensor_reduce(negmax[:, s, k:k + 1], bank[:, 0:w_], AX.X, ALU.max,
                                                  negate=True).then_inc(rowmax, 1)
                            if k == AT_T + 1:
                                bank = tiles.take(dve, ("pgT", s))
                                tiles.copied(dve.tensor_copy(pgT[:, :, :].rearrange("p t h -> p (t h)"),
                                                             bank[:, 0:NT * H]), ("pgT", s))
                            if k == AT_O + 1:
                                bank = tiles.take(dve, ("og", s))
                                tiles.copied(dve.tensor_tensor(ogm[:, :], bank[0:H, 0:D], headrow[:, :], ALU.mult),
                                             ("og", s))
                            if k == AT_1 + 1:
                                dve.wait_ge(o_tok, s * NT + QUERY_TILES.index(0) + 1)
                                bank = tiles.take(dve, ("og1", s))
                                tiles.copied(dve.tensor_copy(x[s][0:1, 0, :], bank[0:1, 0:D]), ("og1", s))
                            if LAG_T <= k < STEPS + LAG_T and (k - LAG_T) % 2 == 0:
                                kt = k - LAG_T
                                bank = tiles.take(dve, ("pT", s, kt))
                                w_ = len(blocks(step(kt)[1])) * P
                                tiles.copied(dve.tensor_copy(probT[kt % 4][:, 0:w_], bank[:, 0:w_]), ("pT", s, kt))
                            if s and k == AT_OT + 1:
                                outputs_turned(0)
                            if s and k == AT_OP + 1:
                                residual(0, "o", xb_ready, 0)
                                statistics(ch, 0)
                            if s and k == AT_N:
                                normalise(NB, 0)
                            if s and k == AT_X + 1:
                                shifted_turned(0)
                            if row_tile(k - 1) is not None:
                                gather(row_tile(k - 1))

                    relu(0, 1)
                    outputs_turned(1)
                    relu(0, 3)
                    residual(0, "o", xb_ready, 1)
                    statistics(ch, 1)
                    relu(0, 5)
                    normalise(NB + 1, 1)
                    residual(1, "down", xb2_ready, 0)
                    shifted_turned(1)
                    for c in range(1, FC, 2):
                        relu(1, c)
                    residual(1, "down", xb2_ready, 1)
                    ph.end_round(dve, layer * ROUNDS + r)
            ch = Chain(dve, dve_chain)
            for s in range(NB):
                statistics(ch, s)
            for s in range(NB):
                normalise(s, s)
            ph.end_round(dve, LAST)


def induce(nc, a, outer):
    with ExitStack() as ctx:
        ph = Phase(nc, "induce", ctx, outer)
        wc = ph.sb("wc", [DP, KT, E])
        fcols = ph.sb("fcols", [DP, 2, KT])
        bc = ph.sb("bc", [P, E])
        win = ph.sb("win", [E, 2, 3, E])
        wout = ph.sb("wout", [E, 2, E])
        l1, l2 = ph.sb("l1", [E, 2, 512]), ph.sb("l2", [P, 2, IF, E])
        ecols = ph.sb("ecols", [E, 2, 6])
        l1b = ph.sb("l1b", [P, 2, IF])
        erows = ph.sb("erows", [P, 2, 3, E])
        gcols, grows = ph.sb("gcols", [E, 2]), ph.sb("grows", [P, 2, E])
        wgate = ph.sb("wgate", [E, G + G * X])
        ind = ph.sb("ind", [P, 1, E])
        ident = ph.sb("ident", [P, P])
        half = ph.sb("half", [P, NT])
        rank = ph.sb("rank", [P, X])
        indT, q1 = ph.sb("indT", [E, P]), ph.sb("q1", [E, 2, P], F32R)
        q1_st = ph.sb("q1_st", [P, IH // 2, P], F32R)
        indb = ph.sb("indb", [P, E])

        def two(name, shape, dt=F32):
            return [ph.sb(f"{name}{s}", shape, dt) for s in range(NB)]

        x, xT = two("x", [P, NT, D]), two("xT", [DP, KT, S])
        h, x2, x3 = two("h", [P, NT, E]), two("x2", [P, NT, E]), two("x3", [P, NT, E])
        x2b = two("x2b", [P, NT, E])
        u1T, u2T = two("u1T", [E, S]), two("u2T", [E, S])
        kq = two("kq", [E, 4, S], F32R)
        k1_st, q2_st = two("k1_st", [P, IH // 2, S], F32R), two("q2_st", [P, IH // 2, S], F32R)
        k2, k2_st = two("k2", [E, 2, P], F32R), two("k2_st", [P, IH // 2, P], F32R)
        v1, v2 = two("v1", [P, NT, IH, W17]), two("v2", [P, IH, W17])
        o1, y1, y1b = two("o1", [P, E]), two("y1", [P, 1, E]), two("y1b", [P, E])
        t1, h1 = two("t1", [E, P]), two("h1", [P, 1, E])
        hid1, ukT = two("hid1", [P, IF, P]), two("ukT", [E, P])
        y2, y2b = two("y2", [P, NT, E]), two("y2b", [P, NT, E])
        hid2 = two("hid2", [P, IF, S])
        h2, x5, z = two("h2", [P, NT, E]), two("x5", [P, NT, E]), two("z", [P, NT, E])
        base = two("base", [P, NT, E])
        N5 = NT * (G + 1)
        all_gates = ph.sb("gates", [P, NB * N5, X])
        gates = [all_gates[:, s * N5:(s + 1) * N5, :] for s in range(NB)]
        giT = two("giT", [G * X, S])
        prob = [ph.sb(f"prob{j}", [P, S]) for j in range(4)]
        probT = [ph.sb(f"probT{j}", [P, S]) for j in range(4)]
        rmax = ph.sb("rmax", [P, NB * IH, NT])
        orec = ph.sb("orec", [P, 2, IH])
        ga, gb, gc = (ph.sb(f"g{c}", [P, NB * N5, X]) for c in "abc")
        gs = ph.sb("gs", [P, 6, NB * N5])
        st6, mv = ph.sb("st6", [P, NB, NT, 6]), ph.sb("mv", [P, NB, NT, 2])
        rstd = ph.sb("rstd", [P, NB, NT])
        banks = [ph.psum(f"bank{b}") for b in range(RING)]
        obank = [ph.psum(f"obank{b}") for b in range(2)]

        LAG_T, LAG_V = 2, 4
        AT_ROWS = 2
        seqs = range(NB)
        att = {1: [], 2: []}
        for at in (1, 2):
            for s in seqs:
                for k in range(IH + LAG_V):
                    if k < IH:
                        att[at].append((f"s{at}", s, k))
                    if LAG_T <= k < IH + LAG_T:
                        att[at].append((f"p{at}T", s, k - LAG_T))
                    if s and k == AT_ROWS:
                        att[at] += [(f"o{at}R", s - 1, c) for c in range(at)]
                if s == NB - 1:
                    att[at] += [(f"o{at}R", s, c) for c in range(at)]

        def each(*names):
            return [(n, s) for s in seqs for n in names]

        order = ([("xT", s, k) for s in seqs for k in range(KT)] + each("logits") + each("u")
                 + each("k1", "q2", "v1") + att[1] + each("o1T") + each("y1") + each("t1") + each("up1")
                 + each("down1") + each("uk") + each("k2", "v2") + att[2] + each("o2T") + each("y2") + each("t2")
                 + [("up2", s, c) for s in seqs for c in range(IF)] + each("down2") + each("x5T") + each("zT")
                 + each("gate") + each("giT"))
        tiles = Tiles(ph, banks, order)

        def by_scalar(at, k):
            return at == 2 or k % 2 == 1

        LNS = {(n, s): i * NB + s for i, n in enumerate(
            ("final", "x2", "x3", "y1", "h1", "y2", "x5", "z")) for s in seqs}
        ROWS = {"y1": 1, "h1": 1}

        weights_in, points = ph.lasting("weights_in"), ph.lasting("points")
        consts_set, scaled = ph.lasting("consts_set"), ph.lasting("scaled")
        q1_out, q1_in = ph.lasting("q1_out"), ph.lasting("q1_in")
        x_in, split_hi = ph.lasting("x_in"), ph.sem("split_hi")
        kq_out, stacked, stacked_q = ph.sem("kq_out"), ph.sem("stacked"), ph.sem("stacked_q")
        k2_out, stacked2 = ph.sem("k2_out"), ph.sem("stacked2")
        rowmax, expd2 = ph.sem("rowmax"), ph.sem("expd2")
        o1_full, o1_free, o2_full, o2_free = (ph.sem(n) for n in ("o1_full", "o1_free", "o2_full", "o2_free"))
        o_clear = ph.lasting("o_clear")
        moments, roots, normed = ph.sem("moments"), ph.sem("roots"), ph.sem("normed")
        x2b_ready, y1b_ready, y2b_ready = ph.sem("x2b_ready"), ph.sem("y1b_ready"), ph.sem("y2b_ready")
        base_ready, z_ready = ph.sem("base_ready"), ph.sem("z_ready")
        gexp_in, gexp_out, gates_set = ph.sem("gexp_in"), ph.sem("gexp_out"), ph.sem("gates_set")
        dve_chain, pool_chain = ph.sem("dve_chain"), ph.sem("pool_chain")
        stored = ph.sem("stored")
        block = ctx.enter_context(nc.Block())
        ROUNDS = B // NB
        BQ, BK, LG1, LB1, LG2, LB2 = range(6)
        BV, BOUT, BL2 = range(3)
        loads = ((wc, "wc"), (fcols, "fcols"), (bc, "bc"), (win, "win"), (wout, "wout"), (l1, "l1"), (l2, "l2"),
                 (ecols, "ecols"), (l1b, "l1b"), (erows, "erows"), (gcols, "gcols"), (grows, "grows"),
                 (wgate, "wgate"), (ind, "ind"), (ident, "ident"), (rank, "rank"))
        NLOADS = 16 * len(loads)

        def stack(buf, head):
            return buf[64 * (head % 2):64 * (head % 2) + 3 * DH, head // 2, :]

        def restack(sp, buf, src_of, sem):
            for row in range(3):
                src = src_of(row).rearrange("(c par d) q -> par d c q", par=2, d=DH)
                for par in range(2):
                    p = 64 * par + DH * row
                    sp.dma_start(buf[p:p + DH, :, :].bitcast(F32), src[par]).then_inc(sem, 16)

        @block.sync
        def _(sp):
            for dst, src in loads:
                sp.dma_start(dst[:], a[src]).then_inc(weights_in, 16)
            def load_x(r):
                for s in seqs:
                    n = LAYERS * B + r * NB + s
                    src = a["x"][n:n + 1] if isinstance(n, int) else a["x"][bass.ds(n, 1)]
                    sp.dma_start(x[s][:, :, :], src.rearrange("o p t d -> (o p) t d")).then_inc(x_in, 16)

            load_x(0)
            sp.wait_ge(points, 10)
            for w in range(2):
                sp.dma_start(a["q1"][w], q1[:, w, :].bitcast(F32)).then_inc(q1_out, 16)
            sp.wait_ge(q1_out, 32)
            restack(sp, q1_st, lambda row: a["q1"][(0, 1, 0)[row]], q1_in)
            with sp.Fori(0, ROUNDS) as r:
                def seq(t, s):
                    return t[bass.ds(r * NB + s, 1)]
                for s in seqs:
                    for k in range(KT):
                        tiles.take(sp, ("xT", s, k))
                load_x(r + 1)
                for n, (key, w, buf) in enumerate((("k1", 0, k1_st), ("q2", 2, q2_st))):
                    for s in seqs:
                        tiles.wait_copied(sp, (key, s))
                        sp.dma_start(a["kq"][s, w:w + 2].rearrange("w p q -> p w q"),
                                     kq[s][:, w:w + 2, :].bitcast(F32)).then_inc(kq_out, 16)
                        sp.wait_ge(kq_out, 16 * (n * NB + s + 1))
                        parts = (0, 0, 1) if key == "k1" else (2, 3, 2)
                        restack(sp, buf[s], lambda row, s=s: a["kq"][s, parts[row]], stacked if n == 0 else stacked_q)
                for s in seqs:
                    tiles.wait_copied(sp, ("k2", s))
                    sp.dma_start(a["k2"][s].rearrange("w p q -> p w q"), k2[s][:, :, :].bitcast(F32))\
                        .then_inc(k2_out, 16)
                    sp.wait_ge(k2_out, 16 * (s + 1))
                    restack(sp, k2_st[s], lambda row, s=s: a["k2"][s, (0, 0, 1)[row]], stacked2)
                for s in seqs:
                    sp.wait_ge(base_ready, s + 1)
                    sp.dma_start(seq(a["base"], s).rearrange("o p t d -> (o p) t d"), base[s][:, :, :])\
                        .then_inc(stored, 16)
                    sp.wait_ge(z_ready, s + 1)
                    sp.dma_start(seq(a["z"], s).rearrange("o p t d -> (o p) t d"), z[s][:, :, :])\
                        .then_inc(stored, 16)
                for s in seqs:
                    tiles.wait_copied(sp, ("zT", s))
                    sp.dma_start(seq(a["zT"], s).rearrange("o p q -> (o p) q"), hid2[s][:, 1, :])\
                        .then_inc(stored, 16)
                for s in seqs:
                    sp.wait_ge(gates_set, 1)
                    sp.dma_start(seq(a["gates"], s).rearrange("o p t d -> (o p) t d"), gates[s][:, :, :])\
                        .then_inc(stored, 16)
                for s in seqs:
                    tiles.wait_copied(sp, ("giT", s))
                    sp.dma_start(seq(a["giT"], s).rearrange("o p q -> (o p) q"), giT[s][:, :]).then_inc(stored, 16)
                sp.wait_ge(stored, 16 * 5 * NB)
                ph.end_round(sp, r)
            sp.wait_ge(x_in, 16 * NB * (ROUNDS + 1))

        @block.gpsimd
        def _(pool):
            pool.memset(half[:, :], -0.5).then_inc(consts_set, 1)
            for s in seqs:
                pool.memset(v1[s][:, :, :, DH:W17], 1.0).then_inc(consts_set, 1)
                pool.memset(v2[s][:, :, DH:W17], 1.0).then_inc(consts_set, 1)
            pool.wait_ge(consts_set, 1 + 2 * NB)
            pool.wait_ge(points, 2)
            pool.tensor_scalar(rstd[:, 0, 0:1], mv[:, 0, 0:1, 1], EPS, None, ALU.add).then_inc(points, 1)
            pool.wait_ge(points, 3)
            pool.tensor_tensor(rstd[:, 0, 0:1], rstd[:, 0, 0:1], half[:, 0:1], ALU.pow).then_inc(points, 1)
            with pool.Fori(0, ROUNDS) as r:
                ch = Chain(pool, pool_chain)

                def root(name):
                    n = ROWS.get(name, NT)
                    for s in seqs:
                        pool.wait_ge(moments, LNS[name, s] + 1)
                        ch.mark(pool.tensor_scalar(rstd[:, s, 0:n], mv[:, s, 0:n, 1], EPS, None, ALU.add))
                        ch.after()
                        pool.tensor_tensor(rstd[:, s, 0:n], rstd[:, s, 0:n], half[:, 0:n], ALU.pow)\
                            .then_inc(roots, 1)

                root("final")
                root("x2")
                root("x3")
                for s in seqs:
                    pool.wait_ge(normed, LNS["x2", s] + 1)
                    pool.tensor_tensor(x2b[s][:, :, :], x2[s][:, :, :],
                                       erows[:, 1, BOUT:BOUT + 1, :].broadcast_to([P, NT, E]), ALU.add)\
                        .then_inc(x2b_ready, 1)
                root("y1")
                for s in seqs:
                    pool.wait_ge(normed, LNS["y1", s] + 1)
                    pool.tensor_tensor(y1b[s][:, :], y1[s][:, 0, :], erows[:, 0, BL2, :], ALU.add)\
                        .then_inc(y1b_ready, 1)
                root("h1")
                root("y2")
                for s in seqs:
                    pool.wait_ge(normed, LNS["y2", s] + 1)
                    ch.mark(pool.tensor_tensor(y2b[s][:, :, :], y2[s][:, :, :],
                                               erows[:, 1, BL2:BL2 + 1, :].broadcast_to([P, NT, E]), ALU.add))
                    ch.after()
                    pool.tensor_tensor(y2b[s][:, :, :], y2b[s][:, :, :], h[s][:, :, :], ALU.add)\
                        .then_inc(y2b_ready, 1)
                root("x5")
                root("z")
                for s in seqs:
                    pool.wait_ge(normed, LNS["x5", s] + 1)
                    pool.tensor_tensor(base[s][:, :, :], h2[s][:, :, :], x5[s][:, :, :], ALU.add)\
                        .then_inc(base_ready, 1)
                for s in seqs:
                    pool.wait_ge(normed, LNS["z", s] + 1)
                    ch.mark(pool.tensor_tensor(z[s][:, :, :], x3[s][:, :, :],
                                               grows[:, 0:1, :].broadcast_to([P, NT, E]), ALU.mult))
                    ch.after()
                    pool.tensor_tensor(z[s][:, :, :], z[s][:, :, :],
                                       grows[:, 1:2, :].broadcast_to([P, NT, E]), ALU.add).then_inc(z_ready, 1)
                ph.zero_round(pool, r)

        @block.tensor
        def _(pe):
            pe.wait_ge(weights_in, NLOADS)
            pe.wait_ge(consts_set, 1 + 2 * NB)
            pe.wait_ge(scaled, 3)
            pe.wait_ge(points, 5)
            pe.transpose(obank[0][:, 0:P], ind[:, 0, :], ident[:, :]).then_inc(points, 1)
            pe.wait_ge(points, 7)
            pe.matmul(obank[0][:, 0:P], win[:, 0, 0, :], indT[:, :], start=True, stop=True).then_inc(points, 1)
            with pe.Fori(0, ROUNDS) as r:

                def turn(key, src, n=NT):
                    bank = tiles.claim(pe, key)
                    for t in range(n):
                        mm = pe.transpose(bank[:, t * P:t * P + P], src[:, t, :], ident[:, :])
                    tiles.filled(mm, key)

                def by_rows(key, lhs, rhs, n=NT):
                    bank = tiles.claim(pe, key)
                    for t in range(n):
                        mm = pe.matmul(bank[:, t * E:t * E + E], lhs[:, t * P:t * P + P], rhs, start=True, stop=True)
                    tiles.filled(mm, key)

                def by_features(key, w, rhs):
                    bank = tiles.claim(pe, key)
                    tiles.filled(pe.matmul(bank[:, 0:rhs.shape[1]], w, rhs, start=True, stop=True), key)

                def normalised(name, s):
                    pe.wait_ge(normed, LNS[name, s] + 1)

                for s in seqs:
                    normalised("final", s)
                    for k in range(KT):
                        bank = tiles.claim(pe, ("xT", s, k))
                        for t in range(NT):
                            mm = pe.transpose(bank[0:DP, t * P:t * P + P], x[s][:, t, k * DP:k * DP + DP], ident[:, :])
                        tiles.filled(mm, ("xT", s, k))
                for s in seqs:
                    for k in range(KT):
                        tiles.wait_copied(pe, ("xT", s, k))
                    bank = tiles.claim(pe, ("logits", s))
                    for t in range(NT):
                        for k in range(KT):
                            mm = pe.matmul(bank[:, t * E:t * E + E], xT[s][:, k, t * P:t * P + P], wc[:, k, :],
                                           start=(k == 0), stop=(k == KT - 1))
                    tiles.filled(mm, ("logits", s))
                for s in seqs:
                    normalised("x3", s)
                    turn(("u", s), x3[s])
                for s in seqs:
                    tiles.wait_copied(pe, ("u", s))
                    by_features(("k1", s), win[:, 0, 1, :], u1T[s][:, :])
                    by_features(("q2", s), win[:, 1, 0, :], u2T[s][:, :])
                    by_rows(("v1", s), u1T[s], win[:, 0, 2, :])
                pe.wait_ge(o_clear, 2)

                def turn_outputs(at, s):
                    pe.wait_ge((o1_free, o2_free)[at - 1], at * (s + 1))
                    for c in range(at):
                        key = (f"o{at}R", s, c)
                        bank = tiles.claim(pe, key)
                        for j in range(2 if at == 1 else NT):
                            src = hid1[s][:, j, :] if at == 1 else hid2[s][:, c, j * P:j * P + P]
                            mm = pe.transpose(bank[:, j * P:j * P + P], src, ident[:, :])
                        tiles.filled(mm, key)

                for at in (1, 2):
                    for s in seqs:
                        if at == 1:
                            pe.wait_ge(q1_in, 16 * 6)
                            pe.wait_ge(stacked, 16 * 6 * (s + 1))
                            tiles.wait_copied(pe, ("v1", s))
                        else:
                            pe.wait_ge(stacked_q, 16 * 6 * (s + 1))
                            pe.wait_ge(stacked2, 16 * 6 * (s + 1))
                            tiles.wait_copied(pe, ("v2", s))
                        for k in range(IH + LAG_V):
                            if k < IH:
                                key = (f"s{at}", s, k)
                                bank = tiles.claim(pe, key)
                                if at == 1:
                                    mm = pe.matmul(bank[:, :], stack(q1_st, k), stack(k1_st[s], k),
                                                   start=True, stop=True)
                                else:
                                    q = stack(q2_st[s], k)
                                    for t in range(NT):
                                        mm = pe.matmul(bank[:, t * P:t * P + P], q[:, t * P:t * P + P],
                                                       stack(k2_st[s], k), start=True, stop=True)
                                tiles.filled(mm, key)
                            if LAG_T <= k < IH + LAG_T:
                                kt = k - LAG_T
                                n = s * IH + kt
                                if at == 1:
                                    tiles.wait_copied(pe, ("s1", s, kt))
                                else:
                                    pe.wait_ge(expd2, n + 1)
                                key = (f"p{at}T", s, kt)
                                bank = tiles.claim(pe, key)
                                for t in range(NT):
                                    mm = pe.transpose(bank[:, t * P:t * P + P], prob[n % 4][:, t * P:t * P + P],
                                                      ident[:, :])
                                tiles.filled(mm, key)
                            if k >= LAG_V:
                                kv = k - LAG_V
                                n = s * IH + kv
                                tiles.wait_copied(pe, (f"p{at}T", s, kv))
                                if kv == 0:
                                    if at == 1 and s:
                                        pe.wait_ge(o1_free, s)
                                    if at == 2:
                                        pe.wait_ge(o1_free, NB)
                                        if s:
                                            pe.wait_ge(o2_free, 2 * s)
                                p, c = 32 * (kv % 4), kv // 4
                                if at == 1:
                                    for t in range(NT):
                                        mm = pe.matmul(obank[0][p:p + W17, c * P:c * P + P], v1[s][:, t, kv, :],
                                                       probT[n % 4][:, t * P:t * P + P],
                                                       start=(t == 0), stop=(t == NT - 1))
                                else:
                                    mm = pe.matmul(obank[c][p:p + W17, :], v2[s][:, kv, :], probT[n % 4][:, :],
                                                   start=True, stop=True)
                                if kv == IH - 1:
                                    mm.then_inc(o1_full if at == 1 else o2_full, 1)
                            if s and k == AT_ROWS:
                                turn_outputs(at, s - 1)
                        if s == NB - 1:
                            turn_outputs(at, s)
                    if at == 1:
                        for s in seqs:
                            tiles.wait_copied(pe, ("o1R", s, 0))
                            bank = tiles.claim(pe, ("o1T", s))
                            tiles.filled(pe.transpose(bank[:, 0:P], o1[s][:, :], ident[:, :]), ("o1T", s))
                        for s in seqs:
                            tiles.wait_copied(pe, ("o1T", s))
                            by_rows(("y1", s), t1[s], wout[:, 0, :], 1)
                        for s in seqs:
                            normalised("y1", s)
                            bank = tiles.claim(pe, ("t1", s))
                            tiles.filled(pe.transpose(bank[:, 0:P], h1[s][:, 0, :], ident[:, :]), ("t1", s))
                        for s in seqs:
                            tiles.wait_copied(pe, ("t1", s))
                            bank = tiles.claim(pe, ("up1", s))
                            for c in range(IF):
                                mm = pe.matmul(bank[:, c * P:c * P + P], l1[:, 0, c * P:c * P + P], t1[s][:, :],
                                               start=True, stop=True)
                            tiles.filled(mm, ("up1", s))
                        for s in seqs:
                            tiles.wait_copied(pe, ("up1", s))
                            bank = tiles.claim(pe, ("down1", s))
                            for c in range(IF):
                                mm = pe.matmul(bank[:, 0:E], hid1[s][:, c, :], l2[:, 0, c, :],
                                               start=(c == 0), stop=(c == IF - 1))
                            tiles.filled(mm, ("down1", s))
                        for s in seqs:
                            normalised("h1", s)
                            turn(("uk", s), y1[s], 1)
                        for s in seqs:
                            tiles.wait_copied(pe, ("uk", s))
                            by_features(("k2", s), win[:, 1, 1, :], ukT[s][:, :])
                            by_rows(("v2", s), ukT[s], win[:, 1, 2, :], 1)
                for s in seqs:
                    for c in range(2):
                        tiles.wait_copied(pe, ("o2R", s, c))
                    turn(("o2T", s), x3[s])
                for s in seqs:
                    tiles.wait_copied(pe, ("o2T", s))
                    by_rows(("y2", s), u1T[s], wout[:, 1, :])
                for s in seqs:
                    normalised("y2", s)
                    turn(("t2", s), x3[s])
                for s in seqs:
                    tiles.wait_copied(pe, ("t2", s))
                    for c in range(IF):
                        by_features(("up2", s, c), l1[:, 1, c * P:c * P + P], u2T[s][:, :])
                for s in seqs:
                    for c in range(IF):
                        tiles.wait_copied(pe, ("up2", s, c))
                    bank = tiles.claim(pe, ("down2", s))
                    for t in range(NT):
                        for c in range(IF):
                            mm = pe.matmul(bank[:, t * E:t * E + E], hid2[s][:, c, t * P:t * P + P], l2[:, 1, c, :],
                                           start=(c == 0), stop=(c == IF - 1))
                    tiles.filled(mm, ("down2", s))
                for s in seqs:
                    normalised("x5", s)
                    turn(("x5T", s), x5[s])
                for s in seqs:
                    normalised("z", s)
                    turn(("zT", s), x3[s])
                for s in seqs:
                    tiles.wait_copied(pe, ("x5T", s))
                    tiles.wait_copied(pe, ("zT", s))
                    bank = tiles.claim(pe, ("gate", s))
                    for t in range(NT):
                        c = t * (G + 1) * X
                        rows = slice(t * P, t * P + P)
                        pe.matmul(bank[:, c:c + G * X], hid2[s][:, 1, rows], wgate[:, G:], start=True, stop=True)
                        mm = pe.matmul(bank[:, c + G * X:c + G * X + G], hid2[s][:, 0, rows], wgate[:, 0:G],
                                       start=True, stop=True)
                    tiles.filled(mm, ("gate", s))
                for s in seqs:
                    pe.wait_ge(gates_set, 1)
                    bank = tiles.claim(pe, ("giT", s))
                    for t in range(NT):
                        mm = pe.transpose(bank[0:G * X, t * P:t * P + P],
                                          gates[s][:, t * (G + 1):t * (G + 1) + G, :]
                                          .rearrange("p g x -> p (g x)"), ident[:, :])
                    tiles.filled(mm, ("giT", s))
                ph.end_round(pe, r)

        @block.scalar
        def _(act):
            act.wait_ge(weights_in, NLOADS)
            act.wait_ge(scaled, 3)
            act.wait_ge(points, 6)
            act.activation(indT[:, :], obank[0][:, 0:P], ACT.Identity, scale=ecols[:, 0, LG1:LG1 + 1],
                           bias=ecols[:, 0, LB1:LB1 + 1]).then_inc(points, 1)
            act.wait_ge(points, 8)
            act.activation(q1[:, 0, :], obank[0][:, 0:P], ACT.Identity, bias=ecols[:, 0, BQ:BQ + 1])\
                .then_inc(points, 1)
            with act.Fori(0, ROUNDS) as r:
                def affine(dst, src, g, b):
                    return act.activation(dst, src, ACT.Identity, scale=g, bias=b)

                for s in seqs:
                    bank = tiles.take(act, ("xT", s, 0))
                    tiles.copied(affine(xT[s][:, 0, :], bank[0:DP, :], fcols[:, 0, 0:1], fcols[:, 1, 0:1]),
                                 ("xT", s, 0))
                for s in seqs:
                    bank = tiles.take(act, ("u", s))
                    affine(u1T[s][:, :], bank[:, :], ecols[:, 0, LG1:LG1 + 1], ecols[:, 0, LB1:LB1 + 1])
                    tiles.copied(affine(u2T[s][:, :], bank[:, :], ecols[:, 1, LG1:LG1 + 1],
                                        ecols[:, 1, LB1:LB1 + 1]), ("u", s))
                for s in seqs:
                    for key, blk, bias, w in (("k1", 0, BK, 0), ("q2", 1, BQ, 2)):
                        bank = tiles.take(act, (key, s))
                        act.activation(kq[s][:, w, :], bank[:, :], ACT.Identity, bias=ecols[:, blk, bias:bias + 1])\
                            .then_inc(split_hi, 1)
                for at in (1, 2):
                    for s in seqs:
                        for k in range(IH + LAG_T):
                            if k < IH:
                                n = s * IH + k
                                if n >= 4:
                                    tiles.take(act, (f"p{at}T", (n - 4) // IH, (n - 4) % IH))
                                if at == 1:
                                    bank = tiles.take(act, ("s1", s, k))
                                    act.wait_ge(rowmax, n + 1)
                                    tiles.copied(act.activation(prob[n % 4][:, :], bank[:, :], ACT.Exp,
                                                                bias=rmax[:, n, 0:1]), ("s1", s, k))
                                else:
                                    tiles.wait_copied(act, ("s2", s, k))
                                    act.activation(prob[n % 4][:, :], prob[n % 4][:, :], ACT.Exp).then_inc(expd2, 1)
                            if k >= LAG_T and by_scalar(at, k - LAG_T):
                                n = s * IH + k - LAG_T
                                key = (f"p{at}T", s, k - LAG_T)
                                bank = tiles.take(act, key)
                                tiles.copied(act.activation(probT[n % 4][:, :], bank[:, :], ACT.Copy), key)
                        if at == 1:
                            act.wait_ge(o1_full, s + 1)
                            act.activation(hid1[s][:, 0:2, :].rearrange("p c d -> p (c d)"), obank[0][:, 0:2 * P],
                                           ACT.Copy).then_inc(o1_free, 1)
                        else:
                            act.wait_ge(o2_full, s + 1)
                            act.activation(hid2[s][:, 0, :], obank[0][:, :], ACT.Copy).then_inc(o2_free, 1)
                    if at == 1:
                        for s in seqs:
                            bank = tiles.take(act, ("o1T", s))
                            tiles.copied(act.activation(t1[s][:, :], bank[:, 0:P], ACT.Copy), ("o1T", s))
                        for s in seqs:
                            bank = tiles.take(act, ("t1", s))
                            tiles.copied(affine(t1[s][:, :], bank[:, 0:P], ecols[:, 0, LG2:LG2 + 1],
                                                ecols[:, 0, LB2:LB2 + 1]), ("t1", s))
                        for s in seqs:
                            bank = tiles.take(act, ("up1", s))
                            for c in range(IF):
                                ins = act.activation(hid1[s][:, c, :], bank[:, c * P:c * P + P], ACT.Gelu,
                                                     bias=l1b[:, 0, c:c + 1])
                            tiles.copied(ins, ("up1", s))
                        for s in seqs:
                            bank = tiles.take(act, ("uk", s))
                            tiles.copied(affine(ukT[s][:, :], bank[:, 0:P], ecols[:, 1, LG1:LG1 + 1],
                                                ecols[:, 1, LB1:LB1 + 1]), ("uk", s))
                        for s in seqs:
                            bank = tiles.take(act, ("k2", s))
                            act.activation(k2[s][:, 0, :], bank[:, 0:P], ACT.Identity, bias=ecols[:, 1, BK:BK + 1])\
                                .then_inc(split_hi, 1)
                for s in seqs:
                    bank = tiles.take(act, ("o2T", s))
                    tiles.copied(act.activation(u1T[s][:, :], bank[:, :], ACT.Copy), ("o2T", s))
                for s in seqs:
                    bank = tiles.take(act, ("t2", s))
                    tiles.copied(affine(u2T[s][:, :], bank[:, :], ecols[:, 1, LG2:LG2 + 1],
                                        ecols[:, 1, LB2:LB2 + 1]), ("t2", s))
                for s in seqs:
                    for c in range(IF):
                        bank = tiles.take(act, ("up2", s, c))
                        tiles.copied(act.activation(hid2[s][:, c, :], bank[:, :], ACT.Gelu, bias=l1b[:, 1, c:c + 1]),
                                     ("up2", s, c))
                for s in seqs:
                    bank = tiles.take(act, ("x5T", s))
                    tiles.copied(act.activation(hid2[s][:, 0, :], bank[:, :], ACT.Copy), ("x5T", s))
                for s in seqs:
                    bank = tiles.take(act, ("zT", s))
                    tiles.copied(affine(hid2[s][:, 1, :], bank[:, :], gcols[:, 0:1], gcols[:, 1:2]), ("zT", s))
                act.wait_ge(gexp_in, 1)
                act.activation(gs[:, 3, :], gs[:, 2, :], ACT.Exp).then_inc(gexp_out, 1)
                for s in seqs:
                    bank = tiles.take(act, ("giT", s))
                    tiles.copied(act.activation(giT[s][:, :], bank[0:G * X, :], ACT.Copy), ("giT", s))
                ph.end_round(act, r)

        @block.vector
        def _(dve):
            dve.wait_ge(weights_in, NLOADS)
            dve.bn_stats(st6[:, 0, 0, :], ind[:, 0, :]).then_inc(points, 1)
            dve.tensor_scalar(win[:, :, 0, :], win[:, :, 0, :], DH ** -0.5, None, ALU.mult).then_inc(scaled, 1)
            dve.tensor_scalar(ecols[:, :, BQ], ecols[:, :, BQ], DH ** -0.5, None, ALU.mult).then_inc(scaled, 1)
            dve.tensor_tensor(indb[:, :], ind[:, 0, :], erows[:, 0, BOUT, :], ALU.add).then_inc(scaled, 1)
            dve.wait_ge(points, 1)
            dve.bn_aggr(mv[:, 0, 0, :], st6[:, 0, 0, :]).then_inc(points, 1)
            dve.wait_ge(scaled, 3)
            dve.wait_ge(points, 4)
            dve.tensor_scalar(ind[:, 0, :], ind[:, 0, :], mv[:, 0, 0, 0:1], rstd[:, 0, 0:1],
                              ALU.subtract, ALU.mult).then_inc(points, 1)
            dve.wait_ge(points, 9)
            dve.scalar_tensor_tensor(q1[:, 1, :], obank[0][:, 0:P], ecols[:, 0, BQ:BQ + 1],
                                     q1[:, 0, :].bitcast(F32), ALU.add, ALU.subtract).then_inc(points, 1)
            dve.wait_ge(points, 10)
            for bank in obank:
                dve.memset(bank[:, :], 0.0).then_inc(o_clear, 1)
            with dve.Fori(0, ROUNDS) as r:
                ch = Chain(dve, dve_chain)

                def wide(t):
                    return t[:, :, :].rearrange("p t d -> p (t d)")

                def layernorm(name, src, dst):
                    n = ROWS.get(name, NT)
                    for s in seqs:
                        for t in range(n):
                            ins = dve.bn_stats(st6[:, s, t, :], src[s][:, t, :])
                        ch.mark(ins)
                        ch.after()
                        for t in range(n):
                            ins = dve.bn_aggr(mv[:, s, t, :], st6[:, s, t, :])
                        ins.then_inc(moments, 1)
                    for s in seqs:
                        dve.wait_ge(moments, LNS[name, s] + 1)
                        dve.wait_ge(roots, LNS[name, s] + 1)
                        for t in range(n):
                            ins = dve.tensor_scalar(dst[s][:, t, :], src[s][:, t, :], mv[:, s, t, 0:1],
                                                    rstd[:, s, t:t + 1], ALU.subtract, ALU.mult)
                        ins.then_inc(normed, 1)
                    for s in seqs:
                        dve.wait_ge(normed, LNS[name, s] + 1)

                def low(key, dst, high, bias, n, width=S):
                    dve.wait_ge(split_hi, n)
                    bank = tiles.take(dve, key)
                    tiles.copied(dve.scalar_tensor_tensor(dst, bank[:, 0:width], bias, high.bitcast(F32),
                                                          ALU.add, ALU.subtract), key)

                def values(key, dst, row, n):
                    bank = tiles.take(dve, key)
                    tiles.copied(dve.tensor_tensor(
                        dst, bank[:, 0:n * E].rearrange("p (t h d) -> p t h d", t=n, d=DH),
                        row.broadcast_to([P, n, E]).rearrange("p t (h d) -> p t h d", d=DH), ALU.add), key)

                ph.wait_lasting(dve, x_in, 16 * NB * (r + 1))
                layernorm("final", x, x)
                for s in seqs:
                    bank = tiles.take(dve, ("xT", s, 1))
                    tiles.copied(dve.tensor_scalar(xT[s][:, 1, :], bank[0:DP, :], fcols[:, 0, 1:2], fcols[:, 1, 1:2],
                                                   ALU.mult, ALU.add), ("xT", s, 1))
                for s in seqs:
                    bank = tiles.take(dve, ("logits", s))
                    tiles.copied(dve.tensor_tensor(h[s][:, :, :], bank[:, :].rearrange("p (t d) -> p t d", d=E),
                                                   bc[:, None, :].broadcast_to([P, NT, E]), ALU.add), ("logits", s))
                for s in seqs:
                    tiles.wait_copied(dve, ("logits", s))
                layernorm("x2", h, x2)
                layernorm("x3", x2, x3)
                for s in seqs:
                    low(("k1", s), kq[s][:, 1, :], kq[s][:, 0, :], ecols[:, 0, BK:BK + 1], 2 * s + 1)
                    low(("q2", s), kq[s][:, 3, :], kq[s][:, 2, :], ecols[:, 1, BQ:BQ + 1], 2 * s + 2)
                    values(("v1", s), v1[s][:, :, :, 0:DH], erows[:, 0, BV:BV + 1, :], NT)

                def rows_of(at, s):
                    for c in range(at):
                        bank = tiles.take(dve, (f"o{at}R", s, c))
                        if at == 1:
                            o = bank[:, 0:IH * 32].rearrange("p (h w) -> p h w", w=32)
                            dst, rec, shape = o1[s][:, :].rearrange("p (h d) -> p h d", d=DH), orec[:, 0, :], [P, IH, DH]
                            total = o[:, :, DH]
                        else:
                            o = bank[:, :].rearrange("p (t h w) -> p t h w", t=NT, w=32)
                            dst = x3[s][:, :, c * 4 * DH:(c + 1) * 4 * DH].rearrange("p t (h d) -> p t h d", d=DH)
                            rec, shape = orec[:, :, :].rearrange("p a h -> p (a h)"), [P, NT, 4, DH]
                            rec = rec.rearrange("p (t h) -> p t h", t=NT)
                            total = o[:, :, :, DH]
                            if c:
                                tiles.wait_copied(dve, ("o2R", s, c - 1))
                        ch.mark(dve.reciprocal(rec, total))
                        ch.after()
                        o = o[:, :, 0:DH] if at == 1 else o[:, :, :, 0:DH]
                        rec = rec[:, :, None] if at == 1 else rec[:, :, :, None]
                        tiles.copied(dve.tensor_tensor(dst, o, rec.broadcast_to(shape), ALU.mult),
                                     (f"o{at}R", s, c))

                for at in (1, 2):
                    for s in seqs:
                        for k in range(IH + LAG_T):
                            if k < IH:
                                n = s * IH + k
                                key = (f"s{at}", s, k)
                                bank = tiles.take(dve, key)
                                if at == 1:
                                    dve.tensor_reduce(rmax[:, n, 0:1], bank[:, :], AX.X, ALU.max, negate=True)\
                                        .then_inc(rowmax, 1)
                                else:
                                    if n >= 4:
                                        tiles.take(dve, ("p2T", (n - 4) // IH, (n - 4) % IH))
                                    view = bank[:, :].rearrange("p (t d) -> p t d", d=P)
                                    ch.mark(dve.tensor_reduce(rmax[:, n, :], view, AX.X, ALU.max))
                                    ch.after()
                                    tiles.copied(dve.tensor_tensor(
                                        prob[n % 4][:, :].rearrange("p (t d) -> p t d", d=P), view,
                                        rmax[:, n, :, None].broadcast_to([P, NT, P]), ALU.subtract), key)
                            if k >= LAG_T and not by_scalar(at, k - LAG_T):
                                n = s * IH + k - LAG_T
                                key = (f"p{at}T", s, k - LAG_T)
                                bank = tiles.take(dve, key)
                                tiles.copied(dve.tensor_copy(probT[n % 4][:, :], bank[:, :]), key)
                            if s and k == AT_ROWS + 1:
                                rows_of(at, s - 1)
                        if at == 2:
                            dve.wait_ge(o2_full, s + 1)
                            dve.tensor_copy(hid2[s][:, 1, :], obank[1][:, :]).then_inc(o2_free, 1)
                        if s == NB - 1:
                            rows_of(at, s)
                    if at == 1:
                        for s in seqs:
                            bank = tiles.take(dve, ("y1", s))
                            tiles.copied(dve.tensor_tensor(y1[s][:, 0, :], bank[:, 0:E], indb[:, :], ALU.add),
                                         ("y1", s))
                        for s in seqs:
                            tiles.wait_copied(dve, ("y1", s))
                        layernorm("y1", y1, h1)
                        for s in seqs:
                            bank = tiles.take(dve, ("down1", s))
                            dve.wait_ge(y1b_ready, s + 1)
                            tiles.copied(dve.tensor_tensor(h1[s][:, 0, :], bank[:, 0:E], y1b[s][:, :], ALU.add),
                                         ("down1", s))
                        for s in seqs:
                            tiles.wait_copied(dve, ("down1", s))
                        layernorm("h1", h1, y1)
                        for s in seqs:
                            low(("k2", s), k2[s][:, 1, :], k2[s][:, 0, :], ecols[:, 1, BK:BK + 1], 2 * NB + s + 1, P)
                            values(("v2", s), v2[s][:, None, :, 0:DH], erows[:, 1, BV:BV + 1, :], 1)
                for s in seqs:
                    bank = tiles.take(dve, ("y2", s))
                    dve.wait_ge(x2b_ready, s + 1)
                    tiles.copied(dve.tensor_tensor(wide(y2[s]), bank[:, :], wide(x2b[s]), ALU.add), ("y2", s))
                for s in seqs:
                    tiles.wait_copied(dve, ("y2", s))
                layernorm("y2", y2, x3)
                for s in seqs:
                    bank = tiles.take(dve, ("down2", s))
                    dve.wait_ge(y2b_ready, s + 1)
                    tiles.copied(dve.tensor_tensor(wide(h2[s]), bank[:, :], wide(y2b[s]), ALU.add), ("down2", s))
                for s in seqs:
                    tiles.wait_copied(dve, ("down2", s))
                layernorm("x5", h2, x5)
                layernorm("z", x5, x3)
                def row(j):
                    return gs[:, j, :]

                def spread(j):
                    return gs[:, j, :, None].broadcast_to([P, NB * N5, X])

                for s in seqs:
                    bank = tiles.take(dve, ("gate", s))
                    ch.mark(dve.memset(gates[s][:, G:N5:G + 1, G:X], -3e30))
                    ch.after()
                    b4 = bank[:, 0:N5 * X].rearrange("p (t c) -> p t c", t=NT)
                    g4 = gates[s][:, :, :].rearrange("p (t g) x -> p t (g x)", t=NT)
                    tiles.copied(dve.tensor_copy(g4[:, :, 0:G * X + G], b4[:, :, 0:G * X + G]), ("gate", s))
                    tiles.wait_copied(dve, ("gate", s))
                lg = all_gates[:, :, :]

                def step(ins):
                    ch.mark(ins)
                    ch.after()

                def first(src, m, hot):
                    step(dve.tensor_reduce(row(m), src, AX.X, ALU.max))
                    step(dve.tensor_tensor(hot, src, spread(m), ALU.is_equal))
                    step(dve.tensor_tensor(hot, hot, rank[:, None, :].broadcast_to([P, NB * N5, X]), ALU.mult))
                    step(dve.tensor_reduce(row(5), hot, AX.X, ALU.max))
                    step(dve.tensor_tensor(hot, hot, spread(5), ALU.is_equal))

                first(lg, 0, ga[:, :, :])
                step(dve.scalar_tensor_tensor(gc[:, :, :], ga[:, :, :], -1e30, lg, ALU.mult, ALU.add))
                first(gc[:, :, :], 1, gb[:, :, :])
                dve.tensor_tensor(row(2), row(1), row(0), ALU.subtract).then_inc(gexp_in, 1)
                dve.wait_ge(gexp_out, 1)
                step(dve.tensor_scalar(row(4), row(3), 1.0, None, ALU.add))
                step(dve.reciprocal(row(4), row(4)))
                step(dve.tensor_tensor(row(3), row(3), row(4), ALU.mult))
                step(dve.tensor_tensor(ga[:, :, :], ga[:, :, :], spread(4), ALU.mult))
                step(dve.tensor_tensor(gb[:, :, :], gb[:, :, :], spread(3), ALU.mult))
                dve.tensor_tensor(lg, ga[:, :, :], gb[:, :, :], ALU.add).then_inc(gates_set, 1)
                ph.end_round(dve, r)


def experts(nc, a, outer):
    with ExitStack() as ctx:
        ph = Phase(nc, "experts", ctx, outer)
        N = B * S
        NG = 4
        ident, ident_in = ph.sb("ident", [P, P]), ph.lasting("ident_in")
        NCH, NTT, TC = N // 512, N // P, 512 // P
        zT, accT = ph.sb("zT", [E, N]), ph.sb("accT", [E, N])
        zhi, zlo = ph.sb("zhi", [E, N], F32R), ph.sb("zlo", [E, N], F32R)
        out = ph.sb("out", [P, NTT, E])
        gates, gw = ph.sb("gates", [P, NTT, G + 1, X]), ph.sb("gw", [P, NTT, 1])
        giT, b2g = ph.sb("giT", [G * X, N]), ph.sb("b2g", [G * X, E])
        w1, w2 = ph.sb("w1", [E, 2, XH]), ph.sb("w2", [P, 2, XC, E])
        w1s, w2s = ph.sb("w1s", [E, 2, 2, XH], F32R), ph.sb("w2s", [P, 2, 2, XC, E], F32R)
        b1c, glrows = ph.sb("b1c", [P, X, XC]), ph.sb("glrows", [P, 2, E])
        relu = [ph.sb(f"relu{j}", [P, 512]) for j in range(XC)]
        hhi = [ph.sb(f"hhi{j}", [P, XC, 512], F32R) for j in range(2)]
        hlo = [ph.sb(f"hlo{j}", [P, XC, 512], F32R) for j in range(2)]
        gate = [ph.sb(f"gate{j}", [P, 512]) for j in range(NG)]
        gated = [ph.sb(f"gated{j}", [P, 512]) for j in range(2)]
        half = ph.sb("half", [P, TC])
        st6, mv, rstd = ph.sb("st6", [P, 2, TC, 6]), ph.sb("mv", [P, 2, TC, 2]), ph.sb("rstd", [P, 2, TC])
        y = [ph.sb(f"y{j}", [P, TC, E]) for j in range(2)]
        banks = [ph.psum(f"bank{b}") for b in range(8)]
        TURN = 2

        AHEAD = 3
        work = [(e, c) for e in range(X - 1) for c in range(NCH)]
        for c in range(NCH):
            at = (X - 2) * NCH + AHEAD + 2 * c
            work.insert(at, (X - 1, c))
        CH = len(work)
        STEPS = CH + 5
        step_of = {item: q for q, item in enumerate(work)}
        LOAD_AT = {step_of[e - 1, 0]: e for e in range(1, X - 1)}
        LOAD_AT |= {step_of[X - 3, 2]: X - 1, step_of[X - 2, 3]: X}
        SPLIT_AT = {step_of[e - 1, 2]: e for e in range(1, X - 1)}
        SPLIT_AT |= {step_of[X - 2, 1]: X - 1}

        def ending(q, lag):
            q -= lag
            return work[q][1] if 0 <= q < CH and work[q][0] == X - 1 else None

        order = []
        for q in range(STEPS):
            if q < NCH:
                order.append(("init", q))
            if q < CH:
                order += [("up", q, k) for k in range(XC)]
            if 1 <= q <= CH:
                order.append(("down", q - 1))
        tiles = Tiles(ph, banks[:-TURN], order)
        turned = Tiles(ph, banks[-TURN:], [("turned", c) for c in range(NCH)], "turned_")
        w0_in, w0_hi, w0_lo = ph.lasting("w0_in"), ph.lasting("w0_hi"), ph.lasting("w0_lo")
        gi_in, biases_in = ph.lasting("gi_in"), ph.lasting("biases_in")
        loaded, half_set = ph.lasting("loaded"), ph.lasting("half_set")
        z_in, z_hi, z_lo = ph.lasting("z_in"), ph.lasting("z_hi"), ph.lasting("z_lo")
        stored = ph.lasting("stored")
        group_in, gate_set = ph.sem("group_in"), ph.sem("gate_set")
        w_in, w_hi, w_lo = [ph.sem("w_in0"), ph.sem("w_in1")], ph.sem("w_hi"), ph.sem("w_lo")
        gate_in = [ph.sem(f"gate_in{j}") for j in range(NG)]
        h_lo, summed = ph.sem("h_lo"), ph.sem("summed")
        moments, roots, shifted = (ph.sem(n) for n in ("moments", "roots", "shifted"))
        added, dve_chain, pool_chain = ph.sem("added"), ph.sem("dve_chain"), ph.sem("pool_chain")
        block = ctx.enter_context(nc.Block())
        NLOADS = 16 * 2 * B

        @block.sync
        def _(sp):
            def load_expert(n, buf, sem):
                src = [a[w][n:n + 1] if isinstance(n, int) else a[w][bass.ds(n, 1)] for w in ("ew1", "ew2")]
                sp.dma_start(w1[:, buf, :], src[0].rearrange("o p n -> (o p) n")).then_inc(sem, 16)
                sp.dma_start(w2[:, buf, :, :], src[1].rearrange("o p k n -> (o p) k n")).then_inc(sem, 16)

            def load_biases(n):
                src = [a[w][n:n + 1] if isinstance(n, int) else a[w][bass.ds(n, 1)] for w in ("eb1", "eb2")]
                sp.dma_start(b1c[:, :, :], src[0].rearrange("o p x k -> (o p) x k")).then_inc(biases_in, 16)
                sp.dma_start(b2g[:, :], src[1].rearrange("o x d -> (o x) d")).then_inc(biases_in, 16)

            for b in range(B):
                sp.dma_start(zT[:, b * 512:b * 512 + 512], a["zT"][b]).then_inc(z_in, 16)
                if b == 0:
                    load_expert(0, 0, w0_in)
            load_biases(0)
            for b in range(B):
                sp.dma_start(giT[:, b * 512:b * 512 + 512], a["giT"][b]).then_inc(gi_in, 16)
            for b in range(B):
                tt = slice(TC * b, TC * b + TC)
                sp.dma_start(out[:, tt, :], a["base"][b]).then_inc(loaded, 16)
                sp.dma_start(gates[:, tt, :, :], a["gates"][b].rearrange("p (t g) x -> p t g x", t=TC))\
                    .then_inc(loaded, 16)
            with sp.Fori(0, G) as g:
                sp.dma_start(glrows[:, :, :], a["glrows"][bass.ds(g, 1)].rearrange("o p r d -> (o p) r d"))\
                    .then_inc(group_in, 16)

                def load_weights(e):
                    if e > 2:
                        sp.wait_ge(w_lo, 2 * (e - 2))
                    load_expert(g * X + e, e % 2, w_in[e % 2])

                for q, (e, c) in enumerate(work):
                    if q in LOAD_AT:
                        load_weights(LOAD_AT[q])
                    if q >= NG:
                        tiles.wait_copied(sp, ("down", q - NG))
                    sp.dma_start(gate[q % NG][:, :], a["giT"][c, bass.ds(g * X + e, 1), :].broadcast_to([P, 512]))\
                        .then_inc(gate_in[q % NG], 16)
                tiles.wait_copied(sp, ("up", CH - 1, XC - 1))
                load_biases(g + 1)
                ph.end_round(sp, g)
            sp.wait_ge(biases_in, 32 * (G + 1))
            for b in range(B):
                sp.dma_start(a["out"][b].rearrange("(t p) d -> p t d", p=P), out[:, TC * b:TC * b + TC, :])\
                    .then_inc(stored, 16)
            sp.wait_ge(stored, 16 * B)

        def weights_arrived(eng, e):
            eng.wait_ge(w_in[e % 2], 32 * ((e + 1) // 2))

        @block.gpsimd
        def _(pool):
            pool.memset(half[:, :], -0.5).then_inc(half_set, 1)
            pool.wait_ge(half_set, 1)
            pool.wait_ge(w0_in, 32)
            pool.tensor_copy(w1s[:, 0, 0, :], w1[:, 0, :]).then_inc(w0_hi, 1)
            pool.tensor_copy(w2s[:, 0, 0, :, :], w2[:, 0, :, :]).then_inc(w0_hi, 1)
            with pool.Fori(0, G) as g:
                ch = Chain(pool, pool_chain)

                def split_weights(e):
                    weights_arrived(pool, e)
                    if e >= 2:
                        tiles.take(pool, ("down", step_of[e - 2, NCH - 1]))
                    pool.tensor_copy(w1s[:, e % 2, 0, :], w1[:, e % 2, :]).then_inc(w_hi, 1)
                    pool.tensor_copy(w2s[:, e % 2, 0, :, :], w2[:, e % 2, :, :]).then_inc(w_hi, 1)

                pool.wait_ge(group_in, 16)
                for q in range(1, STEPS):
                    if q in SPLIT_AT:
                        split_weights(SPLIT_AT[q])
                    if q <= CH:
                        e, c = work[q - 1]
                        tiles.wait_copied(pool, ("down", q - 1))
                        if e:
                            pool.wait_ge(summed, step_of[e - 1, c] + 1)
                        else:
                            tiles.wait_copied(pool, ("init", c))
                        part = accT[:, c * 512:c * 512 + 512]
                        pool.tensor_tensor(part, part, gated[(q - 1) % 2][:, :], ALU.add).then_inc(summed, 1)
                    if (c := ending(q, 2)) is not None:
                        pool.wait_ge(moments, c + 1)
                        ch.mark(pool.tensor_scalar(rstd[:, c % 2, :], mv[:, c % 2, :, 1], EPS, None, ALU.add))
                        ch.after()
                        pool.tensor_tensor(rstd[:, c % 2, :], rstd[:, c % 2, :], half[:, :], ALU.pow)\
                            .then_inc(roots, 1)
                    if (c := ending(q, 3)) is not None:
                        turned.wait_copied(pool, ("turned", c))
                        yc = y[c % 2][:, :, :]
                        ch.mark(pool.tensor_tensor(yc, yc, glrows[:, 0:1, :].broadcast_to([P, TC, E]), ALU.mult))
                        ch.after()
                        pool.tensor_tensor(yc, yc, glrows[:, 1:2, :].broadcast_to([P, TC, E]), ALU.add)\
                            .then_inc(shifted, 1)
                ph.zero_round(pool, g)

        @block.tensor
        def _(pe):
            pe.wait_ge(ident_in, 16)
            pe.wait_ge(gi_in, 16 * B)
            pe.wait_ge(w0_lo, 2)
            with pe.Fori(0, G) as g:
                ph.wait_lasting(pe, biases_in, 32 * (g + 1))
                for q in range(STEPS):
                    if q < NCH:
                        bank = tiles.claim(pe, ("init", q))
                        tiles.filled(pe.matmul(bank[:, :], b2g[:, :], giT[:, q * 512:q * 512 + 512],
                                               start=True, stop=True), ("init", q))
                        pe.wait_ge(z_lo, q + 1)
                    if q < CH:
                        e, c = work[q]
                        if c == 0 and e:
                            pe.wait_ge(w_lo, 2 * e)
                        zc = slice(c * 512, c * 512 + 512)
                        for k in range(XC):
                            bank = tiles.claim(pe, ("up", q, k))
                            hi, lo = (w1s[:, e % 2, part, k * P:k * P + P] for part in range(2))
                            pe.matmul(bank[:, :], hi, zhi[:, zc], start=True, stop=False)
                            pe.matmul(bank[:, :], hi, zlo[:, zc], start=False, stop=False)
                            mm = pe.matmul(bank[:, :], lo, zhi[:, zc], start=False, stop=True)
                            tiles.filled(mm, ("up", q, k))
                    if 1 <= q <= CH:
                        q1 = q - 1
                        bank = tiles.claim(pe, ("down", q1))
                        for k in range(XC):
                            pe.wait_ge(h_lo, XC * q1 + k + 1)
                            hi, lo = (w2s[:, work[q1][0] % 2, part, k, :] for part in range(2))
                            pe.matmul(bank[:, :], hi, hhi[q1 % 2][:, k, :], start=(k == 0), stop=False)
                            pe.matmul(bank[:, :], hi, hlo[q1 % 2][:, k, :], start=False, stop=False)
                            mm = pe.matmul(bank[:, :], lo, hhi[q1 % 2][:, k, :], start=False, stop=(k == XC - 1))
                        tiles.filled(mm, ("down", q1))
                    if (c := ending(q, 2)) is not None:
                        bank = turned.claim(pe, ("turned", c))
                        pe.wait_ge(summed, step_of[X - 1, c] + 1)
                        for t in range(TC):
                            col = (c * TC + t) * P
                            mm = pe.transpose(bank[:, t * P:t * P + P], accT[:, col:col + P], ident[:, :])
                        turned.filled(mm, ("turned", c))
                ph.end_round(pe, g)

        @block.scalar
        def _(act):
            act.dma_start(ident[:, :], a["ident"]).then_inc(ident_in, 16)
            act.wait_ge(z_in, 16 * B)
            for b in range(B):
                act.activation(zhi[:, b * 512:b * 512 + 512], zT[:, b * 512:b * 512 + 512], ACT.Copy)\
                    .then_inc(z_hi, 1)
            with act.Fori(0, G) as g:
                ph.wait_lasting(act, biases_in, 32 * (g + 1))
                for q in range(CH):
                    for k in range(XC):
                        bank = tiles.take(act, ("up", q, k))
                        if q:
                            act.wait_ge(h_lo, XC * (q - 1) + k + 1)
                        if q >= 2:
                            tiles.take(act, ("down", q - 2))
                        bias = b1c[:, work[q][0], k:k + 1]
                        act.activation(relu[k][:, :], bank[:, :], ACT.Relu, bias=bias)
                        tiles.copied(act.activation(hhi[q % 2][:, k, :], bank[:, :], ACT.Relu, bias=bias),
                                     ("up", q, k))
                weights_arrived(act, X)
                tiles.take(act, ("down", step_of[X - 2, NCH - 1]))
                act.activation(w1s[:, 0, 0, :], w1[:, 0, :], ACT.Copy).then_inc(w_hi, 1)
                act.activation(w2s[:, 0, 0, :, :], w2[:, 0, :, :], ACT.Copy).then_inc(w_hi, 1)
                ph.end_round(act, g)

        @block.vector
        def _(dve):
            for b in range(B):
                dve.wait_ge(z_hi, b + 1)
                part = slice(b * 512, b * 512 + 512)
                dve.tensor_tensor(zlo[:, part], zT[:, part], zhi[:, part].bitcast(F32), ALU.subtract)\
                    .then_inc(z_lo, 1)
                if b == 0:
                    dve.wait_ge(w0_hi, 1)
                    dve.tensor_tensor(w1s[:, 0, 1, :], w1[:, 0, :], w1s[:, 0, 0, :].bitcast(F32),
                                      ALU.subtract).then_inc(w0_lo, 1)
                    dve.wait_ge(w0_hi, 2)
                    dve.tensor_tensor(w2s[:, 0, 1, :, :], w2[:, 0, :, :], w2s[:, 0, 0, :, :].bitcast(F32),
                                      ALU.subtract).then_inc(w0_lo, 1)
            with dve.Fori(0, G) as g:
                ch = Chain(dve, dve_chain)

                def split_weights(e):
                    dve.wait_ge(w_hi, 2 * e - 1)
                    dve.tensor_tensor(w1s[:, e % 2, 1, :], w1[:, e % 2, :], w1s[:, e % 2, 0, :].bitcast(F32),
                                      ALU.subtract).then_inc(w_lo, 1)
                    dve.wait_ge(w_hi, 2 * e)
                    dve.tensor_tensor(w2s[:, e % 2, 1, :, :], w2[:, e % 2, :, :],
                                      w2s[:, e % 2, 0, :, :].bitcast(F32), ALU.subtract).then_inc(w_lo, 1)

                for q in range(STEPS):
                    if q < NCH:
                        bank = tiles.take(dve, ("init", q))
                        part = slice(q * 512, q * 512 + 512)
                        tiles.copied(dve.tensor_tensor(accT[:, part], bank[:, :], zT[:, part], ALU.add), ("init", q))
                    if q == NCH:
                        dve.wait_ge(loaded, NLOADS)
                        dve.tensor_copy(gw[:, :, :], gates[:, :, G, bass.ds(g, 1)]).then_inc(gate_set, 1)
                    if q < CH:
                        if q in SPLIT_AT:
                            split_weights(SPLIT_AT[q])
                        for k in range(XC):
                            tiles.wait_copied(dve, ("up", q, k))
                            dve.tensor_tensor(hlo[q % 2][:, k, :], relu[k][:, :], hhi[q % 2][:, k, :].bitcast(F32),
                                              ALU.subtract).then_inc(h_lo, 1)
                    if 1 <= q <= CH:
                        q1 = q - 1
                        bank = tiles.take(dve, ("down", q1))
                        dve.wait_ge(gate_in[q1 % NG], 16 * (q1 // NG + 1))
                        if q1 >= 2:
                            dve.wait_ge(summed, q1 - 1)
                        tiles.copied(dve.tensor_tensor(gated[q1 % 2][:, :], bank[:, :], gate[q1 % NG][:, :],
                                                       ALU.mult), ("down", q1))
                    if (c := ending(q, 3)) is not None:
                        bank = banks[-TURN + c % TURN]
                        dve.wait_ge(roots, c + 1)
                        if c >= 2:
                            dve.wait_ge(added, c - 1)
                        for t in range(TC):
                            ins = dve.tensor_scalar(y[c % 2][:, t, :], bank[:, t * P:t * P + P], mv[:, c % 2, t, 0:1],
                                                    rstd[:, c % 2, t:t + 1], ALU.subtract, ALU.mult)
                        turned.copied(ins, ("turned", c))
                    if (c := ending(q, 2)) is not None:
                        bank = turned.take(dve, ("turned", c))
                        for t in range(TC):
                            ins = dve.bn_stats(st6[:, c % 2, t, :], bank[:, t * P:t * P + P])
                        ch.mark(ins)
                        ch.after()
                        for t in range(TC):
                            ins = dve.bn_aggr(mv[:, c % 2, t, :], st6[:, c % 2, t, :])
                        ins.then_inc(moments, 1)
                    if (c := ending(q, 4)) is not None:
                        if c == 0:
                            dve.wait_ge(gate_set, 1)
                        dve.wait_ge(shifted, c + 1)
                        for t in range(TC):
                            row = out[:, c * TC + t, :]
                            ins = dve.scalar_tensor_tensor(row, y[c % 2][:, t, :], gw[:, c * TC + t, :],
                                                           row, ALU.mult, ALU.add)
                        ins.then_inc(added, 1)
                split_weights(X)
                ph.end_round(dve, g)


def pack_tower(inp):
    def arr(n):
        return np.asarray(inp["L0_tok_" + n])

    def by_in(w, p):
        n_layers, out, inn = w.shape
        return w.transpose(0, 2, 1).reshape(n_layers, inn // p, p, out).transpose(0, 2, 1, 3)

    def by_feature(v, p):
        return v.reshape(v.shape[0], -1, p).transpose(0, 2, 1)

    def on_all(v):
        return np.broadcast_to(v[:, None, :], (v.shape[0], P, v.shape[1]))

    return {
        "wqk": np.stack([by_in(arr("Wq"), DP), by_in(arr("Wk"), DP)], 2),
        "wvo": np.stack([by_in(arr("Wv"), DP), by_in(arr("Wo"), DP)], 2),
        "w1": by_in(arr("W1"), DP),
        "w2": by_in(arr("W2"), P),
        "rows": np.stack([on_all(arr(n)) for n in ("bv", "bo", "g1", "beta1", "b2")], 2),
        "rows2": np.stack([on_all(arr(n)) for n in ("g2", "beta2")], 2),
        "cols": np.stack([by_feature(arr(n), DP) for n in ("bq", "bk", "g1", "beta1")], 2),
        "b1c": by_feature(arr("b1"), P),
        "emb": arr("emb"),
        "ids": np.broadcast_to(np.asarray(inp["x"]).reshape(1, B * S), (P, B * S)),
        "pad": np.asarray(inp["mask_BS_b0_1"]),
    }


def pack_induce(inp):
    def arr(n):
        return np.asarray(inp["L0_" + n])

    def both(f, axis=1):
        return np.stack([f("attn_a1_"), f("attn_a2_")], axis)

    def on_all(v):
        return np.broadcast_to(v[None], (P,) + v.shape)

    def cols(*names):
        return np.stack([arr(n) for n in names], 1)

    ln = ("ln1_g", "ln1_b", "ln2_g", "ln2_b")
    return {
        "wc": arr("tok_Wc").T.reshape(KT, DP, E).transpose(1, 0, 2),
        "fcols": np.stack([arr("tok_gf").reshape(KT, DP).T, arr("tok_betaf").reshape(KT, DP).T], 1),
        "bc": on_all(arr("tok_bc")),
        "win": both(lambda p: arr(p + "in_w").T.reshape(E, 3, E)),
        "wout": both(lambda p: arr(p + "out_w").T),
        "l1": both(lambda p: arr(p + "l1_w").T),
        "l2": both(lambda p: arr(p + "l2_w").T.reshape(IF, P, E).transpose(1, 0, 2)),
        "ecols": both(lambda p: np.concatenate([arr(p + "in_b").reshape(3, E)[0:2].T, cols(*(p + n for n in ln))], 1)),
        "l1b": both(lambda p: arr(p + "l1_b").reshape(IF, P).T),
        "erows": both(lambda p: on_all(np.stack([arr(p + "in_b")[2 * E:], arr(p + "out_b"), arr(p + "l2_b")]))),
        "gcols": cols("ffn_ln_g", "ffn_ln_b"),
        "grows": on_all(np.stack([arr("ffn_ln_g"), arr("ffn_ln_b")])),
        "wgate": np.concatenate([arr("ffn_wg_group"), arr("ffn_wg_inner").transpose(1, 0, 2).reshape(E, G * X)], 1),
        "ind": arr("attn_ind")[:, None, :],
        "rank": np.broadcast_to(np.arange(X, 0, -1, dtype=np.float32), (P, X)),
    }


def pack_experts(inp):
    def arr(n):
        return np.asarray(inp["L0_ffn_" + n])

    def and_first(v):
        return np.concatenate([v, v[0:1]])

    own = np.zeros((G, G, X, E), np.float32)
    own[np.arange(G), np.arange(G)] = arr("b2")
    gl = np.stack([arr("gln_g"), arr("gln_b")], 1)
    return {
        "ew1": and_first(arr("W1").reshape(G * X, E, XH)),
        "ew2": and_first(arr("W2").reshape(G * X, XC, P, E).transpose(0, 2, 1, 3)),
        "eb1": and_first(arr("b1").reshape(G, X, XC, P).transpose(0, 3, 1, 2)),
        "eb2": and_first(own.reshape(G, G * X, E)),
        "glrows": np.broadcast_to(gl[:, None], (G, P, 2, E)),
    }


def constants():
    r, c = np.arange(P)[:, None], np.arange(P)[None, :]
    feature = np.arange(D)
    heads = (feature[:, None] // DH == np.arange(H)[None, :]).astype(np.float32)
    return {
        "ident": np.eye(P, dtype=np.float32),
        "identb": np.eye(P, dtype=mybir.dt.np(BF16)),
        "mask": np.stack([np.where(c >= r, 0.0, NEG), np.where(c <= r, 0.0, NEG)], 1).astype(mybir.dt.np(BF16)),
        "heads": heads.reshape(KT, DP, H).transpose(1, 0, 2).copy(),
        "headrow": heads.T.copy(),
        "iota": np.arange(P, dtype=np.float32)[:, None].copy(),
    }


SCRATCH = {
    "x": (X_SLOTS, P, NT, D), "kb": (KB_SLOTS, 2, S + 2), "qk": (NB, 4, D, S),
    "q1": (2, E, P), "kq": (NB, 4, E, S), "k2": (NB, 2, E, P),
    "base": (B, P, NT, E), "z": (B, P, NT, E), "zT": (B, E, S), "gates": (B, P, NT * (G + 1), X),
    "giT": (B, G * X, S),
}


def build(nc, a):
    for name, shape in SCRATCH.items():
        if name not in a:
            a[name] = nc.dram_tensor(f"scratch_{name}", shape, F32, kind="Internal").ap()
    with ExitStack() as outer:
        embed(nc, a, outer)
        tower(nc, a, outer)
        induce(nc, a, outer)
        experts(nc, a, outer)


def kernel(**inputs):
    import concourse.bacc as bacc
    from concourse.bass_utils import run_bass_kernel_spmd

    arrays = {**pack_tower(inputs), **pack_induce(inputs), **pack_experts(inputs), **constants()}
    arrays = {n: np.ascontiguousarray(v) for n, v in arrays.items()}
    nc = bacc.Bacc("TRN2", target_bir_lowering=False, num_devices=1)
    a = {n: nc.dram_tensor(n, v.shape, mybir.dt.from_np(v.dtype), kind="ExternalInput").ap()
         for n, v in arrays.items()}
    a["out"] = nc.dram_tensor("out", (B, S, E), F32, kind="ExternalOutput").ap()
    build(nc, a)
    r = run_bass_kernel_spmd(nc, [arrays], core_ids=[0])
    return r.results[0]["out"]
```
